# Optimizing a Trainium2 kernel written in Bass

```python
import numpy as np
import jax
import jax.numpy as jnp

def _softmax(x, axis=-1):
    return jax.nn.softmax(x, axis=axis)

def _gelu(x):
    return jax.nn.gelu(x, approximate=True)

def _silu(x):
    return jax.nn.silu(x)

def _sigmoid(x):
    return jax.nn.sigmoid(x)

def _layernorm(x, axis=-1, eps=1e-05):
    m = jnp.mean(x, axis=axis, keepdims=True)
    v = jnp.var(x, axis=axis, keepdims=True)
    return (x - m) / jnp.sqrt(v + eps)

def _scatter_add(tgt, idx, src, axis=0):
    return tgt.at[idx].add(src)

def _segment_sum(src, seg, n):
    return jax.ops.segment_sum(src, seg, n)
kernel_name = 'mk_audio_tower_d1_tok_audfeat512_r4_da5b27'

def setup_inputs(seed: int=0):
    np.random.seed(seed)
    _w = jnp.asarray

    def _rec_inputs():
        import jax
        import jax.numpy as jnp
        _rk = jax.random.key(seed)
        x = -7.10856e-05 + 0.999911 * jax.random.normal(jax.random.fold_in(_rk, 1), (32, 750, 128), jnp.float32)
        return x
    x = _rec_inputs()

    def _L0_tok_setup():
        import jax, jax.numpy as jnp
        import numpy as np
        TOKEN_SIZE = 16
        STRIDE = 8
        EMBED_DIM = 128
        key = jax.random.key(seed)
        k1, k2 = jax.random.split(key)
        B, S, D = (32, 1024, EMBED_DIM)
        x = jax.random.normal(k1, (B, S, D), dtype=jnp.float32)
        fan_in = TOKEN_SIZE * D
        W = jax.random.normal(k2, (fan_in, D), dtype=jnp.float32) / np.sqrt(fan_in)
        b = jnp.zeros((D,), dtype=jnp.float32)
        gamma = jnp.ones((D,), dtype=jnp.float32)
        beta = jnp.zeros((D,), dtype=jnp.float32)
        return {'x': x, 'W': W, 'b': b, 'gamma': gamma, 'beta': beta}
    _L0_tok_all = _L0_tok_setup()
    _L0_tok_in = {k: v for k, v in _L0_tok_all.items() if k in ('W', 'b', 'gamma', 'beta')}
    del _L0_tok_all

    def _L0_attn_setup():
        import jax, jax.numpy as jnp
        import numpy as np
        DIM = 128
        HEADS = 8
        DIM_HEAD = 64
        DIM_INNER = HEADS * DIM_HEAD
        FRAC_GRAD = 0.5
        SCALE = DIM_HEAD ** (-0.5)
        EPS_CUMPROD = 1e-10
        EPS_INV = 1e-08

        def _rms_norm(x, gamma):
            nrm = jnp.linalg.norm(x, axis=-1, keepdims=True)
            return x / jnp.maximum(nrm, 1e-12) * DIM ** 0.5 * gamma

        def _safe_cumprod(t, axis):
            t = jnp.clip(t, EPS_CUMPROD, 1.0)
            return jnp.exp(jnp.cumsum(jnp.log(t), axis=axis))
        key = jax.random.key(seed)
        ks = jax.random.split(key, 8)
        b, n = (2, 512)
        x = jax.random.normal(ks[0], (b, n, DIM), dtype=jnp.float32)
        gamma = jnp.ones((DIM,), dtype=jnp.float32)
        w_qkv = jax.random.normal(ks[1], (DIM, 3 * DIM_INNER), dtype=jnp.float32) * 0.02
        b_qkv = jnp.zeros((3 * DIM_INNER,), dtype=jnp.float32)
        w_a = jax.random.normal(ks[2], (DIM, DIM_INNER), dtype=jnp.float32) * 0.02
        b_a = jnp.full((DIM_INNER,), 2.0, dtype=jnp.float32)
        w_out = jax.random.normal(ks[3], (DIM_INNER, DIM), dtype=jnp.float32) * 0.02
        b_out = jnp.zeros((DIM,), dtype=jnp.float32)
        return {'x': x, 'gamma': gamma, 'w_qkv': w_qkv, 'b_qkv': b_qkv, 'w_a': w_a, 'b_a': b_a, 'w_out': w_out, 'b_out': b_out}
    _L0_attn_all = _L0_attn_setup()
    _L0_attn_in = {k: v for k, v in _L0_attn_all.items() if k in ('gamma', 'w_qkv', 'b_qkv', 'w_a', 'b_a', 'w_out', 'b_out')}
    del _L0_attn_all

    def _L0_ffn_setup():
        import jax, jax.numpy as jnp
        import numpy as np
        from jax import lax
        N_EXPERTS = 16
        TOP_K = 2
        D_MODEL = 128
        D_FF = 512
        key = jax.random.key(seed)
        ks = jax.random.split(key, 7)
        s_in = 1.0 / np.sqrt(D_MODEL)
        s_ff = 1.0 / np.sqrt(D_FF)
        x = jax.random.normal(ks[0], (2, 512, D_MODEL), dtype=jnp.float32)
        router_w = jax.random.uniform(ks[1], (N_EXPERTS, D_MODEL), jnp.float32, -s_in, s_in)
        router_b = jax.random.uniform(ks[2], (N_EXPERTS,), jnp.float32, -s_in, s_in)
        w1 = jax.random.uniform(ks[3], (N_EXPERTS, D_FF, D_MODEL), jnp.float32, -s_in, s_in)
        b1 = jax.random.uniform(ks[4], (N_EXPERTS, D_FF), jnp.float32, -s_in, s_in)
        w2 = jax.random.uniform(ks[5], (N_EXPERTS, D_MODEL, D_FF), jnp.float32, -s_ff, s_ff)
        b2 = jax.random.uniform(ks[6], (N_EXPERTS, D_MODEL), jnp.float32, -s_ff, s_ff)
        return {'x': x, 'router_w': router_w, 'router_b': router_b, 'w1': w1, 'b1': b1, 'w2': w2, 'b2': b2}
    _L0_ffn_all = _L0_ffn_setup()
    _L0_ffn_in = {k: v for k, v in _L0_ffn_all.items() if k in ('router_w', 'router_b', 'w1', 'b1', 'w2', 'b2')}
    del _L0_ffn_all
    return {'x': x, 'L0_tok_W': _L0_tok_in['W'], 'L0_tok_b': _L0_tok_in['b'], 'L0_tok_gamma': _L0_tok_in['gamma'], 'L0_tok_beta': _L0_tok_in['beta'], 'L0_attn_gamma': _L0_attn_in['gamma'], 'L0_attn_w_qkv': _L0_attn_in['w_qkv'], 'L0_attn_b_qkv': _L0_attn_in['b_qkv'], 'L0_attn_w_a': _L0_attn_in['w_a'], 'L0_attn_b_a': _L0_attn_in['b_a'], 'L0_attn_w_out': _L0_attn_in['w_out'], 'L0_attn_b_out': _L0_attn_in['b_out'], 'L0_ffn_router_w': _L0_ffn_in['router_w'], 'L0_ffn_router_b': _L0_ffn_in['router_b'], 'L0_ffn_w1': _L0_ffn_in['w1'], 'L0_ffn_b1': _L0_ffn_in['b1'], 'L0_ffn_w2': _L0_ffn_in['w2'], 'L0_ffn_b2': _L0_ffn_in['b2']}

def reference(x, L0_tok_W, L0_tok_b, L0_tok_gamma, L0_tok_beta, L0_attn_gamma, L0_attn_w_qkv, L0_attn_b_qkv, L0_attn_w_a, L0_attn_b_a, L0_attn_w_out, L0_attn_b_out, L0_ffn_router_w, L0_ffn_router_b, L0_ffn_w1, L0_ffn_b1, L0_ffn_w2, L0_ffn_b2):
    import jax
    import jax.numpy as jnp

    def _L0_tok_ref(x, W, b, gamma, beta):
        import jax, jax.numpy as jnp
        import numpy as np
        TOKEN_SIZE = 16
        STRIDE = 8
        EMBED_DIM = 128
        B, S, D = x.shape
        n_win = (S - TOKEN_SIZE) // STRIDE + 1
        idx = jnp.arange(n_win)[:, None] * STRIDE + jnp.arange(TOKEN_SIZE)[None, :]
        win = x[:, idx, :]
        win = win.reshape(B, n_win, TOKEN_SIZE * D)
        h = jnp.einsum('bnf,fd->bnd', win, W) + b
        h = jax.nn.gelu(h, approximate=False)
        mu = jnp.mean(h, axis=-1, keepdims=True)
        var = jnp.var(h, axis=-1, keepdims=True)
        h = (h - mu) * jax.lax.rsqrt(var + 1e-05)
        return h * gamma + beta

    def _L0_attn_ref(x, gamma, w_qkv, b_qkv, w_a, b_a, w_out, b_out):
        import jax, jax.numpy as jnp
        import numpy as np
        DIM = 128
        HEADS = 8
        DIM_HEAD = 64
        DIM_INNER = HEADS * DIM_HEAD
        FRAC_GRAD = 0.5
        SCALE = DIM_HEAD ** (-0.5)
        EPS_CUMPROD = 1e-10
        EPS_INV = 1e-08

        def _rms_norm(x, gamma):
            nrm = jnp.linalg.norm(x, axis=-1, keepdims=True)
            return x / jnp.maximum(nrm, 1e-12) * DIM ** 0.5 * gamma

        def _safe_cumprod(t, axis):
            t = jnp.clip(t, EPS_CUMPROD, 1.0)
            return jnp.exp(jnp.cumsum(jnp.log(t), axis=axis))
        b, n, _ = x.shape
        x = _rms_norm(x, gamma)
        qkv = x @ w_qkv + b_qkv
        qkv = qkv.reshape(b, n, 3, HEADS, DIM_HEAD).transpose(2, 0, 3, 1, 4)
        q, k, v = (qkv[0], qkv[1], qkv[2])
        q = q * SCALE
        a = (x @ w_a + b_a).reshape(b, n, HEADS, DIM_HEAD).transpose(0, 2, 1, 3)
        a = a * FRAC_GRAD + jax.lax.stop_gradient(a) * (1.0 - FRAC_GRAD)
        a = jax.nn.sigmoid(a)
        a_cum = _safe_cumprod(a, axis=-2)
        a_cum_inv = 1.0 / jnp.maximum(a_cum, EPS_INV)
        q = q * a_cum
        k = k * a_cum_inv
        sim = jnp.einsum('bhid,bhjd->bhij', q, k)
        causal_mask = jnp.triu(jnp.ones((n, n), dtype=bool), k=1)
        attn = jnp.where(causal_mask, 0.0, sim)
        out = jnp.einsum('bhij,bhjd->bhid', attn, v)
        out = out.transpose(0, 2, 1, 3).reshape(b, n, DIM_INNER)
        return out @ w_out + b_out

    def _L0_ffn_ref(x, router_w, router_b, w1, b1, w2, b2):
        import jax, jax.numpy as jnp
        import numpy as np
        from jax import lax
        N_EXPERTS = 16
        TOP_K = 2
        D_MODEL = 128
        D_FF = 512
        B, S, D = x.shape
        xt = x.reshape(-1, D)
        logits = xt @ router_w.T + router_b
        probs = jax.nn.softmax(logits, axis=-1)
        topk_p, topk_i = lax.top_k(probs, TOP_K)
        onehot = jax.nn.one_hot(topk_i, N_EXPERTS, dtype=probs.dtype)
        gates = jnp.sum(onehot * topk_p[..., None], axis=1)

        def expert_step(acc, packed):
            w1e, b1e, w2e, b2e, ge = packed
            h = jax.nn.gelu(xt @ w1e.T + b1e, approximate=False)
            y = h @ w2e.T + b2e
            return (acc + y * ge[:, None], None)
        out, _ = lax.scan(expert_step, jnp.zeros_like(xt), (w1, b1, w2, b2, gates.T))
        return out.reshape(B, S, D)
    h = _L0_tok_ref(x, L0_tok_W, L0_tok_b, L0_tok_gamma, L0_tok_beta)
    h = h + _L0_attn_ref(_layernorm(h, axis=-1), L0_attn_gamma, L0_attn_w_qkv, L0_attn_b_qkv, L0_attn_w_a, L0_attn_b_a, L0_attn_w_out, L0_attn_b_out)
    h = h + _L0_ffn_ref(_layernorm(h, axis=-1), L0_ffn_router_w, L0_ffn_router_b, L0_ffn_w1, L0_ffn_b1, L0_ffn_w2, L0_ffn_b2)
    return h

_drawn_inputs = setup_inputs


def setup_inputs(seed=0):
    import zlib

    import numpy as np

    out = dict(_drawn_inputs(seed))
    spreads = {'L0_tok_b': (0.0, 0.1),
     'L0_tok_gamma': (1.0, 0.2),
     'L0_tok_beta': (0.0, 0.1),
     'L0_attn_gamma': (1.0, 0.6),
     'L0_attn_b_qkv': (0.0, 0.499),
     'L0_attn_b_a': (2.0, 0.6),
     'L0_attn_b_out': (0.0, 0.1)}
    factors = {'L0_attn_w_qkv': 2.739,
     'L0_attn_w_a': 8.0,
     'L0_ffn_router_b': 6.039,
     'L0_ffn_b1': 29.214,
     'L0_ffn_b2': 8.0}
    for name, (base, spread) in spreads.items():
        noise = np.random.default_rng([zlib.crc32(name.encode()), seed]).standard_normal(out[name].shape)
        drawn = base * np.exp(spread * noise) if base else spread * noise
        out[name] = jnp.asarray(drawn.astype(out[name].dtype))
    for name, factor in factors.items():
        out[name] = (out[name] * factor).astype(out[name].dtype)
    return out
```

```python
from contextlib import ExitStack

import concourse.bass as bass
from concourse import mybir

F32 = mybir.dt.float32
F32R = mybir.dt.float32r
U32 = mybir.dt.uint32
I32 = mybir.dt.int32
ALU = mybir.AluOpType
ACT = mybir.ActivationFunctionType
AX_X = mybir.AxisListType.X

BATCH, SEQ, D = 32, 750, 128
TOKEN_SIZE, STRIDE = 16, 8
WIN = (SEQ - TOKEN_SIZE) // STRIDE + 1
CELLS = WIN + TOKEN_SIZE // STRIDE - 1
HALVES = TOKEN_SIZE // STRIDE
HEADS, DH = 8, 64
INNER = HEADS * DH
CHUNKS = INNER // 128
EXPERTS, FF = 16, 512
FFC = FF // 128
TOKENS = BATCH * WIN

GB = 4
GROUPS = BATCH // GB
GT = GB * WIN

BLOCK = 128
CAP = TOKENS + BLOCK
CAP += -CAP % BLOCK
BLOCKS = (2 * TOKENS + EXPERTS * (BLOCK - 1)) // BLOCK
DUMMY = EXPERTS * CAP
ROW = D + 2
NO_ROW = 2 * TOKENS

EPS = 1e-5
SCAN_CAP = 3.0e38
SHIFT = 2.0 ** -64
SCALE = DH ** -0.5

CONST = {}
CONST_COLS = 0
for _name, _n in (("ident", 128), ("causal", GT), ("before", WIN), ("ones", WIN), ("scan_cap", GB * (WIN + 1)),
                  ("first_row", GB * EXPERTS), ("expert", GB * EXPERTS), ("result_row", 2 * GB), ("power", 8)):
    CONST[_name] = (CONST_COLS, _n)
    CONST_COLS += _n

ROWS = {}
ROWS_COLS = 0
for _name, _n in (("gamma", D), ("beta", D), ("b_out", D), ("b_v", INNER), ("router_b", GB * EXPERTS)):
    ROWS[_name] = (ROWS_COLS, _n)
    ROWS_COLS += _n

COLS = {}
COLS_COLS = 0
for _name, _n in (("tok_b", 1), ("attn_gamma", 1), ("b_q", CHUNKS), ("b_k", CHUNKS), ("b_a", CHUNKS),
                  ("b1", EXPERTS * FFC), ("router_w", EXPERTS)):
    COLS[_name] = (COLS_COLS, _n)
    COLS_COLS += _n


SLOTS = 8
OUT_STEPS = 4
OB = BATCH // OUT_STEPS
X_SPLIT = 2 * GB * CELLS


def at(n, size=1):
    return bass.ds(n, size) if not isinstance(n, int) else slice(n, n + size)


def build(nc, x, tok_w, proj_w, out_w, w1, w2, b2, consts, rows, cols, block_nos, out):
    ctx = ExitStack()
    phase_1 = ExitStack()
    phase_2 = ExitStack()
    phase_3 = ExitStack()

    def sb(name, shape, dt=F32, stack=ctx):
        return stack.enter_context(nc.sbuf_tensor(name, shape, dt))

    def sem(name):
        return ctx.enter_context(nc.semaphore(name))

    with ctx:
        const = sb("const", [128, CONST_COLS])
        row = sb("row", [WIN, ROWS_COLS])
        col = sb("col", [128, COLS_COLS])

        def const_of(name, p=128):
            a, n = CONST[name]
            return const[0:p, a:a + n]

        def row_of(name):
            a, n = ROWS[name]
            return row[:, a:a + n]

        def col_of(name, i=0):
            return col[:, COLS[name][0] + i:COLS[name][0] + i + 1]

        ident = const_of("ident")
        neg_b_a = sb("neg_b_a", [128, CHUNKS])
        pw_hi = sb("pw_hi", [128, 4 * INNER], F32R)
        pw_lo = sb("pw_lo", [128, 4 * INNER], F32R)
        xsT_hi = sb("xsT_hi", [128, TOKENS], F32R)
        xsT_lo = sb("xsT_lo", [128, TOKENS], F32R)
        h_all = sb("h_all", [WIN, BATCH * D])
        pad = sb("pad", [128, ROW])
        running = sb("running", [WIN, GB + 1, EXPERTS])

        XG = STRIDE * GB * CELLS
        x_raw = [sb(f"x_raw{u}", [128, XG], stack=phase_1) for u in range(2)]
        x_hi = [sb(f"x_hi{u}", [128, XG], F32R, phase_1) for u in range(2)]
        x_lo = [sb(f"x_lo{u}", [128, XG], F32R, phase_1) for u in range(2)]
        tw_raw = sb("tw_raw", [128, TOKEN_SIZE * D], stack=phase_1)
        tw_hi = sb("tw_hi", [128, TOKEN_SIZE * D], F32R, phase_1)
        tw_lo = sb("tw_lo", [128, TOKEN_SIZE * D], F32R, phase_1)
        pw_raw = sb("pw_raw", [128, 4 * INNER], stack=phase_1)
        geluT = [sb(f"geluT{u}", [128, GT], stack=phase_1) for u in range(2)]
        normed = [sb(f"normed{u}", [WIN, GB * D], stack=phase_1) for u in range(2)]
        scaled = sb("scaled", [WIN, GB * D], stack=phase_1)
        xs = [sb(f"xs{u}", [WIN, GB * D], stack=phase_1) for u in range(2)]
        stat1 = sb("stat1", [WIN, GB, 6], stack=phase_1)
        mv1 = sb("mv1", [WIN, GB, 2], stack=phase_1)
        var1 = sb("var1", [WIN, GB], stack=phase_1)
        neg_mean1 = sb("neg_mean1", [WIN, GB], stack=phase_1)
        rstd1 = sb("rstd1", [WIN, GB], stack=phase_1)
        shift1 = sb("shift1", [WIN, GB], stack=phase_1)
        stat2 = sb("stat2", [WIN, GB, 6], stack=phase_1)
        mv2 = sb("mv2", [WIN, 2, GB, 2], stack=phase_1)
        base2 = sb("base2", [WIN, 2 * GB], stack=phase_1)
        root2 = sb("root2", [WIN, 2 * GB], stack=phase_1)
        norm2 = sb("norm2", [WIN, 3, GB], stack=phase_1)
        scale2 = sb("scale2", [WIN, GB], stack=phase_1)
        phase_1.close()

        w1_all = sb("w1_all", [128, EXPERTS * FF])
        w2_all = sb("w2_all", [128, EXPERTS * FF])
        b2_all = sb("b2_all", [128, EXPERTS * D])

        ow = sb("ow", [128, CHUNKS * D], stack=phase_2)
        decay = sb("decay", [128, GB, WIN + 1], stack=phase_2)
        grown = sb("grown", [128, GB, WIN + 1], stack=phase_2)
        log_grown = sb("log_grown", [128, GB, WIN], stack=phase_2)
        a_cum = [sb(f"a_cum{u}", [128, GB, WIN], stack=phase_2) for u in range(2)]
        a_inv = [sb(f"a_inv{u}", [128, GB, WIN], stack=phase_2) for u in range(2)]
        qT = [sb(f"qT{u}", [128, GT], stack=phase_2) for u in range(2)]
        kT = [sb(f"kT{u}", [128, GT], stack=phase_2) for u in range(2)]
        attnT = [sb(f"attnT{u}", [WIN, 2, GT], stack=phase_2) for u in range(2)]
        xv_hi = sb("xv_hi", [128, GT], F32R, phase_2)
        xv_lo = sb("xv_lo", [128, GT], F32R, phase_2)
        v = [sb(f"v{u}", [WIN, GB, INNER], stack=phase_2) for u in range(2)]
        oT = [[sb(f"oT{u}_{c}", [128, GT], stack=phase_2) for c in range(CHUNKS)] for u in range(2)]
        stat3 = sb("stat3", [WIN, GB, 6], stack=phase_2)
        mv3 = sb("mv3", [WIN, GB, 2], stack=phase_2)
        var3 = sb("var3", [WIN, GB], stack=phase_2)
        rstd3 = sb("rstd3", [WIN, GB], stack=phase_2)
        xm = [sb(f"xm{u}", [WIN, 2, GB, ROW], stack=phase_2) for u in range(2)]
        xmT = sb("xmT", [128, GT], stack=phase_2)
        logits = sb("logits", [WIN, GB, EXPERTS], stack=phase_2)
        top_logit = sb("top_logit", [WIN, GB], stack=phase_2)
        shifted = sb("shifted", [WIN, GB, EXPERTS], stack=phase_2)
        expd = sb("expd", [WIN, GB, EXPERTS], stack=phase_2)
        exp_sum = sb("exp_sum", [WIN, GB], stack=phase_2)
        exp_rec = sb("exp_rec", [WIN, GB], stack=phase_2)
        probs = sb("probs", [WIN, GB, EXPERTS], stack=phase_2)
        top8 = sb("top8", [WIN, GB, 8], stack=phase_2)
        top8_at = sb("top8_at", [WIN, GB, 8], U32, phase_2)
        top8_atf = sb("top8_atf", [WIN, GB, 8], stack=phase_2)
        chosen = sb("chosen", [WIN, 2, GB, EXPERTS], stack=phase_2)
        both = sb("both", [WIN, GB, EXPERTS], stack=phase_2)
        rank = sb("rank", [WIN, GB, EXPERTS], stack=phase_2)
        ranked = sb("ranked", [WIN, GB, EXPERTS], stack=phase_2)
        place = sb("place", [WIN, 2, GB, EXPERTS], stack=phase_2)
        place_f = sb("place_f", [WIN, 2 * GB], stack=phase_2)
        place_u = [sb(f"place_u{u}", [WIN, 2 * GB], U32, phase_2) for u in range(2)]
        phase_2.close()

        n_int = sb("n_int", [1, EXPERTS], I32, phase_3)
        tail_at = sb("tail_at", [1, EXPERTS], I32, phase_3)
        tail_f = sb("tail_f", [1, EXPERTS], stack=phase_3)
        nb_int = sb("nb_int", [1, EXPERTS], I32, phase_3)
        nb_f = sb("nb_f", [1, EXPERTS], stack=phase_3)
        zero16 = sb("zero16", [1, EXPERTS], stack=phase_3)
        nb_end = sb("nb_end", [1, EXPERTS], stack=phase_3)
        block_no = sb("block_no", [1, BLOCKS, EXPERTS], stack=phase_3)
        past = sb("past", [1, BLOCKS, EXPERTS], stack=phase_3)
        past_nb = sb("past_nb", [1, BLOCKS, EXPERTS], stack=phase_3)
        blk_e = sb("blk_e", [1, BLOCKS], stack=phase_3)
        blk_s = sb("blk_s", [1, BLOCKS], stack=phase_3)
        blk_r = sb("blk_r", [1, BLOCKS], stack=phase_3)
        blk_q = sb("blk_q", [1, BLOCKS], stack=phase_3)
        blk_t = sb("blk_t", [1, BLOCKS], stack=phase_3)
        blk_expert = sb("blk_expert", [1, BLOCKS], I32, phase_3)
        blk_row = sb("blk_row", [1, BLOCKS], I32, phase_3)
        xb = [sb(f"xb{u}", [128, ROW], stack=phase_3) for u in range(SLOTS)]
        xbT = [sb(f"xbT{u}", [128, BLOCK], stack=phase_3) for u in range(2)]
        w1_blk = [sb(f"w1_blk{u}", [128, FF], stack=phase_3) for u in range(2)]
        hT = [sb(f"hT{u}", [128, FFC, BLOCK], stack=phase_3) for u in range(2)]
        yb = [sb(f"yb{u}", [128, D], stack=phase_3) for u in range(2)]
        yg = [sb(f"yg{u}", [128, D], stack=phase_3) for u in range(SLOTS)]
        y1 = [sb(f"y1_{k}", [WIN, OB, D], stack=phase_3) for k in range(OUT_STEPS)]
        y2 = [sb(f"y2_{k}", [WIN, OB, D], stack=phase_3) for k in range(OUT_STEPS)]
        phase_3.close()

        bank = [ctx.enter_context(nc.psum_tensor(f"bank{i}", [128, 512], F32)) for i in range(8)]

        sorted_rows = nc.dram_tensor("sorted_rows", (DUMMY + BLOCK, ROW), F32).ap()
        results = nc.dram_tensor("results", (2 * TOKENS, D), F32).ap()

        x_in0 = sem("x_in0")
        tw_in = sem("tw_in")
        const_in = sem("const_in")
        x_in1 = sem("x_in1")
        pw_in = sem("pw_in")
        lo_v_done = sem("lo_v_done")
        lo_p_done = sem("lo_p_done")
        xsT_done = sem("xsT_done")
        pw_done = sem("pw_done")
        ow_in = sem("ow_in")
        experts_in = sem("experts_in")
        placed_done = sem("placed_done")
        scattered0 = sem("scattered0")
        scattered1 = sem("scattered1")
        block_no_in = sem("block_no_in")
        tail_done = sem("tail_done")
        tails_out = sem("tails_out")
        table_done = sem("table_done")
        out_ready = sem("out_ready")
        out_done = sem("out_done")
        tw_done = sem("tw_done")
        gelu_done = sem("gelu_done")
        normed_done = sem("normed_done")
        t1_done = sem("t1_done")
        xs_done = sem("xs_done")
        t2_done = sem("t2_done")
        main_done = sem("main_done")
        v_done = sem("v_done")
        a_done = sem("a_done")
        xv_done = sem("xv_done")
        vT_done = sem("vT_done")
        e_done = sem("e_done")
        qT_done = sem("qT_done")
        q_done = sem("q_done")
        kT_done = sem("kT_done")
        k_done = sem("k_done")
        xm_done = sem("xm_done")
        xmT_ps = sem("xmT_ps")
        attn_done = sem("attn_done")
        sim_done = sem("sim_done")
        both_done = sem("both_done")
        h2_done = sem("h2_done")
        prefix_ps = sem("prefix_ps")
        oT_done = sem("oT_done")
        av_done = sem("av_done")
        xmT_done = sem("xmT_done")
        router_ps = sem("router_ps")
        logits_done = sem("logits_done")
        proj_done = sem("proj_done")
        xT_ps = sem("xT_ps")
        xT_done = sem("xT_done")
        w1_done = sem("w1_done")
        hidden_ps = sem("hidden_ps")
        hidden_done = sem("hidden_done")
        yb_done = sem("yb_done")
        y_ps = sem("y_ps")
        hi_done = sem("hi_done")
        tw_hi_done = sem("tw_hi_done")
        pw_scaled = sem("pw_scaled")
        pw_hi_done = sem("pw_hi_done")
        shift1_done = sem("shift1_done")
        h_done = sem("h_done")
        xsT_hi_done = sem("xsT_hi_done")
        neg_b_done = sem("neg_b_done")
        scan_done = sem("scan_done")
        log_done = sem("log_done")
        cum_done = sem("cum_done")
        shifted_done = sem("shifted_done")
        exp_done = sem("exp_done")
        pad_done = sem("pad_done")
        running_done = sem("running_done")
        stat1_done = sem("stat1_done")
        mv1_done = sem("mv1_done")
        var1_done = sem("var1_done")
        stat2_done = sem("stat2_done")
        mv2_done = sem("mv2_done")
        base2_done = sem("base2_done")
        root2_done = sem("root2_done")
        length_done = sem("length_done")
        guarded_done = sem("guarded_done")
        inverse_done = sem("inverse_done")
        scale2_done = sem("scale2_done")
        setup_done = sem("setup_done")
        clip_done = sem("clip_done")
        inv_done = sem("inv_done")
        hb_done = sem("hb_done")
        stat3_done = sem("stat3_done")
        mv3_done = sem("mv3_done")
        var3_done = sem("var3_done")
        rstd3_done = sem("rstd3_done")
        dest_done = sem("dest_done")
        top_logit_done = sem("top_logit_done")
        sum_done = sem("sum_done")
        rec_done = sem("rec_done")
        probs_done = sem("probs_done")
        top8_done = sem("top8_done")
        top8_at_done = sem("top8_at_done")
        gates_done = sem("gates_done")
        top8_atf_done = sem("top8_atf_done")
        chosen_done = sem("chosen_done")
        rank_done = sem("rank_done")
        ranked_done = sem("ranked_done")
        place_done = sem("place_done")
        place_f_done = sem("place_f_done")
        tail_f_done = sem("tail_f_done")
        n_int_done = sem("n_int_done")
        nb_int_done = sem("nb_int_done")
        nb_f_done = sem("nb_f_done")
        nb_end_done = sem("nb_end_done")
        past_done = sem("past_done")
        past_nb_done = sem("past_nb_done")
        blk_e_done = sem("blk_e_done")
        blk_s_done = sem("blk_s_done")
        blk_expert_done = sem("blk_expert_done")
        blk_r_done = sem("blk_r_done")
        blk_q_done = sem("blk_q_done")
        blk_t_done = sem("blk_t_done")
        yg_done = sem("yg_done")
        sum_done2 = sem("sum_done2")
        rstd1_done = sem("rstd1_done")
        scaled_done = sem("scaled_done")
        pool_go = sem("pool_go")
        xm_twice = sem("xm_twice")
        x_in = (x_in0, x_in1)
        scattered = (scattered0, scattered1)
        xb_in = [sem(f"xb_in{u}") for u in range(SLOTS)]
        y_out = [sem(f"y_out{u}") for u in range(SLOTS)]
        y_in = [sem(f"y_in{k}") for k in range(OUT_STEPS)]

        ident_w = const[0:WIN, CONST["ident"][0]:CONST["ident"][0] + WIN]
        causal = const_of("causal", WIN)
        power = const_of("power", WIN)
        result_row = const_of("result_row", WIN)
        expert_no = const_of("expert", WIN).rearrange("p (b e) -> p b e", b=GB)
        first_row = const_of("first_row", WIN).rearrange("p (b e) -> p b e", b=GB)
        b_a = col[:, COLS["b_a"][0]:COLS["b_a"][0] + CHUNKS]
        b1_all = col[:, COLS["b1"][0]:COLS["b1"][0] + EXPERTS * FFC]
        router_w = col[:, COLS["router_w"][0]:COLS["router_w"][0] + EXPERTS]

        def by_row(a):
            return a.rearrange("p (b d) -> p b d", b=GB)

        def each_row(name):
            return row_of(name).unsqueeze(1).to_broadcast([WIN, GB, D])

        def spread(a):
            return a.unsqueeze(2).to_broadcast([WIN, GB, EXPERTS])

        block = ctx.enter_context(nc.Block())

        def tokenizer_steps(eng, step):
            for g in range(3):
                step(g, g % 2, g)
            with eng.Fori(0, 2) as i:
                for k in range(2):
                    step(i * 2 + 3 + k, (3 + k) % 2, 3)
            for g in range(7, GROUPS + 3):
                step(g, g % 2, g)

        def attention_groups(eng, body):
            for g in range(3):
                body(g, g % 2, g)
            with eng.Fori(0, 2) as i:
                for k in range(2):
                    body(i * 2 + 3 + k, (3 + k) % 2, 3)
            for g in range(7, GROUPS + 3):
                body(g, g % 2, g)

        def expert_steps(eng, step):
            step(0, 0, 0)
            step(1, 1, 1)
            loops = (BLOCKS - 3) // SLOTS
            with eng.Fori(0, loops) as i:
                for k in range(SLOTS):
                    step(i * SLOTS + 2 + k, (2 + k) % SLOTS, 2)
            for j in range(loops * SLOTS + 2, BLOCKS + 1):
                step(j, j % SLOTS, j)

        def has_group(role, lag):
            return 0 <= role - lag < GROUPS

        def has_unit(role, c, lag):
            return 0 <= CHUNKS * role + c - lag < CHUNKS * GROUPS

        def has_block(role, lag):
            return 0 <= role - lag < BLOCKS
        @block.sync
        def _(sp):
            sp.dma_start(x_raw[0][:], x[0]).then_inc(x_in0, 16)
            sp.dma_start(tw_raw[:], tok_w).then_inc(tw_in, 16)
            sp.dma_start(const[:], consts).then_inc(const_in, 16)
            sp.dma_start(row[:], rows).then_inc(const_in, 16)
            sp.dma_start(col[:], cols).then_inc(const_in, 16)
            sp.dma_start(x_raw[1][:], x[1]).then_inc(x_in1, 16)
            sp.dma_start(pw_raw[:], proj_w).then_inc(pw_in, 16)
            with sp.Fori(0, GROUPS // 2 - 1) as i:
                for u in range(2):
                    sp.wait_ge(lo_v_done, i * 2 + u + 1)
                    sp.wait_ge(lo_p_done, i * 2 + u + 1)
                    sp.dma_start(x_raw[u][:], x[at(i * 2 + 2 + u), :, :].rearrange("a p n -> (a p) n")).then_inc(x_in[u], 16)
            sp.wait_ge(xsT_done, GROUPS)
            sp.wait_ge(pw_done, 1)
            sp.dma_start(ow[:], out_w).then_inc(ow_in, 16)
            sp.dma_start(w1_all[:], w1).then_inc(experts_in, 16)
            sp.dma_start(w2_all[:], w2).then_inc(experts_in, 16)
            sp.dma_start(b2_all[:], b2).then_inc(experts_in, 16)
            sp.wait_ge(placed_done, GROUPS)
            sp.wait_ge(scattered0, GROUPS * GB * 16 + 16)
            sp.wait_ge(scattered1, GROUPS * GB * 16 + 16)
            sp.dma_start(block_no[:], block_nos).then_inc(block_no_in, 16)
            sp.wait_ge(tail_done, 1)
            for e in range(EXPERTS):
                start = sp.value_load(tail_at[0:1, e:e + 1], min_val=e * CAP, max_val=e * CAP + TOKENS)
                sp.dma_start(sorted_rows[bass.ds(start, BLOCK), :], pad[:]).then_inc(tails_out, 16)
            sp.wait_ge(tails_out, EXPERTS * 16)
            sp.wait_ge(table_done, 1)

            def load_block(j, slot):
                start = sp.value_load(blk_row[0:1, at(j)], min_val=0, max_val=DUMMY)
                sp.dma_start(xb[slot][:], sorted_rows[bass.ds(start, BLOCK), :]).then_inc(xb_in[slot], 16)

            for j in range(SLOTS):
                load_block(j, j)
            rounds = BLOCKS // SLOTS - 1
            with sp.Fori(0, rounds) as i:
                for k in range(SLOTS):
                    sp.wait_ge(y_out[k], i * 16 + 16)
                    load_block(i * SLOTS + SLOTS + k, k)
            for j in range((rounds + 1) * SLOTS, BLOCKS):
                sp.wait_ge(y_out[j % SLOTS], j // SLOTS * 16)
                load_block(j, j % SLOTS)
            for u in range(SLOTS):
                sp.wait_ge(y_out[u], 16 * len(range(u, BLOCKS, SLOTS)))
            for k in range(OUT_STEPS):
                for t, y in enumerate((y1[k], y2[k])):
                    a = t * TOKENS + k * OB * WIN
                    sp.dma_start(y[:], results[a:a + OB * WIN, :].rearrange("(b i) d -> i b d", i=WIN)).then_inc(y_in[k], 16)
            for k in range(OUT_STEPS):
                sp.wait_ge(out_ready, k + 1)
                sp.dma_start(out[k * OB:(k + 1) * OB].rearrange("b i d -> i b d"), y1[k][:]).then_inc(out_done, 16)
            sp.wait_ge(out_done, 16 * OUT_STEPS)

        @block.tensor
        def _(pe):
            def split_matmul(dst, w_hi, w_lo, m_hi, m_lo, first, last):
                pe.matmul(dst, w_hi, m_hi, start=first, stop=False)
                pe.matmul(dst, w_hi, m_lo, start=False, stop=False)
                return pe.matmul(dst, w_lo, m_hi, start=False, stop=last)

            pe.wait_ge(tw_done, 1)
            pe.wait_ge(const_in, 48)

            def step(g, u, role):
                def windows(t, r, half):
                    return t[:].rearrange("p (r b n) -> p r b n", r=STRIDE, b=GB)[:, r, :, half:half + WIN]

                def main(r0, r1):
                    for r in range(r0, r1):
                        for half in range(HALVES):
                            w = slice((half * STRIDE + r) * D, (half * STRIDE + r + 1) * D)
                            mm = split_matmul(bank[u][:, 0:GT], tw_hi[:, w], tw_lo[:, w], windows(x_hi[u], r, half),
                                              windows(x_lo[u], r, half), r == 0 and half == 0,
                                              r == STRIDE - 1 and half == HALVES - 1)
                    return mm

                if has_group(role, 0):
                    pe.wait_ge(lo_v_done, g + 1)
                    pe.wait_ge(lo_p_done, g + 1)
                    if has_group(role, 2):
                        pe.wait_ge(gelu_done, g - 1)
                    main(0, 2)
                if has_group(role, 1):
                    pe.wait_ge(gelu_done, g)
                    if has_group(role, 2):
                        pe.wait_ge(normed_done, g - 1)
                    for b in range(GB):
                        mm = pe.transpose(bank[2][0:WIN, b * D:(b + 1) * D], geluT[1 - u][:, b * WIN:(b + 1) * WIN], ident)
                    mm.then_inc(t1_done, 1)
                if has_group(role, 0):
                    main(2, 5)
                if has_group(role, 3):
                    pe.wait_ge(xs_done, g - 2)
                    for b in range(GB):
                        mm = pe.transpose(bank[3][:, b * WIN:(b + 1) * WIN], xs[1 - u][:, b * D:(b + 1) * D], ident_w)
                    mm.then_inc(t2_done, 1)
                if has_group(role, 0):
                    main(5, STRIDE).then_inc(main_done, 1)

            tokenizer_steps(pe, step)

            pe.wait_ge(xsT_done, GROUPS)
            pe.wait_ge(normed_done, GROUPS)
            pe.wait_ge(pw_done, 1)

            def project(dst, first_col, g):
                w = slice(first_col, first_col + 128)
                t = at(g * GT, GT)
                return split_matmul(dst[:, 0:GT], pw_hi[:, w], pw_lo[:, w], xsT_hi[:, t], xsT_lo[:, t], True, True)

            def project_v(b):
                t = slice(b * WIN, (b + 1) * WIN)
                w = slice(2 * INNER, 3 * INNER)
                pe.matmul(bank[5][0:WIN, :], xv_hi[:, t], pw_hi[:, w], start=True, stop=False)
                pe.matmul(bank[5][0:WIN, :], xv_lo[:, t], pw_hi[:, w], start=False, stop=False)
                pe.matmul(bank[5][0:WIN, :], xv_hi[:, t], pw_lo[:, w], start=False, stop=True).then_inc(v_done, 1)

            project(bank[0], 3 * INNER, 0).then_inc(a_done, 1)
            for b in range(2):
                pe.wait_ge(xv_done, 1)
                if b:
                    pe.wait_ge(vT_done, b)
                project_v(b)

            def body(g, u, role):
                for c in range(CHUNKS):
                    n = g * CHUNKS + c
                    if has_unit(role, c, -1):
                        if has_unit(role, c, 0):
                            pe.wait_ge(e_done, n + 1)
                        project(bank[0], 3 * INNER + (c + 1) % CHUNKS * 128, g if c + 1 < CHUNKS else g + 1).then_inc(a_done, 1)
                    if has_unit(role, c, 0):
                        if has_unit(role, c, 1):
                            pe.wait_ge(qT_done, n)
                        project(bank[1], c * 128, g).then_inc(q_done, 1)
                        if has_unit(role, c, 1):
                            pe.wait_ge(kT_done, n)
                        project(bank[4], INNER + c * 128, g).then_inc(k_done, 1)
                    if c == 1 and has_group(role, 2):
                        pe.wait_ge(xm_done, g - 1)
                        for b in range(GB):
                            mm = pe.transpose(bank[3][:, b * WIN:(b + 1) * WIN], xm[u][:, 0, b, 0:D], ident_w)
                        mm.then_inc(xmT_ps, 1)
                    if has_unit(role, c, 1):
                        pe.wait_ge(qT_done, n)
                        pe.wait_ge(kT_done, n)
                        if has_unit(role, c, 2):
                            pe.wait_ge(attn_done, n * 2 - 2)
                        for hd in range(2):
                            f = slice(hd * DH, (hd + 1) * DH)
                            for b in range(GB):
                                t = slice(b * WIN, (b + 1) * WIN)
                                mm = pe.matmul(bank[6 + hd][0:WIN, t], kT[(c + 1) % 2][f, t], qT[(c + 1) % 2][f, t],
                                               start=True, stop=True)
                            mm.then_inc(sim_done, 1)
                    if c == 0 and has_group(role, 3):
                        pe.wait_ge(both_done, g - 2)
                        if has_group(role, 2):
                            pe.wait_ge(h2_done, g - 1)
                        m = both[:].rearrange("p b e -> p (b e)")
                        pe.matmul(bank[3][0:WIN, 0:GB * EXPERTS], const_of("before", WIN), m, start=True, stop=True)
                        pe.matmul(bank[3][0:WIN, 256:256 + GB * EXPERTS], const_of("ones", WIN), m, start=True,
                                  stop=True).then_inc(prefix_ps, 1)
                    if has_unit(role, c, -2) and (c + 2) // CHUNKS + role < GROUPS:
                        pe.wait_ge(vT_done, n + 2)
                        if c == 2:
                            pe.wait_ge(xv_done, g + 2)
                        project_v((c + 2) % CHUNKS)
                    if has_unit(role, c, 2):
                        pe.wait_ge(attn_done, n * 2 - 2)
                        if has_unit(role, c, 3):
                            pe.wait_ge(oT_done, n - 2)
                        if c == 2:
                            pe.wait_ge(vT_done, (g + 1) * GB)
                        w = u if c >= 2 else 1 - u
                        for hd in range(2):
                            h0 = (2 * ((c + 2) % CHUNKS) + hd) * DH
                            for b in range(GB):
                                t = slice(b * WIN, (b + 1) * WIN)
                                mm = pe.matmul(bank[2][hd * DH:(hd + 1) * DH, t], v[w][:, b, h0:h0 + DH],
                                               attnT[c % 2][:, hd, t], start=True, stop=True)
                        mm.then_inc(av_done, 1)
                    if c == 1 and has_group(role, 2):
                        pe.wait_ge(xmT_done, g - 1)
                        for b in range(GB):
                            mm = pe.matmul(bank[3][0:WIN, b * EXPERTS:(b + 1) * EXPERTS], xmT[:, b * WIN:(b + 1) * WIN],
                                           router_w, start=True, stop=True)
                        mm.then_inc(router_ps, 1)
                    if c == 2 and has_group(role, 1):
                        pe.wait_ge(oT_done, g * CHUNKS)
                        if has_group(role, 2):
                            pe.wait_ge(logits_done, g - 1)
                        if role == 1:
                            pe.wait_ge(ow_in, 16)
                        for b in range(GB):
                            for k in range(CHUNKS):
                                mm = pe.matmul(bank[3][0:WIN, b * D:(b + 1) * D], oT[1 - u][k][:, b * WIN:(b + 1) * WIN],
                                               ow[:, k * D:(k + 1) * D], start=k == 0, stop=k == CHUNKS - 1)
                        mm.then_inc(proj_done, 1)

            attention_groups(pe, body)

            def turn_block(j, slot):
                pe.transpose(bank[slot % 2][:, 0:BLOCK], xb[slot][:, 0:D], ident).then_inc(xT_ps, 1)

            pe.wait_ge(xb_in[0], 16)
            turn_block(0, 0)
            pe.wait_ge(experts_in, 48)

            def block_step(j, slot, role):
                nxt = (slot + 1) % SLOTS
                if has_block(role, -1):
                    pe.wait_ge(xb_in[nxt], (j + 1 - nxt) * (16 // SLOTS) + 16)
                    if has_block(role, 1):
                        pe.wait_ge(xT_done, j)
                    turn_block(j + 1, nxt)
                if has_block(role, 0):
                    pe.wait_ge(xT_done, j + 1)
                    pe.wait_ge(w1_done, j + 1)
                    for f in range(FFC):
                        mm = pe.matmul(bank[4 + slot % 2][:, f * BLOCK:(f + 1) * BLOCK], w1_blk[slot % 2][:, f * 128:(f + 1) * 128],
                                       xbT[slot % 2][:], start=True, stop=True)
                    mm.then_inc(hidden_ps, 1)
                if has_block(role, 1):
                    p = (slot + 1) % 2
                    e = pe.value_load(blk_expert[0:1, at(j - 1)], min_val=0, max_val=EXPERTS - 1)
                    pe.wait_ge(hidden_done, j)
                    if has_block(role, 2):
                        pe.wait_ge(yb_done, j - 1)
                    for f in range(FFC):
                        mm = pe.matmul(bank[6 + p][:, 0:D], hT[p][:, f, :], w2_all[:, bass.ds(e * FF + f * D, D)],
                                       start=f == 0, stop=f == FFC - 1)
                    mm.then_inc(y_ps, 1)

            expert_steps(pe, block_step)

        @block.scalar
        def _(act):
            act.preload_act_table_set("gelu_and_others")

            def split_hi(g, u):
                act.activation(x_hi[u][:], x_raw[u][:], ACT.Copy).then_inc(hi_done, 1)

            act.wait_ge(tw_in, 16)
            act.activation(tw_hi[:], tw_raw[:], ACT.Copy).then_inc(tw_hi_done, 1)
            act.wait_ge(x_in0, 16)
            split_hi(0, 0)
            act.wait_ge(x_in1, 16)
            split_hi(1, 1)
            act.wait_ge(const_in, 48)
            act.wait_ge(pw_scaled, 1)
            act.activation(pw_hi[:], pw_raw[:], ACT.Copy).then_inc(pw_hi_done, 1)

            def step(g, u, role):
                if has_group(role, 1):
                    act.wait_ge(main_done, g)
                    if has_group(role, 3):
                        act.wait_ge(t1_done, g - 2)
                    act.activation(geluT[1 - u][:], bank[1 - u][:, 0:GT], ACT.Gelu, bias=col_of("tok_b")).then_inc(gelu_done, 1)
                if has_group(role, 1) and has_group(role, -1):
                    act.wait_ge(x_in[1 - u], g * 8 + (24 if u else 16))
                    split_hi(g + 1, 1 - u)
                if has_group(role, 1):
                    act.wait_ge(shift1_done, g)
                    if has_group(role, 3):
                        act.wait_ge(h_done, g - 2)
                    for b in range(GB):
                        ins = act.activation(normed[1 - u][:, b * D:(b + 1) * D], bank[2][0:WIN, b * D:(b + 1) * D], ACT.Identity,
                                             bias=shift1[:, b:b + 1], scale=rstd1[:, b:b + 1])
                    ins.then_inc(normed_done, 1)
                if has_group(role, 3):
                    act.wait_ge(t2_done, g - 2)
                    act.activation(xsT_hi[:, at((g - 3) * GT, GT)], bank[3][:, 0:GT], ACT.Copy).then_inc(xsT_hi_done, 1)

            tokenizer_steps(act, step)

            act.preload_act_table_set("natural_log_exp_and_others")
            act.wait_ge(xsT_done, GROUPS)
            act.wait_ge(neg_b_done, 1)

            def decay_exp(c, n_next, first):
                act.wait_ge(a_done, n_next)
                if not first:
                    act.wait_ge(scan_done, n_next - 1)
                act.activation(decay[:, :, 1:WIN + 1], bank[0][:, 0:GT].rearrange("p (b i) -> p b i", b=GB), ACT.Exp,
                               bias=neg_b_a[:, c:c + 1], scale=-1.0).then_inc(e_done, 1)

            def decay_cum(c, n_next, reused):
                act.wait_ge(scan_done, n_next)
                act.activation(log_grown[:], grown[:, :, 1:WIN + 1], ACT.Ln, scale=SHIFT).then_inc(log_done, 1)
                act.wait_ge(log_done, n_next)
                if reused:
                    act.wait_ge(qT_done, n_next - 2)
                act.activation(a_cum[c % 2][:], log_grown[:], ACT.Exp, scale=-1.0).then_inc(cum_done, 1)

            decay_exp(0, 1, True)
            decay_cum(0, 1, False)

            def body(g, u, role):
                for c in range(CHUNKS):
                    n = g * CHUNKS + c
                    nc_ = (c + 1) % CHUNKS
                    if has_unit(role, c, 3):
                        act.wait_ge(av_done, n - 2)
                        w, k = (u, 0) if c == 3 else (1 - u, c + 1)
                        if has_group(role, 2):
                            act.wait_ge(proj_done, g - 1)
                        act.activation(oT[w][k][:], bank[2][:, 0:GT], ACT.Copy).then_inc(oT_done, 1)
                    if has_unit(role, c, -1):
                        decay_exp(nc_, n + 2, False)
                    if c == 1 and has_group(role, 2):
                        act.wait_ge(xmT_ps, g - 1)
                        act.activation(xmT[:], bank[3][:, 0:GT], ACT.Copy).then_inc(xmT_done, 1)
                    if c == 3 and has_group(role, 2):
                        act.wait_ge(shifted_done, g - 1)
                        act.activation(expd[:], shifted[:], ACT.Exp).then_inc(exp_done, 1)
                    if has_unit(role, c, -1):
                        decay_cum(nc_, n + 2, has_unit(role, c, 1))

            attention_groups(act, body)

            act.preload_act_table_set("gelu_and_others")
            act.wait_ge(table_done, 1)

            def block_step(j, slot, role):
                if has_block(role, 0):
                    p = slot % 2
                    e = act.value_load(blk_expert[0:1, at(j)], min_val=0, max_val=EXPERTS - 1)
                    act.wait_ge(hidden_ps, j + 1)
                    for f in range(FFC):
                        ins = act.activation(hT[p][:, f, :], bank[4 + p][:, f * BLOCK:(f + 1) * BLOCK], ACT.Gelu,
                                             bias=b1_all[:, bass.ds(e * FFC + f, 1)])
                    ins.then_inc(hidden_done, 1)

            expert_steps(act, block_step)

        @block.vector
        def _(dve):
            dve.memset(pad[:], 0.0).then_inc(pad_done, 1)
            dve.memset(running[:], 0.0).then_inc(running_done, 1)
            dve.wait_ge(pad_done, 1)
            dve.memset(pad[:, D:D + 1].bitcast(U32), NO_ROW).then_inc(pad_done, 1)

            def split_lo(g, u):
                dve.tensor_tensor(x_lo[u][:, X_SPLIT:], x_raw[u][:, X_SPLIT:], x_hi[u][:, X_SPLIT:].bitcast(F32),
                                  ALU.subtract).then_inc(lo_v_done, 1)

            dve.wait_ge(tw_hi_done, 1)
            dve.tensor_tensor(tw_lo[:], tw_raw[:], tw_hi[:].bitcast(F32), ALU.subtract).then_inc(tw_done, 1)
            dve.wait_ge(hi_done, 1)
            split_lo(0, 0)
            dve.wait_ge(hi_done, 2)
            split_lo(1, 1)
            dve.wait_ge(pw_in, 16)
            dve.wait_ge(const_in, 48)
            dve.tensor_scalar(pw_raw[:], pw_raw[:], col_of("attn_gamma"), None, ALU.mult).then_inc(pw_scaled, 1)
            dve.tensor_scalar(neg_b_a[:], b_a, -1.0, None, ALU.mult).then_inc(neg_b_done, 1)
            dve.wait_ge(pw_hi_done, 1)
            dve.tensor_tensor(pw_lo[:], pw_raw[:], pw_hi[:].bitcast(F32), ALU.subtract).then_inc(pw_done, 1)

            def step(g, u, role):
                if has_group(role, 1):
                    dve.wait_ge(t1_done, g)
                    for b in range(GB):
                        ins = dve.bn_stats(stat1[:, b, :], bank[2][0:WIN, b * D:(b + 1) * D])
                    ins.then_inc(stat1_done, 1)
                    dve.wait_ge(const_in, 48)
                    dve.wait_ge(stat1_done, g)
                    for b in range(GB):
                        ins = dve.bn_aggr(mv1[:, b, :], stat1[:, b, :])
                    ins.then_inc(mv1_done, 1)
                    dve.wait_ge(mv1_done, g)
                    dve.tensor_scalar(neg_mean1[:], mv1[:, :, 0], -1.0, None, ALU.mult)
                    dve.tensor_scalar(var1[:], mv1[:, :, 1], EPS, None, ALU.add).then_inc(var1_done, 1)
                if has_group(role, 2):
                    dve.wait_ge(h_done, g - 1)
                    for b in range(GB):
                        ins = dve.bn_stats(stat2[:, b, :], h_all[:, at((g - 2) * (GB * D) + b * D, D)])
                    ins.then_inc(stat2_done, 1)
                    dve.wait_ge(const_in, 48)
                    dve.wait_ge(stat2_done, g - 1)
                    for b in range(GB):
                        ins = dve.bn_aggr(mv2[:, u, b, :], stat2[:, b, :])
                    ins.then_inc(mv2_done, 1)
                    dve.wait_ge(mv2_done, g - 1)
                    dve.tensor_scalar(base2[:, 0:GB], mv2[:, u, :, 1], EPS, None, ALU.add)
                    dve.tensor_scalar(base2[:, GB:2 * GB], mv2[:, u, :, 1], float(D), None, ALU.mult).then_inc(base2_done, 1)
                if has_group(role, 1) and has_group(role, -1):
                    dve.wait_ge(hi_done, g + 2)
                    split_lo(g + 1, 1 - u)
                if has_group(role, 3):
                    dve.wait_ge(xsT_hi_done, g - 2)
                    t = at((g - 3) * GT, GT)
                    dve.tensor_tensor(xsT_lo[:, t], bank[3][:, 0:GT], xsT_hi[:, t].bitcast(F32), ALU.subtract).then_inc(xsT_done, 1)
                if has_group(role, 2):
                    dve.wait_ge(root2_done, g - 1)
                    dve.tensor_tensor(norm2[:, 0, :], root2[:, 0:GB], root2[:, GB:2 * GB], ALU.mult).then_inc(length_done, 1)
                    dve.wait_ge(length_done, g - 1)
                    dve.tensor_scalar(norm2[:, 1, :], norm2[:, 0, :], 1e-12, None, ALU.max).then_inc(guarded_done, 1)
                    dve.wait_ge(guarded_done, g - 1)
                    dve.reciprocal(norm2[:, 2, :], norm2[:, 1, :]).then_inc(inverse_done, 1)
                    dve.wait_ge(inverse_done, g - 1)
                    dve.scalar_tensor_tensor(scale2[:], root2[:, 0:GB], float(D) ** 0.5, norm2[:, 2, :], ALU.mult,
                                             ALU.mult).then_inc(scale2_done, 1)
                    dve.wait_ge(scale2_done, g - 1)
                    for b in range(GB):
                        ins = dve.tensor_scalar(xs[u][:, b * D:(b + 1) * D], h_all[:, at((g - 2) * (GB * D) + b * D, D)],
                                                mv2[:, u, b, 0:1], scale2[:, b:b + 1], ALU.subtract, ALU.mult)
                    ins.then_inc(xs_done, 1)

            tokenizer_steps(dve, step)

            dve.wait_ge(main_done, GROUPS)
            dve.memset(decay[:, :, 0:1], 1.0).then_inc(setup_done, 1)
            dve.wait_ge(setup_done, 1)

            def scan(n_next, reused):
                dve.wait_ge(e_done, n_next)
                dve.tensor_scalar(decay[:, :, 1:WIN + 1], decay[:, :, 1:WIN + 1], 1.0, 1e10, ALU.add, ALU.min).then_inc(clip_done, 1)
                dve.wait_ge(clip_done, n_next)
                if reused:
                    dve.wait_ge(log_done, n_next - 1)
                    dve.wait_ge(inv_done, n_next - 1)
                dve.tensor_tensor_scan(grown[:].rearrange("p b i -> p (b i)"), decay[:].rearrange("p b i -> p (b i)"),
                                       const_of("scan_cap"), 1.0, ALU.mult, ALU.min).then_inc(scan_done, 1)

            def store_v(w, b, count):
                dve.wait_ge(v_done, count)
                dve.tensor_tensor(v[w][:, b, :], bank[5][0:WIN, :], row_of("b_v"), ALU.add).then_inc(vT_done, 1)

            scan(1, False)
            store_v(0, 0, 1)
            store_v(0, 1, 2)

            def body(g, u, role):
                for c in range(CHUNKS):
                    n = g * CHUNKS + c
                    if has_unit(role, c, -1):
                        scan(n + 2, True)
                    if has_unit(role, c, 0):
                        dve.wait_ge(q_done, n + 1)
                        dve.wait_ge(cum_done, n + 1)
                        dve.scalar_tensor_tensor(qT[c % 2][:], bank[1][:, 0:GT], col_of("b_q", c),
                                                 a_cum[c % 2][:].rearrange("p b i -> p (b i)"), ALU.add, ALU.mult).then_inc(qT_done, 1)
                        dve.wait_ge(k_done, n + 1)
                        dve.wait_ge(inv_done, n + 1)
                        dve.scalar_tensor_tensor(kT[c % 2][:], bank[4][:, 0:GT], col_of("b_k", c),
                                                 a_inv[c % 2][:].rearrange("p b i -> p (b i)"), ALU.add, ALU.mult).then_inc(kT_done, 1)
                    if has_unit(role, c, 1):
                        for hd in range(2):
                            dve.wait_ge(sim_done, n * 2 - 1 + hd)
                            if hd == 0 and has_unit(role, c, 3):
                                dve.wait_ge(av_done, n - 2)
                            dve.tensor_tensor(attnT[(c + 1) % 2][:, hd, :], bank[6 + hd][0:WIN, 0:GT], causal,
                                              ALU.mult).then_inc(attn_done, 1)
                    if c == 0 and has_group(role, 3):
                        sort_group(g, u)
                    if has_unit(role, c, -2) and (c + 2) // CHUNKS + role < GROUPS:
                        store_v(u if c < 2 else 1 - u, (c + 2) % CHUNKS, n + 3)
                    if c == 0 and has_group(role, 2):
                        norm_3(g, u, role)
                    if c == 2 and has_group(role, 2):
                        router_logits(g)
                    if c == 3 and has_group(role, 2):
                        choose(g, u)
                    if c == 3 and has_group(role, 1):
                        residual(g)

            def residual(g):
                dve.wait_ge(proj_done, g)
                dve.wait_ge(hb_done, g)
                h = at((g - 1) * (GB * D), GB * D)
                dve.tensor_tensor(h_all[:, h], bank[3][0:WIN, :], h_all[:, h], ALU.add).then_inc(h2_done, 1)
                dve.wait_ge(const_in, 48)
                dve.wait_ge(h2_done, g)
                for b in range(GB):
                    ins = dve.bn_stats(stat3[:, b, :], h_all[:, at((g - 1) * (GB * D) + b * D, D)])
                ins.then_inc(stat3_done, 1)
                dve.wait_ge(const_in, 48)
                dve.wait_ge(stat3_done, g)
                for b in range(GB):
                    ins = dve.bn_aggr(mv3[:, b, :], stat3[:, b, :])
                ins.then_inc(mv3_done, 1)
                dve.wait_ge(mv3_done, g)
                dve.tensor_scalar(var3[:], mv3[:, :, 1], EPS, None, ALU.add).then_inc(var3_done, 1)

            def norm_3(g, u, role):
                dve.wait_ge(rstd3_done, g - 1)
                if has_group(role, 3):
                    dve.wait_ge(scattered[u], (g - u - 2) * (GB * 16) + 16)
                for b in range(GB):
                    ins = dve.tensor_scalar(xm[u][:, 0, b, 0:D], h_all[:, at((g - 2) * (GB * D) + b * D, D)],
                                            mv3[:, b, 0:1], rstd3[:, b:b + 1], ALU.subtract, ALU.mult)
                ins.then_inc(xm_done, 1)
                dve.tensor_scalar(xm[u][:, :, :, D].bitcast(U32), result_row, 1.0, None, ALU.mult).then_inc(dest_done, 1)
                dve.wait_ge(dest_done, g * 2 - 3)
                dve.tensor_scalar(result_row, result_row, float(GT), None, ALU.add).then_inc(dest_done, 1)
                dve.wait_ge(dest_done, g * 2 - 2)

            def router_logits(g):
                dve.wait_ge(router_ps, g - 1)
                dve.tensor_tensor(logits[:].rearrange("p b e -> p (b e)"), bank[3][0:WIN, 0:GB * EXPERTS], row_of("router_b"),
                                  ALU.add).then_inc(logits_done, 1)
                dve.wait_ge(logits_done, g - 1)
                dve.tensor_reduce(top_logit[:], logits[:], AX_X, ALU.max).then_inc(top_logit_done, 1)
                dve.wait_ge(top_logit_done, g - 1)
                dve.tensor_tensor(shifted[:], logits[:], spread(top_logit[:]), ALU.subtract).then_inc(shifted_done, 1)

            def choose(g, u):
                dve.wait_ge(exp_done, g - 1)
                dve.tensor_reduce(exp_sum[:], expd[:], AX_X, ALU.add).then_inc(sum_done, 1)
                dve.wait_ge(sum_done, g - 1)
                dve.reciprocal(exp_rec[:], exp_sum[:]).then_inc(rec_done, 1)
                dve.wait_ge(rec_done, g - 1)
                dve.tensor_tensor(probs[:], expd[:], spread(exp_rec[:]), ALU.mult).then_inc(probs_done, 1)
                dve.wait_ge(const_in, 48)
                dve.wait_ge(probs_done, g - 1)
                for b in range(GB):
                    ins = dve.max(top8[:, b, :], probs[:, b, :])
                ins.then_inc(top8_done, 1)
                dve.wait_ge(const_in, 48)
                dve.wait_ge(top8_done, g - 1)
                for b in range(GB):
                    ins = dve.max_index(top8_at[:, b, :], top8[:, b, :], probs[:, b, :])
                ins.then_inc(top8_at_done, 1)
                dve.tensor_copy(xm[u][:, :, :, D + 1], top8[:, :, 0:2].rearrange("p b t -> p t b")).then_inc(gates_done, 1)
                dve.wait_ge(top8_at_done, g - 1)
                dve.tensor_copy(top8_atf[:], top8_at[:]).then_inc(top8_atf_done, 1)
                dve.wait_ge(top8_atf_done, g - 1)
                for t in range(2):
                    ins = dve.tensor_tensor(chosen[:, t], expert_no, spread(top8_atf[:, :, t]), ALU.is_equal)
                ins.then_inc(chosen_done, 1)
                dve.wait_ge(chosen_done, g - 1)
                dve.tensor_tensor(both[:], chosen[:, 0], chosen[:, 1], ALU.add).then_inc(both_done, 1)

            def sort_group(g, u):
                dve.wait_ge(prefix_ps, g - 2)
                dve.wait_ge(running_done, (g - 3) * (GB + 1) + 1)
                dve.tensor_copy(running[:, 0, :], running[:, GB, :]).then_inc(running_done, 1)
                for b in range(GB):
                    dve.wait_ge(running_done, (g - 3) * (GB + 1) + 2 + b)
                    dve.tensor_tensor(running[:, b + 1, :], bank[3][0:WIN, 256 + b * EXPERTS:256 + (b + 1) * EXPERTS],
                                      running[:, b, :], ALU.add).then_inc(running_done, 1)
                dve.tensor_tensor(rank[:], bank[3][0:WIN, 0:GB * EXPERTS].rearrange("p (b e) -> p b e", b=GB),
                                  running[:, 0:GB, :], ALU.add).then_inc(rank_done, 1)
                dve.wait_ge(rank_done, g - 2)
                dve.tensor_tensor(ranked[:], rank[:], first_row, ALU.add).then_inc(ranked_done, 1)
                dve.wait_ge(ranked_done, g - 2)
                for t in range(2):
                    ins = dve.tensor_tensor(place[:, t], chosen[:, t], ranked[:], ALU.mult)
                ins.then_inc(place_done, 1)
                dve.wait_ge(place_done, g - 2)
                dve.tensor_reduce(place_f[:], place[:].rearrange("p t b e -> p (t b) e"), AX_X, ALU.add).then_inc(place_f_done, 1)
                dve.wait_ge(place_f_done, g - 2)
                dve.tensor_copy(place_u[1 - u][:], place_f[:]).then_inc(placed_done, 1)

            attention_groups(dve, body)

            dve.wait_ge(running_done, GROUPS * (GB + 1) + 1)
            dve.wait_ge(placed_done, GROUPS)
            counts = running[0:1, GB, :]
            dve.tensor_tensor(tail_f[:], counts, first_row[0:1, 0, :], ALU.add).then_inc(tail_f_done, 1)
            dve.tensor_scalar(n_int[:], counts, float(BLOCK - 1), None, ALU.add).then_inc(n_int_done, 1)
            dve.memset(zero16[:], 0.0)
            dve.wait_ge(tail_f_done, 1)
            dve.tensor_copy(tail_at[:], tail_f[:]).then_inc(tail_done, 1)
            dve.wait_ge(n_int_done, 1)
            dve.tensor_scalar(nb_int[:], n_int[:], BLOCK.bit_length() - 1, None, ALU.arith_shift_right).then_inc(nb_int_done, 1)
            dve.wait_ge(nb_int_done, 1)
            dve.tensor_copy(nb_f[:], nb_int[:]).then_inc(nb_f_done, 1)
            dve.wait_ge(nb_f_done, 1)
            dve.tensor_tensor_scan(nb_end[:], nb_f[:], zero16[:], 0.0, ALU.add, ALU.add).then_inc(nb_end_done, 1)
            dve.wait_ge(nb_end_done, 1)
            dve.wait_ge(block_no_in, 16)
            dve.tensor_tensor(past[:], nb_end[:].unsqueeze(1).to_broadcast([1, BLOCKS, EXPERTS]), block_no[:],
                              ALU.is_le).then_inc(past_done, 1)
            dve.wait_ge(past_done, 1)
            dve.tensor_tensor(past_nb[:], past[:], nb_f[:].unsqueeze(1).to_broadcast([1, BLOCKS, EXPERTS]),
                              ALU.mult).then_inc(past_nb_done, 1)
            dve.tensor_reduce(blk_e[:], past[:], AX_X, ALU.add).then_inc(blk_e_done, 1)
            dve.wait_ge(past_nb_done, 1)
            dve.tensor_reduce(blk_s[:], past_nb[:], AX_X, ALU.add).then_inc(blk_s_done, 1)
            dve.wait_ge(blk_e_done, 1)
            dve.tensor_scalar(blk_expert[:], blk_e[:], float(EXPERTS - 1), None, ALU.min).then_inc(blk_expert_done, 1)
            dve.wait_ge(blk_s_done, 1)
            dve.tensor_tensor(blk_r[:], block_no[:, :, 0], blk_s[:], ALU.subtract).then_inc(blk_r_done, 1)
            dve.tensor_scalar(blk_q[:], blk_e[:], float(CAP), None, ALU.mult).then_inc(blk_q_done, 1)
            dve.wait_ge(blk_q_done, 1)
            dve.scalar_tensor_tensor(blk_t[:], blk_r[:], float(BLOCK), blk_q[:], ALU.mult, ALU.add).then_inc(blk_t_done, 1)
            dve.wait_ge(blk_t_done, 1)
            dve.tensor_scalar(blk_row[:], blk_t[:], float(DUMMY), None, ALU.min).then_inc(table_done, 1)
            dve.wait_ge(table_done, 1)
            dve.wait_ge(experts_in, 48)

            def prepare(j, p):
                e = dve.value_load(blk_expert[0:1, at(j)], min_val=0, max_val=EXPERTS - 1)
                dve.tensor_copy(w1_blk[p][:], w1_all[:, bass.ds(e * FF, FF)]).then_inc(w1_done, 1)
                dve.wait_ge(xT_ps, j + 1)
                dve.tensor_copy(xbT[p][:], bank[p][:, 0:BLOCK]).then_inc(xT_done, 1)

            prepare(0, 0)

            def block_step(j, slot, role):
                if has_block(role, -1):
                    if has_block(role, 1):
                        dve.wait_ge(hidden_ps, j)
                    prepare(j + 1, (slot + 1) % 2)
                if has_block(role, 1):
                    p, last = (slot + 1) % 2, (slot - 1) % SLOTS
                    e = dve.value_load(blk_expert[0:1, at(j - 1)], min_val=0, max_val=EXPERTS - 1)
                    dve.wait_ge(y_ps, j)
                    dve.tensor_tensor(yb[p][:], bank[6 + p][:, 0:D], b2_all[:, bass.ds(e * D, D)], ALU.add).then_inc(yb_done, 1)
                    dve.wait_ge(yb_done, j)
                    dve.tensor_scalar(yg[last][:], yb[p][:], xb[last][:, D + 1:D + 2], None, ALU.mult).then_inc(yg_done, 1)

            expert_steps(dve, block_step)

            for k in range(OUT_STEPS):
                dve.wait_ge(y_in[k], 32)
                h = h_all[:, k * OB * D:(k + 1) * OB * D]
                f1, f2 = (y[k][:].rearrange("p b d -> p (b d)") for y in (y1, y2))
                dve.tensor_tensor(f1, f1, f2, ALU.add).then_inc(sum_done2, 1)
                dve.wait_ge(sum_done2, k + 1)
                dve.tensor_tensor(f1, f1, h, ALU.add).then_inc(out_ready, 1)

        @block.gpsimd
        def _(pool):
            def split_lo(g, u):
                pool.tensor_tensor(x_lo[u][:, 0:X_SPLIT], x_raw[u][:, 0:X_SPLIT], x_hi[u][:, 0:X_SPLIT].bitcast(F32),
                                   ALU.subtract).then_inc(lo_p_done, 1)

            pool.wait_ge(hi_done, 1)
            split_lo(0, 0)
            pool.wait_ge(hi_done, 2)
            split_lo(1, 1)
            pool.wait_ge(const_in, 48)
            pool.wait_ge(pad_done, 2)
            half = BLOCK // 2
            for u in range(2):
                pool.dma_start(sorted_rows[DUMMY + u * half:DUMMY + (u + 1) * half, :], pad[u * half:(u + 1) * half, :]).then_inc(scattered[u], 16)

            def step(g, u, role):
                if has_group(role, 1):
                    pool.wait_ge(var1_done, g)
                    if has_group(role, 2):
                        pool.wait_ge(normed_done, g - 1)
                    pool.tensor_tensor(rstd1[:], var1[:], power[:, 0:GB], ALU.pow).then_inc(rstd1_done, 1)
                    pool.wait_ge(rstd1_done, g)
                    pool.tensor_tensor(shift1[:], neg_mean1[:], rstd1[:], ALU.mult).then_inc(shift1_done, 1)
                if has_group(role, 2):
                    pool.wait_ge(base2_done, g - 1)
                    pool.tensor_tensor(root2[:], base2[:], power, ALU.pow).then_inc(root2_done, 1)
                if has_group(role, 1) and has_group(role, -1):
                    pool.wait_ge(hi_done, g + 2)
                    split_lo(g + 1, 1 - u)
                if has_group(role, 1):
                    pool.wait_ge(normed_done, g)
                    pool.tensor_tensor(by_row(scaled[:]), by_row(normed[1 - u][:]), each_row("gamma"), ALU.mult).then_inc(scaled_done, 1)
                    pool.wait_ge(scaled_done, g)
                    pool.tensor_tensor(by_row(h_all[:, at((g - 1) * (GB * D), GB * D)]), by_row(scaled[:]), each_row("beta"), ALU.add).then_inc(h_done, 1)

            tokenizer_steps(pool, step)

            def inverse(c, n_next, reused):
                pool.wait_ge(scan_done, n_next)
                if reused:
                    pool.wait_ge(kT_done, n_next - 2)
                pool.sem_inc(pool_go, 1)
                pool.tensor_scalar(a_inv[c % 2][:], grown[:, :, 1:WIN + 1], 1e8, SHIFT, ALU.min, ALU.mult).then_inc(inv_done, 1)

            def stage_v(g):
                t = at(g * GT, GT)
                pool.tensor_copy(xv_hi[:], xsT_hi[:, t].bitcast(F32))
                pool.tensor_copy(xv_lo[:], xsT_lo[:, t].bitcast(F32)).then_inc(xv_done, 1)

            pool.wait_ge(xsT_done, GROUPS)
            stage_v(0)
            inverse(0, 1, False)

            def scatter(g, u, batches):
                for b in batches:
                    for t in range(2):
                        pool.indirect_dma_start(sorted_rows, bass.IndirectOffsetOnAxis(ap=place_u[1 - u][:, t * GB + b:t * GB + b + 1], axis=0),
                                                xm[1 - u][:, t, b, :], None).then_inc(scattered[1 - u], 16)

            def body(g, u, role):
                for c in range(CHUNKS):
                    n = g * CHUNKS + c
                    if has_unit(role, c, -1):
                        inverse((c + 1) % CHUNKS, n + 2, has_unit(role, c, 1))
                    if c == 2 and role + 1 < GROUPS:
                        pool.wait_ge(v_done, (g + 1) * GB)
                        pool.sem_inc(pool_go, 1)
                        stage_v(g + 1)
                    if c == 0 and has_group(role, 0):
                        h = by_row(h_all[:, at(g * (GB * D), GB * D)])
                        pool.tensor_tensor(h, h, each_row("b_out"), ALU.add).then_inc(hb_done, 1)
                    if c == 3 and has_group(role, 1):
                        pool.wait_ge(var3_done, g)
                        pool.tensor_tensor(rstd3[:], var3[:], power[:, 0:GB], ALU.pow).then_inc(rstd3_done, 1)
                    if c == 1 and has_group(role, 2):
                        pool.wait_ge(xm_done, g - 1)
                        pool.sem_inc(pool_go, 1)
                        pool.tensor_copy(xm[u][:, 1, :, 0:D], xm[u][:, 0, :, 0:D]).then_inc(xm_twice, 1)
                    if c in (1, 2) and has_group(role, 3):
                        if c == 1:
                            pool.wait_ge(placed_done, g - 2)
                            pool.wait_ge(gates_done, g - 2)
                            pool.wait_ge(dest_done, g * 2 - 4)
                            pool.wait_ge(xm_twice, g - 2)
                            pool.sem_inc(pool_go, 1)
                        scatter(g, u, range(2 * c - 2, 2 * c))

            attention_groups(pool, body)

            def block_step(j, slot, role):
                if has_block(role, 1):
                    last = (slot - 1) % SLOTS
                    pool.wait_ge(yg_done, j)
                    pool.sem_inc(pool_go, 1)
                    pool.indirect_dma_start(results, bass.IndirectOffsetOnAxis(ap=xb[last][:, D:D + 1].bitcast(U32), axis=0),
                                            yg[last][:], None, bounds_check=NO_ROW - 1, oob_is_err=False).then_inc(y_out[last], 16)

            expert_steps(pool, block_step)


def shape_constants(np):
    f = np.float32
    i = np.arange(WIN)
    parts = {
        "ident": np.eye(128),
        "causal": np.tile(np.where(i[None, :] >= i[:, None], SCALE, 0.0), (1, GB)),
        "before": (i[:, None] < i[None, :]).astype(f),
        "ones": np.ones((WIN, WIN)),
        "scan_cap": np.tile(np.where(np.arange(WIN + 1) == 0, 1.0, SCAN_CAP), (128, GB)),
        "first_row": np.tile(np.arange(EXPERTS) * CAP, (128, GB)),
        "expert": np.tile(np.arange(EXPERTS), (128, GB)),
        "result_row": (np.arange(2)[None, :, None] * TOKENS + np.arange(GB)[None, None, :] * WIN
                       + np.arange(128)[:, None, None]).reshape(128, 2 * GB),
        "power": np.tile(np.repeat([-0.5, 0.5], GB), (128, 1)),
    }
    out = np.zeros((128, CONST_COLS), f)
    for name, a in parts.items():
        out[:a.shape[0], CONST[name][0]:CONST[name][0] + a.shape[1]] = a
    return out


def kernel(x, L0_tok_W, L0_tok_b, L0_tok_gamma, L0_tok_beta, L0_attn_gamma, L0_attn_w_qkv, L0_attn_b_qkv, L0_attn_w_a,
           L0_attn_b_a, L0_attn_w_out, L0_attn_b_out, L0_ffn_router_w, L0_ffn_router_b, L0_ffn_w1, L0_ffn_b1, L0_ffn_w2, L0_ffn_b2):
    import numpy as np
    import concourse.bacc as bacc
    from concourse.bass_utils import run_bass_kernel_spmd

    def repeated(a, n):
        return np.broadcast_to(np.asarray(a).reshape(1, -1), (n, np.asarray(a).size))

    def columns(a):
        return np.asarray(a).reshape(-1, 128).T

    used = np.asarray(x)[:, :CELLS * STRIDE].reshape(GROUPS, GB, CELLS, STRIDE, D)
    rows = np.zeros((WIN, ROWS_COLS), np.float32)
    for name, a in (("gamma", L0_tok_gamma), ("beta", L0_tok_beta), ("b_out", L0_attn_b_out),
                    ("b_v", np.asarray(L0_attn_b_qkv)[2 * INNER:]), ("router_b", np.tile(L0_ffn_router_b, GB))):
        rows[:, ROWS[name][0]:ROWS[name][0] + ROWS[name][1]] = repeated(a, WIN)
    cols = np.zeros((128, COLS_COLS), np.float32)
    for name, a in (("tok_b", columns(L0_tok_b)), ("attn_gamma", columns(L0_attn_gamma)),
                    ("b_q", columns(np.asarray(L0_attn_b_qkv)[:INNER])), ("b_k", columns(np.asarray(L0_attn_b_qkv)[INNER:2 * INNER])),
                    ("b_a", columns(L0_attn_b_a)), ("b1", columns(L0_ffn_b1)), ("router_w", np.asarray(L0_ffn_router_w).T)):
        cols[:, COLS[name][0]:COLS[name][0] + COLS[name][1]] = a
    arrays = {
        "x_dram": used.transpose(0, 4, 3, 1, 2).reshape(GROUPS, D, STRIDE * GB * CELLS),
        "tok_w_dram": np.asarray(L0_tok_W).reshape(TOKEN_SIZE, D, D).transpose(1, 0, 2).reshape(D, TOKEN_SIZE * D),
        "proj_w_dram": np.concatenate([np.asarray(L0_attn_w_qkv), np.asarray(L0_attn_w_a)], axis=1),
        "out_w_dram": np.asarray(L0_attn_w_out).reshape(CHUNKS, 128, D).transpose(1, 0, 2).reshape(128, CHUNKS * D),
        "w1_dram": np.asarray(L0_ffn_w1).transpose(2, 0, 1).reshape(D, EXPERTS * FF),
        "w2_dram": np.asarray(L0_ffn_w2).reshape(EXPERTS, D, FFC, 128).transpose(3, 0, 2, 1).reshape(128, EXPERTS * FF),
        "b2_dram": repeated(L0_ffn_b2, 128),
        "consts_dram": shape_constants(np),
        "rows_dram": rows,
        "cols_dram": cols,
        "block_nos_dram": np.repeat(np.arange(BLOCKS), EXPERTS).reshape(1, BLOCKS, EXPERTS).astype(np.float32),
    }
    arrays = {name: np.ascontiguousarray(a) for name, a in arrays.items()}
    nc = bacc.Bacc("TRN2", target_bir_lowering=False, num_devices=1)
    args = [nc.dram_tensor(name, a.shape, mybir.dt.from_np(a.dtype), kind="ExternalInput").ap() for name, a in arrays.items()]
    out = nc.dram_tensor("out_dram", (BATCH, WIN, D), F32, kind="ExternalOutput").ap()
    build(nc, *args, out)
    got = run_bass_kernel_spmd(nc, [arrays], core_ids=[0])
    return got.results[0]["out_dram"]
```

```python
from contextlib import ExitStack

import concourse.bass as bass
from concourse import mybir

F32 = mybir.dt.float32
F32R = mybir.dt.float32r
U32 = mybir.dt.uint32
I32 = mybir.dt.int32
ALU = mybir.AluOpType
ACT = mybir.ActivationFunctionType
AX_X = mybir.AxisListType.X

BATCH, SEQ, D = 32, 750, 128
TOKEN_SIZE, STRIDE = 16, 8
WIN = (SEQ - TOKEN_SIZE) // STRIDE + 1
CELLS = WIN + TOKEN_SIZE // STRIDE - 1
HALVES = TOKEN_SIZE // STRIDE
HEADS, DH = 8, 64
INNER = HEADS * DH
CHUNKS = INNER // 128
EXPERTS, FF = 16, 512
FFC = FF // 128
TOKENS = BATCH * WIN

GB = 4
GROUPS = BATCH // GB
GT = GB * WIN

BLOCK = 128
CAP = TOKENS + BLOCK
CAP += -CAP % BLOCK
BLOCKS = (2 * TOKENS + EXPERTS * (BLOCK - 1)) // BLOCK
DUMMY = EXPERTS * CAP
ROW = D + 2
NO_ROW = 2 * TOKENS

EPS = 1e-5
LOG_CAP = 87.3
SCALE = DH ** -0.5

CONST = {}
CONST_COLS = 0
for _name, _n in (("ident", 128), ("causal", GT), ("before", WIN), ("ones", WIN), ("log_cap", GB * (WIN + 1)),
                  ("first_row", GB * EXPERTS), ("expert", GB * EXPERTS), ("result_row", 2 * GB),
                  ("group_tokens", 2 * GB), ("power", 8)):
    CONST[_name] = (CONST_COLS, _n)
    CONST_COLS += _n

ROWS = {}
ROWS_COLS = 0
for _name, _n in (("gamma", D), ("beta", D), ("b_out", D), ("b_v", INNER), ("router_b", GB * EXPERTS)):
    ROWS[_name] = (ROWS_COLS, _n)
    ROWS_COLS += _n

COLS = {}
COLS_COLS = 0
for _name, _n in (("tok_b", 1), ("attn_gamma", 1), ("b_q", CHUNKS), ("b_k", CHUNKS), ("b_a", CHUNKS),
                  ("b1", EXPERTS * FFC), ("router_w", EXPERTS)):
    COLS[_name] = (COLS_COLS, _n)
    COLS_COLS += _n


SLOTS = 8
OUT_STEPS = 4
OB = BATCH // OUT_STEPS
X_SPLIT = 2 * GB * CELLS


def at(n, size=1):
    return bass.ds(n, size) if not isinstance(n, int) else slice(n, n + size)


def build(nc, x, tok_w, proj_w, out_w, w1, w2, b2, consts, rows, cols, block_nos, out):
    ctx = ExitStack()
    phase_1 = ExitStack()
    phase_2 = ExitStack()
    phase_3 = ExitStack()

    def sb(name, shape, dt=F32, stack=ctx):
        return stack.enter_context(nc.sbuf_tensor(name, shape, dt))

    def sem(name):
        return ctx.enter_context(nc.semaphore(name))

    with ctx:
        const = sb("const", [128, CONST_COLS])
        row = sb("row", [WIN, ROWS_COLS])
        col = sb("col", [128, COLS_COLS])

        def const_of(name, p=128):
            a, n = CONST[name]
            return const[0:p, a:a + n]

        def row_of(name):
            a, n = ROWS[name]
            return row[:, a:a + n]

        def col_of(name, i=0):
            return col[:, COLS[name][0] + i:COLS[name][0] + i + 1]

        ident = const_of("ident")
        neg_b_a = sb("neg_b_a", [128, CHUNKS])
        pw_hi = sb("pw_hi", [128, 4 * INNER], F32R)
        pw_lo = sb("pw_lo", [128, 4 * INNER], F32R)
        xsT_hi = sb("xsT_hi", [128, TOKENS], F32R)
        xsT_lo = sb("xsT_lo", [128, TOKENS], F32R)
        h_all = sb("h_all", [WIN, BATCH * D])
        pad = sb("pad", [128, ROW])
        running = sb("running", [WIN, GB + 1, EXPERTS])

        XG = STRIDE * GB * CELLS
        geluT = [sb(f"geluT{u}", [128, GT], stack=phase_1) for u in range(2)]
        normed = [sb(f"normed{u}", [WIN, GB * D], stack=phase_1) for u in range(2)]
        scaled = sb("scaled", [WIN, GB * D], stack=phase_1)
        xs = [sb(f"xs{u}", [WIN, GB * D], stack=phase_1) for u in range(2)]
        stat1 = sb("stat1", [WIN, GB, 6], stack=phase_1)
        mv1 = sb("mv1", [WIN, GB, 2], stack=phase_1)
        var1 = sb("var1", [WIN, GB], stack=phase_1)
        neg_mean1 = sb("neg_mean1", [WIN, GB], stack=phase_1)
        rstd1 = sb("rstd1", [WIN, GB], stack=phase_1)
        shift1 = sb("shift1", [WIN, GB], stack=phase_1)
        stat2 = sb("stat2", [WIN, GB, 6], stack=phase_1)
        mv2 = sb("mv2", [WIN, 2, GB, 2], stack=phase_1)
        base2 = sb("base2", [WIN, 2 * GB], stack=phase_1)
        root2 = sb("root2", [WIN, 2 * GB], stack=phase_1)
        norm2 = sb("norm2", [WIN, 3, GB], stack=phase_1)
        scale2 = sb("scale2", [WIN, GB], stack=phase_1)
        x_raw = [sb(f"x_raw{u}", [128, XG], stack=phase_1) for u in range(2)]
        x_hi = [sb(f"x_hi{u}", [128, XG], F32R, phase_1) for u in range(2)]
        x_lo = [sb(f"x_lo{u}", [128, XG], F32R, phase_1) for u in range(2)]
        tw_raw = sb("tw_raw", [128, TOKEN_SIZE * D], stack=phase_1)
        tw_hi = sb("tw_hi", [128, TOKEN_SIZE * D], F32R, phase_1)
        tw_lo = sb("tw_lo", [128, TOKEN_SIZE * D], F32R, phase_1)
        pw_raw = sb("pw_raw", [128, 4 * INNER], stack=phase_1)
        phase_1.close()

        w1_all = sb("w1_all", [128, EXPERTS * FF])
        w2_all = sb("w2_all", [128, EXPERTS * FF])
        b2_all = sb("b2_all", [128, EXPERTS * D])

        ow = sb("ow", [128, CHUNKS * D], stack=phase_2)
        growth = [sb(f"growth{u}", [128, GT], stack=phase_2) for u in range(2)]
        log_growth = sb("log_growth", [128, GB, WIN + 1], stack=phase_2)
        log_sum = sb("log_sum", [128, GB, WIN + 1], stack=phase_2)
        a_cum = [sb(f"a_cum{u}", [128, GB, WIN], stack=phase_2) for u in range(2)]
        a_inv = [sb(f"a_inv{u}", [128, GB, WIN], stack=phase_2) for u in range(2)]
        kb = [sb(f"kb{u}", [128, GT], stack=phase_2) for u in range(2)]
        qT = [sb(f"qT{u}", [128, GT], stack=phase_2) for u in range(2)]
        kT = [sb(f"kT{u}", [128, GT], stack=phase_2) for u in range(2)]
        attnT = [sb(f"attnT{u}", [WIN, 2, GT], stack=phase_2) for u in range(2)]
        xv_hi = [sb(f"xv_hi{u}", [128, GT], F32R, phase_2) for u in range(2)]
        xv_lo = [sb(f"xv_lo{u}", [128, GT], F32R, phase_2) for u in range(2)]
        v = [sb(f"v{u}", [WIN, GB, INNER], stack=phase_2) for u in range(2)]
        oT = [sb(f"oT{c}", [128, GT], stack=phase_2) for c in range(CHUNKS)]
        stat3 = sb("stat3", [WIN, GB, 6], stack=phase_2)
        mv3 = sb("mv3", [WIN, GB, 2], stack=phase_2)
        var3 = sb("var3", [WIN, GB], stack=phase_2)
        rstd3 = sb("rstd3", [WIN, GB], stack=phase_2)
        neg_mean3 = sb("neg_mean3", [WIN, GB], stack=phase_2)
        shift3 = sb("shift3", [WIN, GB], stack=phase_2)
        counts = sb("counts", [WIN, 2, GB, EXPERTS], stack=phase_2)
        xm = [sb(f"xm{u}", [WIN, 2, GB, ROW], stack=phase_2) for u in range(2)]
        xmT = sb("xmT", [128, GT], stack=phase_2)
        logits = sb("logits", [WIN, GB, EXPERTS], stack=phase_2)
        top_logit = sb("top_logit", [WIN, GB], stack=phase_2)
        shifted = sb("shifted", [WIN, GB, EXPERTS], stack=phase_2)
        expd = sb("expd", [WIN, GB, EXPERTS], stack=phase_2)
        exp_sum = sb("exp_sum", [WIN, GB], stack=phase_2)
        exp_rec = sb("exp_rec", [WIN, GB], stack=phase_2)
        probs = sb("probs", [WIN, GB, EXPERTS], stack=phase_2)
        top8 = sb("top8", [WIN, GB, 8], stack=phase_2)
        top8_at = sb("top8_at", [WIN, GB, 8], U32, phase_2)
        top8_atf = sb("top8_atf", [WIN, GB, 8], stack=phase_2)
        chosen = sb("chosen", [WIN, 2, GB, EXPERTS], stack=phase_2)
        both = sb("both", [WIN, GB, EXPERTS], stack=phase_2)
        rank = sb("rank", [WIN, GB, EXPERTS], stack=phase_2)
        ranked = sb("ranked", [WIN, GB, EXPERTS], stack=phase_2)
        place = sb("place", [WIN, 2, GB, EXPERTS], stack=phase_2)
        place_8 = sb("place_8", [WIN, 2 * GB, 8], stack=phase_2)
        place_4 = sb("place_4", [WIN, 2 * GB, 4], stack=phase_2)
        place_2 = sb("place_2", [WIN, 2 * GB, 2], stack=phase_2)
        place_f = sb("place_f", [WIN, 2 * GB], stack=phase_2)
        place_u = [sb(f"place_u{u}", [WIN, 2 * GB], U32, phase_2) for u in range(2)]
        phase_2.close()

        n_int = sb("n_int", [1, EXPERTS], I32, phase_3)
        tail_at = sb("tail_at", [1, EXPERTS], I32, phase_3)
        tail_f = sb("tail_f", [1, EXPERTS], stack=phase_3)
        nb_int = sb("nb_int", [1, EXPERTS], I32, phase_3)
        nb_f = sb("nb_f", [1, EXPERTS], stack=phase_3)
        zero16 = sb("zero16", [1, EXPERTS], stack=phase_3)
        nb_end = sb("nb_end", [1, EXPERTS], stack=phase_3)
        block_no = sb("block_no", [1, BLOCKS, EXPERTS], stack=phase_3)
        past = sb("past", [1, BLOCKS, EXPERTS], stack=phase_3)
        past_nb = sb("past_nb", [1, BLOCKS, EXPERTS], stack=phase_3)
        blk_e = sb("blk_e", [1, BLOCKS], stack=phase_3)
        blk_s = sb("blk_s", [1, BLOCKS], stack=phase_3)
        blk_r = sb("blk_r", [1, BLOCKS], stack=phase_3)
        blk_q = sb("blk_q", [1, BLOCKS], stack=phase_3)
        blk_t = sb("blk_t", [1, BLOCKS], stack=phase_3)
        blk_expert = sb("blk_expert", [1, BLOCKS], I32, phase_3)
        blk_row = sb("blk_row", [1, BLOCKS], I32, phase_3)
        xb = [sb(f"xb{u}", [128, ROW], stack=phase_3) for u in range(SLOTS)]
        xbT = [sb(f"xbT{u}", [128, BLOCK], stack=phase_3) for u in range(2)]
        w1_blk = [sb(f"w1_blk{u}", [128, FF], stack=phase_3) for u in range(2)]
        hT = [sb(f"hT{u}", [128, FFC, BLOCK], stack=phase_3) for u in range(2)]
        yb = [sb(f"yb{u}", [128, D], stack=phase_3) for u in range(2)]
        yg = [sb(f"yg{u}", [128, D], stack=phase_3) for u in range(SLOTS)]
        y1 = [sb(f"y1_{k}", [WIN, OB, D], stack=phase_3) for k in range(OUT_STEPS)]
        y2 = [sb(f"y2_{k}", [WIN, OB, D], stack=phase_3) for k in range(OUT_STEPS)]
        phase_3.close()

        bank = [ctx.enter_context(nc.psum_tensor(f"bank{i}", [128, 512], F32)) for i in range(8)]

        sorted_rows = nc.dram_tensor("sorted_rows", (DUMMY + BLOCK, ROW), F32).ap()
        results = nc.dram_tensor("results", (2 * TOKENS, D), F32).ap()

        x_in0 = sem("x_in0")
        tw_in = sem("tw_in")
        const_in = sem("const_in")
        x_in1 = sem("x_in1")
        pw_in = sem("pw_in")
        lo_v_done = sem("lo_v_done")
        lo_p_done = sem("lo_p_done")
        main_done = sem("main_done")
        pw_done = sem("pw_done")
        xsT_done = sem("xsT_done")
        ow_in = sem("ow_in")
        experts_in = sem("experts_in")
        v_done = sem("v_done")
        placed_done = sem("placed_done")
        scattered0 = sem("scattered0")
        scattered1 = sem("scattered1")
        block_no_in = sem("block_no_in")
        tail_done = sem("tail_done")
        tails_out = sem("tails_out")
        table_done = sem("table_done")
        out_ready = sem("out_ready")
        out_done = sem("out_done")
        tw_done = sem("tw_done")
        gelu_done = sem("gelu_done")
        normed_done = sem("normed_done")
        t1_done = sem("t1_done")
        xs_done = sem("xs_done")
        t2_done = sem("t2_done")
        a_done = sem("a_done")
        e_done = sem("e_done")
        xv_in0 = sem("xv_in0")
        vT_done = sem("vT_done")
        qT_done = sem("qT_done")
        xmT_done = sem("xmT_done")
        router_ps = sem("router_ps")
        logits_done = sem("logits_done")
        q_done = sem("q_done")
        kb_done = sem("kb_done")
        k_done = sem("k_done")
        kT_done = sem("kT_done")
        attn_done = sem("attn_done")
        sim_done = sem("sim_done")
        xm_done = sem("xm_done")
        h2_done = sem("h2_done")
        xmT_ps = sem("xmT_ps")
        both_done = sem("both_done")
        oT_done = sem("oT_done")
        prefix_ps = sem("prefix_ps")
        av_done = sem("av_done")
        proj_done = sem("proj_done")
        xT_ps = sem("xT_ps")
        xT_done = sem("xT_done")
        w1_done = sem("w1_done")
        hidden_ps = sem("hidden_ps")
        hidden_done = sem("hidden_done")
        yb_done = sem("yb_done")
        y_ps = sem("y_ps")
        hi_done = sem("hi_done")
        tw_hi_done = sem("tw_hi_done")
        pw_scaled = sem("pw_scaled")
        pw_hi_done = sem("pw_hi_done")
        shift1_done = sem("shift1_done")
        h_done = sem("h_done")
        xsT_hi_done = sem("xsT_hi_done")
        log_done = sem("log_done")
        clip_done = sem("clip_done")
        scan_done = sem("scan_done")
        cum_done = sem("cum_done")
        inv_done = sem("inv_done")
        neg_b_done = sem("neg_b_done")
        log_start_done = sem("log_start_done")
        counts_done = sem("counts_done")
        shift3_done = sem("shift3_done")
        xm_twice = sem("xm_twice")
        shifted_done = sem("shifted_done")
        exp_done = sem("exp_done")
        pad_done = sem("pad_done")
        running_done = sem("running_done")
        stat1_done = sem("stat1_done")
        mv1_done = sem("mv1_done")
        var1_done = sem("var1_done")
        stat2_done = sem("stat2_done")
        mv2_done = sem("mv2_done")
        base2_done = sem("base2_done")
        root2_done = sem("root2_done")
        length_done = sem("length_done")
        guarded_done = sem("guarded_done")
        inverse_done = sem("inverse_done")
        scale2_done = sem("scale2_done")
        hb_done = sem("hb_done")
        stat3_done = sem("stat3_done")
        dve_go = sem("dve_go")
        mv3_done = sem("mv3_done")
        var3_done = sem("var3_done")
        top_logit_done = sem("top_logit_done")
        sum_done = sem("sum_done")
        rec_done = sem("rec_done")
        probs_done = sem("probs_done")
        top8_done = sem("top8_done")
        top8_at_done = sem("top8_at_done")
        gates_done = sem("gates_done")
        top8_atf_done = sem("top8_atf_done")
        place_done = sem("place_done")
        chosen_done = sem("chosen_done")
        tail_f_done = sem("tail_f_done")
        n_int_done = sem("n_int_done")
        nb_int_done = sem("nb_int_done")
        nb_f_done = sem("nb_f_done")
        nb_end_done = sem("nb_end_done")
        past_done = sem("past_done")
        past_nb_done = sem("past_nb_done")
        blk_e_done = sem("blk_e_done")
        blk_s_done = sem("blk_s_done")
        blk_expert_done = sem("blk_expert_done")
        blk_r_done = sem("blk_r_done")
        blk_q_done = sem("blk_q_done")
        blk_t_done = sem("blk_t_done")
        yg_done = sem("yg_done")
        sum_done2 = sem("sum_done2")
        rstd1_done = sem("rstd1_done")
        scaled_done = sem("scaled_done")
        pool_go = sem("pool_go")
        rank_done = sem("rank_done")
        ranked_done = sem("ranked_done")
        place_8_done = sem("place_8_done")
        place_4_done = sem("place_4_done")
        place_2_done = sem("place_2_done")
        place_f_done = sem("place_f_done")
        rstd3_done = sem("rstd3_done")
        dest_done = sem("dest_done")
        xv_in1 = sem("xv_in1")
        x_in = (x_in0, x_in1)
        scattered = (scattered0, scattered1)
        xv_in = (xv_in0, xv_in1)
        xb_in = [sem(f"xb_in{u}") for u in range(SLOTS)]
        y_out = [sem(f"y_out{u}") for u in range(SLOTS)]
        y_in = [sem(f"y_in{k}") for k in range(OUT_STEPS)]

        ident_w = const[0:WIN, CONST["ident"][0]:CONST["ident"][0] + WIN]
        causal = const_of("causal", WIN)
        power = const_of("power", WIN)
        result_row = const_of("result_row", WIN).rearrange("p (t b) -> p t b", t=2)
        group_tokens = const_of("group_tokens", WIN).rearrange("p (t b) -> p t b", t=2)
        expert_no = const_of("expert", WIN).rearrange("p (b e) -> p b e", b=GB)
        first_row = const_of("first_row", WIN).rearrange("p (b e) -> p b e", b=GB)
        b_a = col[:, COLS["b_a"][0]:COLS["b_a"][0] + CHUNKS]
        b1_all = col[:, COLS["b1"][0]:COLS["b1"][0] + EXPERTS * FFC]
        router_w = col[:, COLS["router_w"][0]:COLS["router_w"][0] + EXPERTS]

        def by_row(a):
            return a.rearrange("p (b d) -> p b d", b=GB)

        def each_row(name):
            return row_of(name).unsqueeze(1).to_broadcast([WIN, GB, D])

        def spread(a):
            return a.unsqueeze(2).to_broadcast([WIN, GB, EXPERTS])

        block = ctx.enter_context(nc.Block())

        def tokenizer_and_attention(eng, step, start, unit):
            for g in range(3):
                step(g, g % 2, g)
            with eng.Fori(0, 2) as i:
                for k in range(2):
                    step(i * 2 + 3 + k, (3 + k) % 2, 3)
            for g in range(7, GROUPS + 1):
                step(g, g % 2, g)
            start()
            step(GROUPS + 1, (GROUPS + 1) % 2, GROUPS + 1)
            for c in range(2):
                unit(0, 0, 0, c)
            step(GROUPS + 2, (GROUPS + 2) % 2, GROUPS + 2)
            for c in range(2, CHUNKS):
                unit(0, 0, 0, c)
            for g in range(1, 3):
                for c in range(CHUNKS):
                    unit(g, g % 2, g, c)
            with eng.Fori(0, 2) as i:
                for k in range(2):
                    for c in range(CHUNKS):
                        unit(i * 2 + 3 + k, (3 + k) % 2, 3, c)
            for g in range(7, GROUPS + 3):
                for c in range(CHUNKS):
                    unit(g, g % 2, g, c)

        def expert_steps(eng, step):
            step(0, 0, 0)
            step(1, 1, 1)
            loops = (BLOCKS - 3) // SLOTS
            with eng.Fori(0, loops) as i:
                for k in range(SLOTS):
                    step(i * SLOTS + 2 + k, (2 + k) % SLOTS, 2)
            for j in range(loops * SLOTS + 2, BLOCKS + 1):
                step(j, j % SLOTS, j)

        def has_group(role, lag):
            return 0 <= role - lag < GROUPS

        def has_unit(role, c, lag):
            return 0 <= CHUNKS * role + c - lag < CHUNKS * GROUPS

        def has_block(role, lag):
            return 0 <= role - lag < BLOCKS
        @block.sync
        def _(sp):
            sp.dma_start(x_raw[0][:], x[0]).then_inc(x_in0, 16)
            sp.dma_start(tw_raw[:], tok_w).then_inc(tw_in, 16)
            sp.dma_start(const[:], consts).then_inc(const_in, 16)
            sp.dma_start(row[:], rows).then_inc(const_in, 16)
            sp.dma_start(col[:], cols).then_inc(const_in, 16)
            sp.dma_start(x_raw[1][:], x[1]).then_inc(x_in1, 16)
            sp.dma_start(pw_raw[:], proj_w).then_inc(pw_in, 16)
            with sp.Fori(0, GROUPS // 2 - 1) as i:
                for u in range(2):
                    sp.wait_ge(lo_v_done, i * 2 + u + 1)
                    sp.wait_ge(lo_p_done, i * 2 + u + 1)
                    sp.dma_start(x_raw[u][:], x[at(i * 2 + 2 + u), :, :].rearrange("a p n -> (a p) n")).then_inc(x_in[u], 16)

            def stage_v(g, u):
                t = at(g * GT, GT)
                sp.dma_start(xv_hi[u][:].bitcast(F32), xsT_hi[:, t].bitcast(F32)).then_inc(xv_in[u], 16)
                sp.dma_start(xv_lo[u][:].bitcast(F32), xsT_lo[:, t].bitcast(F32)).then_inc(xv_in[u], 16)

            sp.wait_ge(main_done, GROUPS)
            sp.wait_ge(pw_done, 1)
            sp.wait_ge(xsT_done, 2)
            for g in range(2):
                stage_v(g, g)
            sp.dma_start(ow[:], out_w).then_inc(ow_in, 16)
            sp.wait_ge(xsT_done, GROUPS)
            sp.dma_start(w1_all[:], w1).then_inc(experts_in, 16)
            sp.dma_start(w2_all[:], w2).then_inc(experts_in, 16)
            sp.dma_start(b2_all[:], b2).then_inc(experts_in, 16)
            with sp.Fori(0, GROUPS // 2 - 1) as i:
                for u in range(2):
                    sp.wait_ge(v_done, i * (2 * GB) + (u + 1) * GB)
                    stage_v(i * 2 + 2 + u, u)
            sp.wait_ge(placed_done, GROUPS)
            sp.wait_ge(scattered0, GROUPS * GB * 16 + 16)
            sp.wait_ge(scattered1, GROUPS * GB * 16 + 16)
            sp.dma_start(block_no[:], block_nos).then_inc(block_no_in, 16)
            sp.wait_ge(tail_done, 1)
            for e in range(EXPERTS):
                start = sp.value_load(tail_at[0:1, e:e + 1], min_val=e * CAP, max_val=e * CAP + TOKENS)
                sp.dma_start(sorted_rows[bass.ds(start, BLOCK), :], pad[:]).then_inc(tails_out, 16)
            sp.wait_ge(tails_out, EXPERTS * 16)
            sp.wait_ge(table_done, 1)

            def load_block(j, slot):
                start = sp.value_load(blk_row[0:1, at(j)], min_val=0, max_val=DUMMY)
                sp.dma_start(xb[slot][:], sorted_rows[bass.ds(start, BLOCK), :]).then_inc(xb_in[slot], 16)

            for j in range(SLOTS):
                load_block(j, j)
            rounds = BLOCKS // SLOTS - 1
            with sp.Fori(0, rounds) as i:
                for k in range(SLOTS):
                    sp.wait_ge(y_out[k], i * 16 + 16)
                    load_block(i * SLOTS + SLOTS + k, k)
            for j in range((rounds + 1) * SLOTS, BLOCKS):
                sp.wait_ge(y_out[j % SLOTS], j // SLOTS * 16)
                load_block(j, j % SLOTS)
            for u in range(SLOTS):
                sp.wait_ge(y_out[u], 16 * len(range(u, BLOCKS, SLOTS)))
            for k in range(OUT_STEPS):
                for t, y in enumerate((y1[k], y2[k])):
                    a = t * TOKENS + k * OB * WIN
                    sp.dma_start(y[:], results[a:a + OB * WIN, :].rearrange("(b i) d -> i b d", i=WIN)).then_inc(y_in[k], 16)
            for k in range(OUT_STEPS):
                sp.wait_ge(out_ready, k + 1)
                sp.dma_start(out[k * OB:(k + 1) * OB].rearrange("b i d -> i b d"), y1[k][:]).then_inc(out_done, 16)
            sp.wait_ge(out_done, 16 * OUT_STEPS)

        @block.tensor
        def _(pe):
            def split_matmul(dst, w_hi, w_lo, m_hi, m_lo, first, last):
                pe.matmul(dst, w_hi, m_hi, start=first, stop=False)
                pe.matmul(dst, w_hi, m_lo, start=False, stop=False)
                return pe.matmul(dst, w_lo, m_hi, start=False, stop=last)

            pe.wait_ge(tw_done, 1)
            pe.wait_ge(const_in, 48)

            def step(g, u, role):
                def windows(t, r, half):
                    return t[:].rearrange("p (r b n) -> p r b n", r=STRIDE, b=GB)[:, r, :, half:half + WIN]

                def main(r0, r1):
                    for r in range(r0, r1):
                        for half in range(HALVES):
                            w = slice((half * STRIDE + r) * D, (half * STRIDE + r + 1) * D)
                            mm = split_matmul(bank[u][:, 0:GT], tw_hi[:, w], tw_lo[:, w], windows(x_hi[u], r, half),
                                              windows(x_lo[u], r, half), r == 0 and half == 0,
                                              r == STRIDE - 1 and half == HALVES - 1)
                    return mm

                if has_group(role, 0):
                    pe.wait_ge(lo_v_done, g + 1)
                    pe.wait_ge(lo_p_done, g + 1)
                    if has_group(role, 2):
                        pe.wait_ge(gelu_done, g - 1)
                    main(0, 2)
                if has_group(role, 1):
                    pe.wait_ge(gelu_done, g)
                    if has_group(role, 2):
                        pe.wait_ge(normed_done, g - 1)
                    for b in range(GB):
                        mm = pe.transpose(bank[2][0:WIN, b * D:(b + 1) * D], geluT[1 - u][:, b * WIN:(b + 1) * WIN], ident)
                    mm.then_inc(t1_done, 1)
                if has_group(role, 0):
                    main(2, 5)
                if has_group(role, 3):
                    pe.wait_ge(xs_done, g - 2)
                    for b in range(GB):
                        mm = pe.transpose(bank[3][:, b * WIN:(b + 1) * WIN], xs[1 - u][:, b * D:(b + 1) * D], ident_w)
                    mm.then_inc(t2_done, 1)
                if has_group(role, 0):
                    main(5, STRIDE).then_inc(main_done, 1)

            def project(dst, first_col, g):
                w = slice(first_col, first_col + 128)
                t = at(g * GT, GT)
                return split_matmul(dst[:, 0:GT], pw_hi[:, w], pw_lo[:, w], xsT_hi[:, t], xsT_lo[:, t], True, True)

            def project_a(g, c):
                project(bank[0], 3 * INNER + c * 128, g).then_inc(a_done, 1)

            def project_v(u, b):
                t = slice(b * WIN, (b + 1) * WIN)
                w = slice(2 * INNER, 3 * INNER)
                pe.matmul(bank[5][0:WIN, :], xv_hi[u][:, t], pw_hi[:, w], start=True, stop=False)
                pe.matmul(bank[5][0:WIN, :], xv_lo[u][:, t], pw_hi[:, w], start=False, stop=False)
                pe.matmul(bank[5][0:WIN, :], xv_hi[u][:, t], pw_lo[:, w], start=False, stop=True).then_inc(v_done, 1)

            def start():
                pe.wait_ge(xsT_done, 2)
                pe.wait_ge(pw_done, 1)
                project_a(0, 0)
                pe.wait_ge(e_done, 1)
                project_a(0, 1)
                pe.wait_ge(xv_in0, 32)
                project_v(0, 0)
                pe.wait_ge(vT_done, 1)
                project_v(0, 1)

            def unit(g, u, role, c):
                n = g * CHUNKS + c
                if has_unit(role, c, -2):
                    pe.wait_ge(e_done, n + 2)
                    project_a(g if c + 2 < CHUNKS else g + 1, (c + 2) % CHUNKS)
                if c == 3 and has_group(role, 2):
                    pe.wait_ge(qT_done, n if has_unit(role, c, 1) else GROUPS * CHUNKS)
                    pe.wait_ge(xmT_done, g - 1)
                    for b in range(GB):
                        mm = pe.matmul(bank[1][0:WIN, GT + b * EXPERTS:GT + (b + 1) * EXPERTS], xmT[:, b * WIN:(b + 1) * WIN],
                                       router_w, start=True, stop=True)
                    mm.then_inc(router_ps, 1)
                if has_unit(role, c, 0):
                    if has_unit(role, c, 1):
                        pe.wait_ge(qT_done, n)
                    if c == 0 and has_group(role, 3):
                        pe.wait_ge(logits_done, g - 2)
                    project(bank[1], c * 128, g).then_inc(q_done, 1)
                    if has_unit(role, c, 1):
                        pe.wait_ge(kb_done, n)
                    project(bank[4], INNER + c * 128, g).then_inc(k_done, 1)
                if has_unit(role, c, 1):
                    pe.wait_ge(qT_done, n)
                    pe.wait_ge(kT_done, n)
                    if has_unit(role, c, 2):
                        pe.wait_ge(attn_done, n * 2 - 2)
                    for hd in range(2):
                        f = slice(hd * DH, (hd + 1) * DH)
                        for b in range(GB):
                            t = slice(b * WIN, (b + 1) * WIN)
                            mm = pe.matmul(bank[6 + hd][0:WIN, t], kT[(c + 1) % 2][f, t], qT[(c + 1) % 2][f, t],
                                           start=True, stop=True)
                        mm.then_inc(sim_done, 1)
                if c == 2 and has_group(role, 2):
                    pe.wait_ge(xm_done, g - 1)
                    pe.wait_ge(h2_done, g - 1)
                    for b in range(GB):
                        mm = pe.transpose(bank[3][:, b * WIN:(b + 1) * WIN], xm[u][:, 0, b, 0:D], ident_w)
                    mm.then_inc(xmT_ps, 1)
                if has_unit(role, c, -2) and (c + 2) // CHUNKS + role < GROUPS:
                    pe.wait_ge(vT_done, n + 2)
                    w = u if c < 2 else 1 - u
                    if c == 2:
                        pe.wait_ge(xv_in[w], g * 16 + (48 if u else 32))
                    project_v(w, (c + 2) % CHUNKS)
                if c == 1 and has_group(role, 3):
                    pe.wait_ge(both_done, g - 2)
                    pe.wait_ge(oT_done, n - 2 if has_unit(role, c, 3) else GROUPS * CHUNKS)
                    m = both[:].rearrange("p b e -> p (b e)")
                    pe.matmul(bank[2][0:WIN, GT:GT + GB * EXPERTS], const_of("before", WIN), m, start=True, stop=True)
                    pe.matmul(bank[2][0:WIN, GT + GB * EXPERTS:GT + 2 * GB * EXPERTS], const_of("ones", WIN), m, start=True,
                              stop=True).then_inc(prefix_ps, 1)
                if has_unit(role, c, 2):
                    pe.wait_ge(attn_done, n * 2 - 2)
                    if has_unit(role, c, 3):
                        pe.wait_ge(oT_done, n - 2)
                    if c == 2:
                        pe.wait_ge(vT_done, (g + 1) * GB)
                    w = u if c >= 2 else 1 - u
                    for hd in range(2):
                        h0 = (2 * ((c + 2) % CHUNKS) + hd) * DH
                        for b in range(GB):
                            t = slice(b * WIN, (b + 1) * WIN)
                            mm = pe.matmul(bank[2][hd * DH:(hd + 1) * DH, t], v[w][:, b, h0:h0 + DH],
                                           attnT[c % 2][:, hd, t], start=True, stop=True)
                    mm.then_inc(av_done, 1)
                if c == 2 and has_group(role, 1):
                    pe.wait_ge(oT_done, g * CHUNKS)
                    if has_group(role, 2):
                        pe.wait_ge(xmT_done, g - 1)
                    if role == 1:
                        pe.wait_ge(ow_in, 16)
                    for b in range(GB):
                        for k in range(CHUNKS):
                            mm = pe.matmul(bank[3][0:WIN, b * D:(b + 1) * D], oT[k][:, b * WIN:(b + 1) * WIN],
                                           ow[:, k * D:(k + 1) * D], start=k == 0, stop=k == CHUNKS - 1)
                    mm.then_inc(proj_done, 1)

            tokenizer_and_attention(pe, step, start, unit)

            def turn_block(j, slot):
                pe.transpose(bank[slot % 2][:, 0:BLOCK], xb[slot][:, 0:D], ident).then_inc(xT_ps, 1)

            pe.wait_ge(xb_in[0], 16)
            turn_block(0, 0)
            pe.wait_ge(experts_in, 48)

            def block_step(j, slot, role):
                nxt = (slot + 1) % SLOTS
                if has_block(role, -1):
                    pe.wait_ge(xb_in[nxt], (j + 1 - nxt) * (16 // SLOTS) + 16)
                    if has_block(role, 1):
                        pe.wait_ge(xT_done, j)
                    turn_block(j + 1, nxt)
                if has_block(role, 0):
                    pe.wait_ge(xT_done, j + 1)
                    pe.wait_ge(w1_done, j + 1)
                    for f in range(FFC):
                        mm = pe.matmul(bank[4 + slot % 2][:, f * BLOCK:(f + 1) * BLOCK], w1_blk[slot % 2][:, f * 128:(f + 1) * 128],
                                       xbT[slot % 2][:], start=True, stop=True)
                    mm.then_inc(hidden_ps, 1)
                if has_block(role, 1):
                    p = (slot + 1) % 2
                    e = pe.value_load(blk_expert[0:1, at(j - 1)], min_val=0, max_val=EXPERTS - 1)
                    pe.wait_ge(hidden_done, j)
                    if has_block(role, 2):
                        pe.wait_ge(yb_done, j - 1)
                    for f in range(FFC):
                        mm = pe.matmul(bank[6 + p][:, 0:D], hT[p][:, f, :], w2_all[:, bass.ds(e * FF + f * D, D)],
                                       start=f == 0, stop=f == FFC - 1)
                    mm.then_inc(y_ps, 1)

            expert_steps(pe, block_step)

        @block.scalar
        def _(act):
            act.preload_act_table_set("gelu_and_others")

            def split_hi(g, u):
                act.activation(x_hi[u][:], x_raw[u][:], ACT.Copy).then_inc(hi_done, 1)

            act.wait_ge(tw_in, 16)
            act.activation(tw_hi[:], tw_raw[:], ACT.Copy).then_inc(tw_hi_done, 1)
            act.wait_ge(x_in0, 16)
            split_hi(0, 0)
            act.wait_ge(x_in1, 16)
            split_hi(1, 1)
            act.wait_ge(const_in, 48)
            act.wait_ge(pw_scaled, 1)
            act.activation(pw_hi[:], pw_raw[:], ACT.Copy).then_inc(pw_hi_done, 1)

            def step(g, u, role):
                if has_group(role, 1):
                    act.wait_ge(main_done, g)
                    if has_group(role, 3):
                        act.wait_ge(t1_done, g - 2)
                    act.activation(geluT[1 - u][:], bank[1 - u][:, 0:GT], ACT.Gelu, bias=col_of("tok_b")).then_inc(gelu_done, 1)
                if has_group(role, 1) and has_group(role, -1):
                    act.wait_ge(x_in[1 - u], g * 8 + (24 if u else 16))
                    split_hi(g + 1, 1 - u)
                if has_group(role, 1):
                    act.wait_ge(shift1_done, g)
                    if has_group(role, 3):
                        act.wait_ge(h_done, g - 2)
                    for b in range(GB):
                        ins = act.activation(normed[1 - u][:, b * D:(b + 1) * D], bank[2][0:WIN, b * D:(b + 1) * D], ACT.Identity,
                                             bias=shift1[:, b:b + 1], scale=rstd1[:, b:b + 1])
                    ins.then_inc(normed_done, 1)
                if has_group(role, 3):
                    act.wait_ge(t2_done, g - 2)
                    act.activation(xsT_hi[:, at((g - 3) * GT, GT)], bank[3][:, 0:GT], ACT.Copy).then_inc(xsT_hi_done, 1)

            def exp_minus_a(c, k, reused):
                act.wait_ge(a_done, k + 1)
                if reused:
                    act.wait_ge(log_done, k - 1)
                act.activation(growth[c % 2][:], bank[0][:, 0:GT], ACT.Exp, bias=neg_b_a[:, c:c + 1], scale=-1.0).then_inc(e_done, 1)

            def log(c, k, reused):
                act.wait_ge(clip_done, k + 1)
                if reused:
                    act.wait_ge(scan_done, k)
                act.activation(log_growth[:, :, 1:WIN + 1], growth[c % 2][:].rearrange("p (b i) -> p b i", b=GB),
                               ACT.Ln).then_inc(log_done, 1)

            def cumulate(c, k, reused):
                act.wait_ge(scan_done, k + 1)
                if reused:
                    act.wait_ge(qT_done, k - 1)
                    act.wait_ge(kT_done, k - 1)
                act.activation(a_cum[c % 2][:], log_sum[:, :, 1:WIN + 1], ACT.Exp, scale=-1.0).then_inc(cum_done, 1)
                act.activation(a_inv[c % 2][:], log_sum[:, :, 1:WIN + 1], ACT.Exp).then_inc(inv_done, 1)

            def start():
                act.preload_act_table_set("natural_log_exp_and_others")
                act.wait_ge(main_done, GROUPS)
                act.wait_ge(neg_b_done, 1)
                act.wait_ge(log_start_done, 1)
                exp_minus_a(0, 0, False)
                exp_minus_a(1, 1, False)
                log(0, 0, False)
                cumulate(0, 0, False)

            def unit(g, u, role, c):
                n = g * CHUNKS + c
                if has_unit(role, c, -1):
                    log((c + 1) % CHUNKS, n + 1, True)
                if c == 2 and has_group(role, 3):
                    act.wait_ge(prefix_ps, g - 2)
                    if has_unit(role, c, 3):
                        act.wait_ge(av_done, n - 2)
                    act.activation(counts[:].rearrange("p t b e -> p (t b e)"), bank[2][0:WIN, GT:GT + 2 * GB * EXPERTS],
                                   ACT.Copy).then_inc(counts_done, 1)
                if has_unit(role, c, 3):
                    act.wait_ge(av_done, n - 2)
                    if c == 3 and has_group(role, 1):
                        act.wait_ge(proj_done, g)
                    act.activation(oT[(c + 1) % CHUNKS][:], bank[2][:, 0:GT], ACT.Copy).then_inc(oT_done, 1)
                if has_unit(role, c, -2):
                    exp_minus_a((c + 2) % CHUNKS, n + 2, True)
                if has_unit(role, c, -1):
                    cumulate((c + 1) % CHUNKS, n + 1, has_unit(role, c, 1))
                if has_unit(role, c, 0):
                    act.wait_ge(k_done, n + 1)
                    if has_unit(role, c, 2):
                        act.wait_ge(kT_done, n - 1)
                    act.activation(kb[c % 2][:], bank[4][:, 0:GT], ACT.Identity, bias=col_of("b_k", c)).then_inc(kb_done, 1)
                if c == 1 and has_group(role, 2):
                    act.wait_ge(shift3_done, g - 1)
                    if has_group(role, 3):
                        act.wait_ge(scattered[u], (g - u - 2) * (GB * 16) + 16)
                    for b in range(GB):
                        ins = act.activation(xm[u][:, 0, b, 0:D], h_all[:, at((g - 2) * (GB * D) + b * D, D)], ACT.Identity,
                                             bias=shift3[:, b:b + 1], scale=rstd3[:, b:b + 1])
                    ins.then_inc(xm_done, 1)
                if c == 2 and has_group(role, 2):
                    act.wait_ge(xmT_ps, g - 1)
                    act.activation(xmT[:], bank[3][:, 0:GT], ACT.Copy).then_inc(xmT_done, 1)
                    act.activation(xm[u][:, 1, :, 0:D], xm[u][:, 0, :, 0:D], ACT.Copy).then_inc(xm_twice, 1)
                if c == 3 and has_group(role, 2):
                    act.wait_ge(shifted_done, g - 1)
                    act.activation(expd[:], shifted[:], ACT.Exp).then_inc(exp_done, 1)

            tokenizer_and_attention(act, step, start, unit)

            act.preload_act_table_set("gelu_and_others")
            act.wait_ge(table_done, 1)

            def block_step(j, slot, role):
                if has_block(role, 0):
                    p = slot % 2
                    e = act.value_load(blk_expert[0:1, at(j)], min_val=0, max_val=EXPERTS - 1)
                    act.wait_ge(hidden_ps, j + 1)
                    for f in range(FFC):
                        ins = act.activation(hT[p][:, f, :], bank[4 + p][:, f * BLOCK:(f + 1) * BLOCK], ACT.Gelu,
                                             bias=b1_all[:, bass.ds(e * FFC + f, 1)])
                    ins.then_inc(hidden_done, 1)

            expert_steps(act, block_step)

        @block.vector
        def _(dve):
            dve.memset(pad[:], 0.0).then_inc(pad_done, 1)
            dve.memset(running[:], 0.0).then_inc(running_done, 1)
            dve.wait_ge(pad_done, 1)
            dve.memset(pad[:, D:D + 1].bitcast(U32), NO_ROW).then_inc(pad_done, 1)

            def split_lo(g, u):
                dve.tensor_tensor(x_lo[u][:, X_SPLIT:], x_raw[u][:, X_SPLIT:], x_hi[u][:, X_SPLIT:].bitcast(F32),
                                  ALU.subtract).then_inc(lo_v_done, 1)

            dve.wait_ge(tw_hi_done, 1)
            dve.tensor_tensor(tw_lo[:], tw_raw[:], tw_hi[:].bitcast(F32), ALU.subtract).then_inc(tw_done, 1)
            dve.wait_ge(hi_done, 1)
            split_lo(0, 0)
            dve.wait_ge(hi_done, 2)
            split_lo(1, 1)
            dve.wait_ge(pw_in, 16)
            dve.wait_ge(const_in, 48)
            dve.tensor_scalar(pw_raw[:], pw_raw[:], col_of("attn_gamma"), None, ALU.mult).then_inc(pw_scaled, 1)
            dve.tensor_scalar(neg_b_a[:], b_a, -1.0, None, ALU.mult).then_inc(neg_b_done, 1)
            dve.wait_ge(pw_hi_done, 1)
            dve.tensor_tensor(pw_lo[:], pw_raw[:], pw_hi[:].bitcast(F32), ALU.subtract).then_inc(pw_done, 1)

            def step(g, u, role):
                if has_group(role, 1):
                    dve.wait_ge(t1_done, g)
                    for b in range(GB):
                        ins = dve.bn_stats(stat1[:, b, :], bank[2][0:WIN, b * D:(b + 1) * D])
                    ins.then_inc(stat1_done, 1)
                    dve.wait_ge(const_in, 48)
                    dve.wait_ge(stat1_done, g)
                    for b in range(GB):
                        ins = dve.bn_aggr(mv1[:, b, :], stat1[:, b, :])
                    ins.then_inc(mv1_done, 1)
                    dve.wait_ge(mv1_done, g)
                    dve.tensor_scalar(neg_mean1[:], mv1[:, :, 0], -1.0, None, ALU.mult)
                    dve.tensor_scalar(var1[:], mv1[:, :, 1], EPS, None, ALU.add).then_inc(var1_done, 1)
                if has_group(role, 2):
                    dve.wait_ge(h_done, g - 1)
                    for b in range(GB):
                        ins = dve.bn_stats(stat2[:, b, :], h_all[:, at((g - 2) * (GB * D) + b * D, D)])
                    ins.then_inc(stat2_done, 1)
                    dve.wait_ge(const_in, 48)
                    dve.wait_ge(stat2_done, g - 1)
                    for b in range(GB):
                        ins = dve.bn_aggr(mv2[:, u, b, :], stat2[:, b, :])
                    ins.then_inc(mv2_done, 1)
                    dve.wait_ge(mv2_done, g - 1)
                    dve.tensor_scalar(base2[:, 0:GB], mv2[:, u, :, 1], EPS, None, ALU.add)
                    dve.tensor_scalar(base2[:, GB:2 * GB], mv2[:, u, :, 1], float(D), None, ALU.mult).then_inc(base2_done, 1)
                if has_group(role, 1) and has_group(role, -1):
                    dve.wait_ge(hi_done, g + 2)
                    split_lo(g + 1, 1 - u)
                if has_group(role, 3):
                    dve.wait_ge(xsT_hi_done, g - 2)
                    t = at((g - 3) * GT, GT)
                    dve.tensor_tensor(xsT_lo[:, t], bank[3][:, 0:GT], xsT_hi[:, t].bitcast(F32), ALU.subtract).then_inc(xsT_done, 1)
                if has_group(role, 2):
                    dve.wait_ge(root2_done, g - 1)
                    dve.tensor_tensor(norm2[:, 0, :], root2[:, 0:GB], root2[:, GB:2 * GB], ALU.mult).then_inc(length_done, 1)
                    dve.wait_ge(length_done, g - 1)
                    dve.tensor_scalar(norm2[:, 1, :], norm2[:, 0, :], 1e-12, None, ALU.max).then_inc(guarded_done, 1)
                    dve.wait_ge(guarded_done, g - 1)
                    dve.reciprocal(norm2[:, 2, :], norm2[:, 1, :]).then_inc(inverse_done, 1)
                    dve.wait_ge(inverse_done, g - 1)
                    dve.scalar_tensor_tensor(scale2[:], root2[:, 0:GB], float(D) ** 0.5, norm2[:, 2, :], ALU.mult,
                                             ALU.mult).then_inc(scale2_done, 1)
                    dve.wait_ge(scale2_done, g - 1)
                    for b in range(GB):
                        ins = dve.tensor_scalar(xs[u][:, b * D:(b + 1) * D], h_all[:, at((g - 2) * (GB * D) + b * D, D)],
                                                mv2[:, u, b, 0:1], scale2[:, b:b + 1], ALU.subtract, ALU.mult)
                    ins.then_inc(xs_done, 1)

            def clip(c, k):
                dve.wait_ge(e_done, k + 1)
                dve.tensor_scalar(growth[c % 2][:], growth[c % 2][:], 1.0, 1e10, ALU.add, ALU.min).then_inc(clip_done, 1)

            def scan(k, reused):
                dve.wait_ge(log_done, k + 1)
                if reused:
                    dve.wait_ge(inv_done, k)
                dve.tensor_tensor_scan(log_sum[:].rearrange("p b i -> p (b i)"), log_growth[:].rearrange("p b i -> p (b i)"),
                                       const_of("log_cap"), 0.0, ALU.add, ALU.min).then_inc(scan_done, 1)

            def store_v(w, b, count):
                dve.wait_ge(v_done, count)
                dve.tensor_tensor(v[w][:, b, :], bank[5][0:WIN, :], row_of("b_v"), ALU.add).then_inc(vT_done, 1)

            def start():
                dve.wait_ge(main_done, GROUPS)
                dve.memset(log_growth[:, :, 0:1], 0.0).then_inc(log_start_done, 1)
                clip(0, 0)
                clip(1, 1)
                scan(0, False)
                store_v(0, 0, 1)
                store_v(0, 1, 2)

            def unit(g, u, role, c):
                n = g * CHUNKS + c
                if has_unit(role, c, -1):
                    scan(n + 1, True)
                if has_unit(role, c, 0):
                    dve.wait_ge(q_done, n + 1)
                    dve.wait_ge(cum_done, n + 1)
                    dve.scalar_tensor_tensor(qT[c % 2][:], bank[1][:, 0:GT], col_of("b_q", c),
                                             a_cum[c % 2][:].rearrange("p b i -> p (b i)"), ALU.add, ALU.mult).then_inc(qT_done, 1)
                if c == 3 and has_group(role, 2):
                    router_logits(g, role)
                if has_unit(role, c, -2):
                    clip((c + 2) % CHUNKS, n + 2)

                def mask(hd):
                    dve.wait_ge(sim_done, n * 2 - 1 + hd)
                    if hd == 0 and has_unit(role, c, 3):
                        dve.wait_ge(av_done, n - 2)
                    dve.tensor_tensor(attnT[(c + 1) % 2][:, hd, :], bank[6 + hd][0:WIN, 0:GT], causal,
                                      ALU.mult).then_inc(attn_done, 1)

                if has_unit(role, c, 1):
                    mask(0)
                if has_unit(role, c, 0):
                    dve.wait_ge(kb_done, n + 1)
                    dve.wait_ge(inv_done, n + 1)
                    dve.scalar_tensor_tensor(kT[c % 2][:], a_inv[c % 2][:].rearrange("p b i -> p (b i)"), 1e8,
                                             kb[c % 2][:], ALU.min, ALU.mult).then_inc(kT_done, 1)
                if has_unit(role, c, 1):
                    mask(1)
                if c == 0 and has_group(role, 2):
                    statistics_3(g)
                if has_unit(role, c, -2) and (c + 2) // CHUNKS + role < GROUPS:
                    store_v(u if c < 2 else 1 - u, (c + 2) % CHUNKS, n + 3)
                if c == 0 and has_group(role, 3):
                    choose(g, u)
                if c == 3 and has_group(role, 1):
                    residual(g)

            def residual(g):
                dve.wait_ge(proj_done, g)
                dve.wait_ge(hb_done, g)
                h = at((g - 1) * (GB * D), GB * D)
                dve.tensor_tensor(h_all[:, h], bank[3][0:WIN, :], h_all[:, h], ALU.add).then_inc(h2_done, 1)
                dve.wait_ge(const_in, 48)
                dve.wait_ge(h2_done, g)
                for b in range(GB):
                    ins = dve.bn_stats(stat3[:, b, :], h_all[:, at((g - 1) * (GB * D) + b * D, D)])
                ins.then_inc(stat3_done, 1)

            def statistics_3(g):
                dve.wait_ge(stat3_done, g - 1)
                dve.sem_inc(dve_go, 1)
                for b in range(GB):
                    ins = dve.bn_aggr(mv3[:, b, :], stat3[:, b, :])
                ins.then_inc(mv3_done, 1)
                dve.wait_ge(mv3_done, g - 1)
                dve.tensor_scalar(neg_mean3[:], mv3[:, :, 0], -1.0, None, ALU.mult)
                dve.tensor_scalar(var3[:], mv3[:, :, 1], EPS, None, ALU.add).then_inc(var3_done, 1)

            def router_logits(g, role):
                dve.wait_ge(router_ps, g - 1)
                if has_group(role, 0):
                    dve.wait_ge(q_done, (g + 1) * CHUNKS)
                dve.tensor_tensor(logits[:].rearrange("p b e -> p (b e)"), bank[1][0:WIN, GT:GT + GB * EXPERTS], row_of("router_b"),
                                  ALU.add).then_inc(logits_done, 1)
                dve.wait_ge(logits_done, g - 1)
                dve.tensor_reduce(top_logit[:], logits[:], AX_X, ALU.max).then_inc(top_logit_done, 1)
                dve.wait_ge(top_logit_done, g - 1)
                dve.tensor_tensor(shifted[:], logits[:], spread(top_logit[:]), ALU.subtract).then_inc(shifted_done, 1)

            def choose(g, u):
                dve.wait_ge(exp_done, g - 2)
                dve.tensor_reduce(exp_sum[:], expd[:], AX_X, ALU.add).then_inc(sum_done, 1)
                dve.wait_ge(sum_done, g - 2)
                dve.reciprocal(exp_rec[:], exp_sum[:]).then_inc(rec_done, 1)
                dve.wait_ge(rec_done, g - 2)
                dve.tensor_tensor(probs[:], expd[:], spread(exp_rec[:]), ALU.mult).then_inc(probs_done, 1)
                dve.wait_ge(const_in, 48)
                dve.wait_ge(probs_done, g - 2)
                for b in range(GB):
                    ins = dve.max(top8[:, b, :], probs[:, b, :])
                ins.then_inc(top8_done, 1)
                dve.wait_ge(const_in, 48)
                dve.wait_ge(top8_done, g - 2)
                for b in range(GB):
                    ins = dve.max_index(top8_at[:, b, :], top8[:, b, :], probs[:, b, :])
                ins.then_inc(top8_at_done, 1)
                dve.tensor_copy(xm[1 - u][:, :, :, D + 1], top8[:, :, 0:2].rearrange("p b t -> p t b")).then_inc(gates_done, 1)
                dve.wait_ge(top8_at_done, g - 2)
                dve.tensor_copy(top8_atf[:], top8_at[:]).then_inc(top8_atf_done, 1)
                dve.wait_ge(top8_atf_done, g - 2)
                dve.wait_ge(place_done, g - 2)
                for t in range(2):
                    ins = dve.tensor_tensor(chosen[:, t], expert_no, spread(top8_atf[:, :, t]), ALU.is_equal)
                ins.then_inc(chosen_done, 1)

            tokenizer_and_attention(dve, step, start, unit)

            dve.wait_ge(running_done, GROUPS * (GB + 1) + 1)
            dve.wait_ge(placed_done, GROUPS)
            in_all = running[0:1, GB, :]
            dve.tensor_tensor(tail_f[:], in_all, first_row[0:1, 0, :], ALU.add).then_inc(tail_f_done, 1)
            dve.tensor_scalar(n_int[:], in_all, float(BLOCK - 1), None, ALU.add).then_inc(n_int_done, 1)
            dve.memset(zero16[:], 0.0)
            dve.wait_ge(tail_f_done, 1)
            dve.tensor_copy(tail_at[:], tail_f[:]).then_inc(tail_done, 1)
            dve.wait_ge(n_int_done, 1)
            dve.tensor_scalar(nb_int[:], n_int[:], BLOCK.bit_length() - 1, None, ALU.arith_shift_right).then_inc(nb_int_done, 1)
            dve.wait_ge(nb_int_done, 1)
            dve.tensor_copy(nb_f[:], nb_int[:]).then_inc(nb_f_done, 1)
            dve.wait_ge(nb_f_done, 1)
            dve.tensor_tensor_scan(nb_end[:], nb_f[:], zero16[:], 0.0, ALU.add, ALU.add).then_inc(nb_end_done, 1)
            dve.wait_ge(nb_end_done, 1)
            dve.wait_ge(block_no_in, 16)
            dve.tensor_tensor(past[:], nb_end[:].unsqueeze(1).to_broadcast([1, BLOCKS, EXPERTS]), block_no[:],
                              ALU.is_le).then_inc(past_done, 1)
            dve.wait_ge(past_done, 1)
            dve.tensor_tensor(past_nb[:], past[:], nb_f[:].unsqueeze(1).to_broadcast([1, BLOCKS, EXPERTS]),
                              ALU.mult).then_inc(past_nb_done, 1)
            dve.tensor_reduce(blk_e[:], past[:], AX_X, ALU.add).then_inc(blk_e_done, 1)
            dve.wait_ge(past_nb_done, 1)
            dve.tensor_reduce(blk_s[:], past_nb[:], AX_X, ALU.add).then_inc(blk_s_done, 1)
            dve.wait_ge(blk_e_done, 1)
            dve.tensor_scalar(blk_expert[:], blk_e[:], float(EXPERTS - 1), None, ALU.min).then_inc(blk_expert_done, 1)
            dve.wait_ge(blk_s_done, 1)
            dve.tensor_tensor(blk_r[:], block_no[:, :, 0], blk_s[:], ALU.subtract).then_inc(blk_r_done, 1)
            dve.tensor_scalar(blk_q[:], blk_e[:], float(CAP), None, ALU.mult).then_inc(blk_q_done, 1)
            dve.wait_ge(blk_q_done, 1)
            dve.scalar_tensor_tensor(blk_t[:], blk_r[:], float(BLOCK), blk_q[:], ALU.mult, ALU.add).then_inc(blk_t_done, 1)
            dve.wait_ge(blk_t_done, 1)
            dve.tensor_scalar(blk_row[:], blk_t[:], float(DUMMY), None, ALU.min).then_inc(table_done, 1)
            dve.wait_ge(table_done, 1)
            dve.wait_ge(experts_in, 48)

            def prepare(j, p):
                e = dve.value_load(blk_expert[0:1, at(j)], min_val=0, max_val=EXPERTS - 1)
                dve.tensor_copy(w1_blk[p][:], w1_all[:, bass.ds(e * FF, FF)]).then_inc(w1_done, 1)
                dve.wait_ge(xT_ps, j + 1)
                dve.tensor_copy(xbT[p][:], bank[p][:, 0:BLOCK]).then_inc(xT_done, 1)

            prepare(0, 0)

            def block_step(j, slot, role):
                if has_block(role, -1):
                    if has_block(role, 1):
                        dve.wait_ge(hidden_ps, j)
                    prepare(j + 1, (slot + 1) % 2)
                if has_block(role, 1):
                    p, last = (slot + 1) % 2, (slot - 1) % SLOTS
                    e = dve.value_load(blk_expert[0:1, at(j - 1)], min_val=0, max_val=EXPERTS - 1)
                    dve.wait_ge(y_ps, j)
                    dve.tensor_tensor(yb[p][:], bank[6 + p][:, 0:D], b2_all[:, bass.ds(e * D, D)], ALU.add).then_inc(yb_done, 1)
                    dve.wait_ge(yb_done, j)
                    dve.tensor_scalar(yg[last][:], yb[p][:], xb[last][:, D + 1:D + 2], None, ALU.mult).then_inc(yg_done, 1)

            expert_steps(dve, block_step)

            for k in range(OUT_STEPS):
                dve.wait_ge(y_in[k], 32)
                h = h_all[:, k * OB * D:(k + 1) * OB * D]
                f1, f2 = (y[k][:].rearrange("p b d -> p (b d)") for y in (y1, y2))
                dve.tensor_tensor(f1, f1, f2, ALU.add).then_inc(sum_done2, 1)
                dve.wait_ge(sum_done2, k + 1)
                dve.tensor_tensor(f1, f1, h, ALU.add).then_inc(out_ready, 1)

        @block.gpsimd
        def _(pool):
            def split_lo(g, u):
                pool.tensor_tensor(x_lo[u][:, 0:X_SPLIT], x_raw[u][:, 0:X_SPLIT], x_hi[u][:, 0:X_SPLIT].bitcast(F32),
                                   ALU.subtract).then_inc(lo_p_done, 1)

            pool.wait_ge(hi_done, 1)
            split_lo(0, 0)
            pool.wait_ge(hi_done, 2)
            split_lo(1, 1)
            pool.wait_ge(const_in, 48)
            pool.wait_ge(pad_done, 2)
            half = BLOCK // 2
            for u in range(2):
                pool.dma_start(sorted_rows[DUMMY + u * half:DUMMY + (u + 1) * half, :], pad[u * half:(u + 1) * half, :]).then_inc(scattered[u], 16)

            def step(g, u, role):
                if has_group(role, 1):
                    pool.wait_ge(var1_done, g)
                    if has_group(role, 2):
                        pool.wait_ge(normed_done, g - 1)
                    pool.tensor_tensor(rstd1[:], var1[:], power[:, 0:GB], ALU.pow).then_inc(rstd1_done, 1)
                    pool.wait_ge(rstd1_done, g)
                    pool.tensor_tensor(shift1[:], neg_mean1[:], rstd1[:], ALU.mult).then_inc(shift1_done, 1)
                if has_group(role, 2):
                    pool.wait_ge(base2_done, g - 1)
                    pool.tensor_tensor(root2[:], base2[:], power, ALU.pow).then_inc(root2_done, 1)
                if has_group(role, 1) and has_group(role, -1):
                    pool.wait_ge(hi_done, g + 2)
                    split_lo(g + 1, 1 - u)
                if has_group(role, 1):
                    pool.wait_ge(normed_done, g)
                    pool.tensor_tensor(by_row(scaled[:]), by_row(normed[1 - u][:]), each_row("gamma"), ALU.mult).then_inc(scaled_done, 1)
                    pool.wait_ge(scaled_done, g)
                    pool.tensor_tensor(by_row(h_all[:, at((g - 1) * (GB * D), GB * D)]), by_row(scaled[:]), each_row("beta"), ALU.add).then_inc(h_done, 1)

            def scatter(g, u, batches):
                for b in batches:
                    for t in range(2):
                        pool.indirect_dma_start(sorted_rows, bass.IndirectOffsetOnAxis(ap=place_u[1 - u][:, t * GB + b:t * GB + b + 1], axis=0),
                                                xm[1 - u][:, t, b, :], None).then_inc(scattered[1 - u], 16)

            def start():
                pool.sem_inc(place_done, 1)

            def sort_group(g, u, role):
                pool.wait_ge(counts_done, g - 2)
                pool.wait_ge(running_done, (g - 3) * (GB + 1) + 1)
                pool.sem_inc(pool_go, 1)
                pool.tensor_copy(running[:, 0, :], running[:, GB, :]).then_inc(running_done, 1)
                for b in range(GB):
                    pool.wait_ge(running_done, (g - 3) * (GB + 1) + 2 + b)
                    pool.tensor_tensor(running[:, b + 1, :], counts[:, 1, b, :], running[:, b, :], ALU.add).then_inc(running_done, 1)
                pool.tensor_tensor(rank[:], counts[:, 0], running[:, 0:GB, :], ALU.add).then_inc(rank_done, 1)
                pool.wait_ge(rank_done, g - 2)
                pool.tensor_tensor(ranked[:], rank[:], first_row, ALU.add).then_inc(ranked_done, 1)
                pool.wait_ge(ranked_done, g - 2)
                for t in range(2):
                    ins = pool.tensor_tensor(place[:, t], chosen[:, t], ranked[:], ALU.mult)
                ins.then_inc(place_done, 1)
                pool.wait_ge(place_done, g - 1)
                p = place[:].rearrange("p t b e -> p (t b) e")
                pool.tensor_tensor(place_8[:], p[:, :, 0:8], p[:, :, 8:16], ALU.add).then_inc(place_8_done, 1)
                pool.wait_ge(place_8_done, g - 2)
                pool.tensor_tensor(place_4[:], place_8[:, :, 0:4], place_8[:, :, 4:8], ALU.add).then_inc(place_4_done, 1)
                pool.wait_ge(place_4_done, g - 2)
                pool.tensor_tensor(place_2[:], place_4[:, :, 0:2], place_4[:, :, 2:4], ALU.add).then_inc(place_2_done, 1)
                pool.wait_ge(place_2_done, g - 2)
                pool.tensor_tensor(place_f[:], place_2[:, :, 0], place_2[:, :, 1], ALU.add).then_inc(place_f_done, 1)
                pool.wait_ge(place_f_done, g - 2)
                pool.sem_inc(pool_go, 1)
                pool.tensor_copy(place_u[1 - u][:], place_f[:]).then_inc(placed_done, 1)

            def unit(g, u, role, c):
                if c == 0 and has_group(role, 2):
                    pool.wait_ge(var3_done, g - 1)
                    pool.tensor_tensor(rstd3[:], var3[:], power[:, 0:GB], ALU.pow).then_inc(rstd3_done, 1)
                    pool.wait_ge(rstd3_done, g - 1)
                    pool.tensor_tensor(shift3[:], neg_mean3[:], rstd3[:], ALU.mult).then_inc(shift3_done, 1)
                if c == 0 and has_group(role, 0):
                    h = by_row(h_all[:, at(g * (GB * D), GB * D)])
                    pool.tensor_tensor(h, h, each_row("b_out"), ALU.add).then_inc(hb_done, 1)
                if c == 0 and has_group(role, 3):
                    pool.wait_ge(chosen_done, g - 2)
                    pool.tensor_tensor(both[:], chosen[:, 0], chosen[:, 1], ALU.add).then_inc(both_done, 1)
                if c == 1 and has_group(role, 2):
                    if has_group(role, 3):
                        pool.wait_ge(scattered[u], (g - u - 2) * (GB * 16) + 16)
                        pool.sem_inc(pool_go, 1)
                    pool.tensor_copy(xm[u][:, :, :, D].bitcast(U32), result_row).then_inc(dest_done, 1)
                    pool.wait_ge(dest_done, g * 2 - 3)
                    pool.tensor_tensor(result_row, result_row, group_tokens, ALU.add).then_inc(dest_done, 1)
                    pool.wait_ge(dest_done, g * 2 - 2)
                if c == 2 and has_group(role, 3):
                    sort_group(g, u, role)
                    pool.wait_ge(placed_done, g - 2)
                    pool.wait_ge(gates_done, g - 2)
                    pool.wait_ge(dest_done, g * 2 - 4)
                    pool.wait_ge(xm_twice, g - 2)
                    pool.sem_inc(pool_go, 1)
                if c >= 2 and has_group(role, 3):
                    scatter(g, u, range(2 * c - 4, 2 * c - 2))

            tokenizer_and_attention(pool, step, start, unit)

            def block_step(j, slot, role):
                if has_block(role, 1):
                    last = (slot - 1) % SLOTS
                    pool.wait_ge(yg_done, j)
                    pool.sem_inc(pool_go, 1)
                    pool.indirect_dma_start(results, bass.IndirectOffsetOnAxis(ap=xb[last][:, D:D + 1].bitcast(U32), axis=0),
                                            yg[last][:], None, bounds_check=NO_ROW - 1, oob_is_err=False).then_inc(y_out[last], 16)

            expert_steps(pool, block_step)


def shape_constants(np):
    f = np.float32
    i = np.arange(WIN)
    parts = {
        "ident": np.eye(128),
        "causal": np.tile(np.where(i[None, :] >= i[:, None], SCALE, 0.0), (1, GB)),
        "before": (i[:, None] < i[None, :]).astype(f),
        "ones": np.ones((WIN, WIN)),
        "log_cap": np.tile(np.where(np.arange(WIN + 1) == 0, 0.0, LOG_CAP), (128, GB)),
        "first_row": np.tile(np.arange(EXPERTS) * CAP, (128, GB)),
        "expert": np.tile(np.arange(EXPERTS), (128, GB)),
        "result_row": (np.arange(2)[None, :, None] * TOKENS + np.arange(GB)[None, None, :] * WIN
                       + np.arange(128)[:, None, None]).reshape(128, 2 * GB),
        "group_tokens": np.full((128, 2 * GB), GT),
        "power": np.tile(np.repeat([-0.5, 0.5], GB), (128, 1)),
    }
    out = np.zeros((128, CONST_COLS), f)
    for name, a in parts.items():
        out[:a.shape[0], CONST[name][0]:CONST[name][0] + a.shape[1]] = a
    return out


def kernel(x, L0_tok_W, L0_tok_b, L0_tok_gamma, L0_tok_beta, L0_attn_gamma, L0_attn_w_qkv, L0_attn_b_qkv, L0_attn_w_a,
           L0_attn_b_a, L0_attn_w_out, L0_attn_b_out, L0_ffn_router_w, L0_ffn_router_b, L0_ffn_w1, L0_ffn_b1, L0_ffn_w2, L0_ffn_b2):
    import numpy as np
    import concourse.bacc as bacc
    from concourse.bass_utils import run_bass_kernel_spmd

    def repeated(a, n):
        return np.broadcast_to(np.asarray(a).reshape(1, -1), (n, np.asarray(a).size))

    def columns(a):
        return np.asarray(a).reshape(-1, 128).T

    used = np.asarray(x)[:, :CELLS * STRIDE].reshape(GROUPS, GB, CELLS, STRIDE, D)
    rows = np.zeros((WIN, ROWS_COLS), np.float32)
    for name, a in (("gamma", L0_tok_gamma), ("beta", L0_tok_beta), ("b_out", L0_attn_b_out),
                    ("b_v", np.asarray(L0_attn_b_qkv)[2 * INNER:]), ("router_b", np.tile(L0_ffn_router_b, GB))):
        rows[:, ROWS[name][0]:ROWS[name][0] + ROWS[name][1]] = repeated(a, WIN)
    cols = np.zeros((128, COLS_COLS), np.float32)
    for name, a in (("tok_b", columns(L0_tok_b)), ("attn_gamma", columns(L0_attn_gamma)),
                    ("b_q", columns(np.asarray(L0_attn_b_qkv)[:INNER])), ("b_k", columns(np.asarray(L0_attn_b_qkv)[INNER:2 * INNER])),
                    ("b_a", columns(L0_attn_b_a)), ("b1", columns(L0_ffn_b1)), ("router_w", np.asarray(L0_ffn_router_w).T)):
        cols[:, COLS[name][0]:COLS[name][0] + COLS[name][1]] = a
    arrays = {
        "x_dram": used.transpose(0, 4, 3, 1, 2).reshape(GROUPS, D, STRIDE * GB * CELLS),
        "tok_w_dram": np.asarray(L0_tok_W).reshape(TOKEN_SIZE, D, D).transpose(1, 0, 2).reshape(D, TOKEN_SIZE * D),
        "proj_w_dram": np.concatenate([np.asarray(L0_attn_w_qkv), np.asarray(L0_attn_w_a)], axis=1),
        "out_w_dram": np.asarray(L0_attn_w_out).reshape(CHUNKS, 128, D).transpose(1, 0, 2).reshape(128, CHUNKS * D),
        "w1_dram": np.asarray(L0_ffn_w1).transpose(2, 0, 1).reshape(D, EXPERTS * FF),
        "w2_dram": np.asarray(L0_ffn_w2).reshape(EXPERTS, D, FFC, 128).transpose(3, 0, 2, 1).reshape(128, EXPERTS * FF),
        "b2_dram": repeated(L0_ffn_b2, 128),
        "consts_dram": shape_constants(np),
        "rows_dram": rows,
        "cols_dram": cols,
        "block_nos_dram": np.repeat(np.arange(BLOCKS), EXPERTS).reshape(1, BLOCKS, EXPERTS).astype(np.float32),
    }
    arrays = {name: np.ascontiguousarray(a) for name, a in arrays.items()}
    nc = bacc.Bacc("TRN2", target_bir_lowering=False, num_devices=1)
    args = [nc.dram_tensor(name, a.shape, mybir.dt.from_np(a.dtype), kind="ExternalInput").ap() for name, a in arrays.items()]
    out = nc.dram_tensor("out_dram", (BATCH, WIN, D), F32, kind="ExternalOutput").ap()
    build(nc, *args, out)
    got = run_bass_kernel_spmd(nc, [arrays], core_ids=[0])
    return got.results[0]["out_dram"]
```

```python
from contextlib import ExitStack

import concourse.bass as bass
from concourse import mybir

F32 = mybir.dt.float32
F32R = mybir.dt.float32r
U32 = mybir.dt.uint32
I32 = mybir.dt.int32
ALU = mybir.AluOpType
ACT = mybir.ActivationFunctionType
AX_X = mybir.AxisListType.X

BATCH, SEQ, D = 32, 750, 128
TOKEN_SIZE, STRIDE = 16, 8
WIN = (SEQ - TOKEN_SIZE) // STRIDE + 1
CELLS = WIN + TOKEN_SIZE // STRIDE - 1
HALVES = TOKEN_SIZE // STRIDE
HEADS, DH = 8, 64
INNER = HEADS * DH
CHUNKS = INNER // 128
EXPERTS, FF = 16, 512
FFC = FF // 128
TOKENS = BATCH * WIN

GB = 4
GROUPS = BATCH // GB
GT = GB * WIN

BLOCK = 128
CAP = TOKENS + BLOCK
CAP += -CAP % BLOCK
BLOCKS = (2 * TOKENS + EXPERTS * (BLOCK - 1)) // BLOCK
DUMMY = EXPERTS * CAP
ROW = D + 2
NO_ROW = 2 * TOKENS
PACKED = 6
TABLE = BLOCKS + 2 * PACKED

EPS = 1e-5
LOG_CAP = 87.3
SCALE = DH ** -0.5

CONST = {}
CONST_COLS = 0
for _name, _n in (("ident", 128), ("causal", GT), ("before", WIN), ("ones", WIN), ("log_cap", GB * (WIN + 1)),
                  ("first_row", GB * EXPERTS), ("expert", GB * EXPERTS), ("result_row", 2 * GB),
                  ("group_tokens", 2 * GB), ("power", 8)):
    CONST[_name] = (CONST_COLS, _n)
    CONST_COLS += _n

ROWS = {}
ROWS_COLS = 0
for _name, _n in (("gamma", D), ("beta", D), ("b_out", D), ("b_v", INNER), ("router_b", GB * EXPERTS)):
    ROWS[_name] = (ROWS_COLS, _n)
    ROWS_COLS += _n

COLS = {}
COLS_COLS = 0
for _name, _n in (("tok_b", 1), ("attn_gamma", 1), ("b_q", CHUNKS), ("b_k", CHUNKS), ("b_a", CHUNKS),
                  ("b1", EXPERTS * FFC), ("router_w", EXPERTS)):
    COLS[_name] = (COLS_COLS, _n)
    COLS_COLS += _n

SLOTS = 12
OUT_STEPS = 8
POOL_OUT = (2, 5)
BOTH, FIRST, SECOND = 0, 1, 2
WEIGHT_PARTS = GROUPS // 2
PARTS = 4
OB = BATCH // OUT_STEPS
X_SPLIT = GB * CELLS


def at(n, size=1):
    return bass.ds(n, size) if not isinstance(n, int) else slice(n, n + size)


def build(nc, x, tok_w, proj_w, out_w, w1, w2, b2, consts, rows, cols, block_nos, out):
    ctx = ExitStack()
    phase_1 = ExitStack()
    phase_2 = ExitStack()
    phase_3 = ExitStack()

    def sb(name, shape, dt=F32, stack=ctx):
        return stack.enter_context(nc.sbuf_tensor(name, shape, dt))

    def sem(name):
        return ctx.enter_context(nc.semaphore(name))

    with ctx:
        const = sb("const", [128, CONST_COLS])
        row = sb("row", [WIN, ROWS_COLS])
        col = sb("col", [128, COLS_COLS])

        def const_of(name, p=128):
            a, n = CONST[name]
            return const[0:p, a:a + n]

        def row_of(name):
            a, n = ROWS[name]
            return row[:, a:a + n]

        def col_of(name, i=0):
            return col[:, COLS[name][0] + i:COLS[name][0] + i + 1]

        ident = const_of("ident")
        neg_b_a = sb("neg_b_a", [128, CHUNKS])
        pw_hi = sb("pw_hi", [128, 4 * INNER], F32R)
        pw_lo = sb("pw_lo", [128, 4 * INNER], F32R)
        xsT_hi = sb("xsT_hi", [128, TOKENS], F32R)
        xsT_lo = sb("xsT_lo", [128, TOKENS], F32R)
        h_all = sb("h_all", [WIN, BATCH * D])
        pad = sb("pad", [128, ROW])
        running = sb("running", [WIN, GB + 1, EXPERTS])

        XG = STRIDE * GB * CELLS
        geluT = [sb(f"geluT{u}", [128, GT], stack=phase_1) for u in range(2)]
        normed = [sb(f"normed{u}", [WIN, GB * D], stack=phase_1) for u in range(2)]
        scaled = sb("scaled", [WIN, GB * D], stack=phase_1)
        xs = [sb(f"xs{u}", [WIN, GB * D], stack=phase_1) for u in range(2)]
        stat1 = sb("stat1", [WIN, GB, 6], stack=phase_1)
        mv1 = sb("mv1", [WIN, GB, 2], stack=phase_1)
        var1 = sb("var1", [WIN, GB], stack=phase_1)
        neg_mean1 = sb("neg_mean1", [WIN, GB], stack=phase_1)
        rstd1 = sb("rstd1", [WIN, GB], stack=phase_1)
        shift1 = sb("shift1", [WIN, GB], stack=phase_1)
        stat2 = sb("stat2", [WIN, GB, 6], stack=phase_1)
        mv2 = sb("mv2", [WIN, 2, GB, 2], stack=phase_1)
        base2 = sb("base2", [WIN, 2 * GB], stack=phase_1)
        root2 = sb("root2", [WIN, 2 * GB], stack=phase_1)
        norm2 = sb("norm2", [WIN, 3, GB], stack=phase_1)
        scale2 = sb("scale2", [WIN, GB], stack=phase_1)
        x_raw = [sb(f"x_raw{u}", [128, XG], stack=phase_1) for u in range(2)]
        x_hi = [sb(f"x_hi{u}", [128, XG], F32R, phase_1) for u in range(2)]
        x_lo = [sb(f"x_lo{u}", [128, XG], F32R, phase_1) for u in range(2)]
        tw_raw = sb("tw_raw", [128, TOKEN_SIZE * D], stack=phase_1)
        tw_hi = sb("tw_hi", [128, TOKEN_SIZE * D], F32R, phase_1)
        tw_lo = sb("tw_lo", [128, TOKEN_SIZE * D], F32R, phase_1)
        pw_raw = sb("pw_raw", [128, 4 * INNER], stack=phase_1)
        phase_1.close()

        w1_all = sb("w1_all", [128, EXPERTS * FF])
        w2_all = sb("w2_all", [128, EXPERTS * FF])
        b2_all = sb("b2_all", [128, EXPERTS * D])

        ow = sb("ow", [128, CHUNKS * D], stack=phase_2)
        growth = [sb(f"growth{u}", [128, GT], stack=phase_2) for u in range(2)]
        log_growth = sb("log_growth", [128, GB, WIN + 1], stack=phase_2)
        log_sum = sb("log_sum", [128, GB, WIN + 1], stack=phase_2)
        a_cum = [sb(f"a_cum{u}", [128, GB, WIN], stack=phase_2) for u in range(2)]
        a_inv = [sb(f"a_inv{u}", [128, GB, WIN], stack=phase_2) for u in range(2)]
        kb = [sb(f"kb{u}", [128, GT], stack=phase_2) for u in range(2)]
        qT = [sb(f"qT{u}", [128, GT], stack=phase_2) for u in range(2)]
        kT = [sb(f"kT{u}", [128, GT], stack=phase_2) for u in range(2)]
        attnT = [sb(f"attnT{u}", [WIN, 2, GT], stack=phase_2) for u in range(2)]
        xv_hi = [sb(f"xv_hi{u}", [128, GT], F32R, phase_2) for u in range(2)]
        xv_lo = [sb(f"xv_lo{u}", [128, GT], F32R, phase_2) for u in range(2)]
        v = [sb(f"v{u}", [WIN, GB, INNER], stack=phase_2) for u in range(2)]
        oT = [sb(f"oT{c}", [128, GT], stack=phase_2) for c in range(CHUNKS)]
        stat3 = sb("stat3", [WIN, GB, 6], stack=phase_2)
        mv3 = sb("mv3", [WIN, GB, 2], stack=phase_2)
        var3 = sb("var3", [WIN, GB], stack=phase_2)
        rstd3 = sb("rstd3", [WIN, GB], stack=phase_2)
        neg_mean3 = sb("neg_mean3", [WIN, GB], stack=phase_2)
        shift3 = sb("shift3", [WIN, GB], stack=phase_2)
        counts = sb("counts", [WIN, 2, GB, EXPERTS], stack=phase_2)
        xm = [sb(f"xm{u}", [WIN, 2, GB, ROW], stack=phase_2) for u in range(2)]
        xmT = sb("xmT", [128, GT], stack=phase_2)
        logits = sb("logits", [WIN, GB, EXPERTS], stack=phase_2)
        top_logit = sb("top_logit", [WIN, GB], stack=phase_2)
        shifted = sb("shifted", [WIN, GB, EXPERTS], stack=phase_2)
        expd = sb("expd", [WIN, GB, EXPERTS], stack=phase_2)
        exp_sum = sb("exp_sum", [WIN, GB], stack=phase_2)
        exp_rec = sb("exp_rec", [WIN, GB], stack=phase_2)
        probs = sb("probs", [WIN, GB, EXPERTS], stack=phase_2)
        top8 = sb("top8", [WIN, GB, 8], stack=phase_2)
        top8_at = sb("top8_at", [WIN, GB, 8], U32, phase_2)
        top8_atf = sb("top8_atf", [WIN, GB, 8], stack=phase_2)
        chosen = sb("chosen", [WIN, 2, GB, EXPERTS], stack=phase_2)
        both = sb("both", [WIN, GB, EXPERTS], stack=phase_2)
        rank = sb("rank", [WIN, GB, EXPERTS], stack=phase_2)
        ranked = sb("ranked", [WIN, GB, EXPERTS], stack=phase_2)
        place = sb("place", [WIN, 2, GB, EXPERTS], stack=phase_2)
        place_8 = sb("place_8", [WIN, 2 * GB, 8], stack=phase_2)
        place_4 = sb("place_4", [WIN, 2 * GB, 4], stack=phase_2)
        place_2 = sb("place_2", [WIN, 2 * GB, 2], stack=phase_2)
        place_f = sb("place_f", [WIN, 2 * GB], stack=phase_2)
        place_u = [sb(f"place_u{u}", [WIN, 2 * GB], U32, phase_2) for u in range(2)]
        phase_2.close()

        n_int = sb("n_int", [1, EXPERTS], I32, phase_3)
        tail_at = sb("tail_at", [1, EXPERTS], I32, phase_3)
        tail_f = sb("tail_f", [1, EXPERTS], stack=phase_3)
        nb_int = sb("nb_int", [1, EXPERTS], I32, phase_3)
        nb_f = sb("nb_f", [1, EXPERTS], stack=phase_3)
        zero16 = sb("zero16", [1, EXPERTS], stack=phase_3)
        nb_end = sb("nb_end", [1, EXPERTS], stack=phase_3)
        block_no = sb("block_no", [1, TABLE, EXPERTS], stack=phase_3)
        past = sb("past", [1, TABLE, EXPERTS], stack=phase_3)
        blk_e = sb("blk_e", [1, TABLE], stack=phase_3)
        blk_s = sb("blk_s", [1, TABLE], stack=phase_3)
        blk_r = sb("blk_r", [1, TABLE], stack=phase_3)
        blk_q = sb("blk_q", [1, TABLE], stack=phase_3)
        blk_t = sb("blk_t", [1, TABLE], stack=phase_3)
        blk_expert = sb("blk_expert", [1, TABLE], stack=phase_3)
        expert_pairs = sb("expert_pairs", [1, TABLE], stack=phase_3)
        expert_fours = sb("expert_fours", [1, TABLE], stack=phase_3)
        packed = sb("packed", [1, BLOCKS], I32, phase_3)
        blk_row = sb("blk_row", [1, TABLE], I32, phase_3)
        xb = [sb(f"xb{u}", [128, ROW], stack=phase_3) for u in range(SLOTS)]
        xbT = [sb(f"xbT{u}", [128, BLOCK], stack=phase_3) for u in range(2)]
        w1_blk = [sb(f"w1_blk{u}", [128, FF], stack=phase_3) for u in range(2)]
        hT = [sb(f"hT{u}", [128, FFC, BLOCK], stack=phase_3) for u in range(2)]
        yb = [sb(f"yb{u}", [128, D], stack=phase_3) for u in range(2)]
        yg = [sb(f"yg{u}", [128, D], stack=phase_3) for u in range(SLOTS)]
        y1 = [sb(f"y1_{k}", [WIN, OB, D], stack=phase_3) for k in range(OUT_STEPS)]
        y2 = [sb(f"y2_{k}", [WIN, OB, D], stack=phase_3) for k in range(OUT_STEPS)]
        phase_3.close()

        bank = [ctx.enter_context(nc.psum_tensor(f"bank{i}", [128, 512], F32)) for i in range(8)]

        sorted_rows = nc.dram_tensor("sorted_rows", (DUMMY + BLOCK, ROW), F32).ap()
        results = nc.dram_tensor("results", (2 * TOKENS, D), F32).ap()

        const_in = sem("const_in")
        x_in1 = sem("x_in1")
        pw_in = sem("pw_in")
        part_done = sem("part_done")
        x_in0 = sem("x_in0")
        lo_v_done = sem("lo_v_done")
        lo_p_done = sem("lo_p_done")
        main_done = sem("main_done")
        pw_done = sem("pw_done")
        xsT_done = sem("xsT_done")
        ow_in = sem("ow_in")
        experts_in = sem("experts_in")
        v_done = sem("v_done")
        proj_done = sem("proj_done")
        block_no_in = sem("block_no_in")
        tail_done = sem("tail_done")
        table_done = sem("table_done")
        scattered0 = sem("scattered0")
        scattered1 = sem("scattered1")
        out_done = sem("out_done")
        gelu_done = sem("gelu_done")
        normed_done = sem("normed_done")
        t1_done = sem("t1_done")
        xs_done = sem("xs_done")
        t2_done = sem("t2_done")
        a_done = sem("a_done")
        e_done = sem("e_done")
        xv_in0 = sem("xv_in0")
        vT_done = sem("vT_done")
        both_done = sem("both_done")
        oT_done = sem("oT_done")
        prefix_ps = sem("prefix_ps")
        qT_done = sem("qT_done")
        xmT_done = sem("xmT_done")
        router_ps = sem("router_ps")
        logits_done = sem("logits_done")
        q_done = sem("q_done")
        kb_done = sem("kb_done")
        k_done = sem("k_done")
        kT_done = sem("kT_done")
        attn_done = sem("attn_done")
        sim_done = sem("sim_done")
        xm_done = sem("xm_done")
        h2_done = sem("h2_done")
        xmT_ps = sem("xmT_ps")
        av_done = sem("av_done")
        counts_done = sem("counts_done")
        xT_ps = sem("xT_ps")
        packed_done = sem("packed_done")
        xT_done = sem("xT_done")
        w1_done = sem("w1_done")
        hidden_ps = sem("hidden_ps")
        hidden_done = sem("hidden_done")
        yb_done = sem("yb_done")
        y_ps = sem("y_ps")
        hi_done = sem("hi_done")
        part_hi_done = sem("part_hi_done")
        pw_scaled = sem("pw_scaled")
        pw_hi_done = sem("pw_hi_done")
        neg_b_done = sem("neg_b_done")
        log_start_done = sem("log_start_done")
        shift1_done = sem("shift1_done")
        h_done = sem("h_done")
        xsT_hi_done = sem("xsT_hi_done")
        log_done = sem("log_done")
        clip_done = sem("clip_done")
        scan_done = sem("scan_done")
        cum_done = sem("cum_done")
        inv_done = sem("inv_done")
        shift3_done = sem("shift3_done")
        shifted_done = sem("shifted_done")
        exp_done = sem("exp_done")
        xm_twice = sem("xm_twice")
        pad_done = sem("pad_done")
        running_done = sem("running_done")
        stat1_done = sem("stat1_done")
        mv1_done = sem("mv1_done")
        var1_done = sem("var1_done")
        stat2_done = sem("stat2_done")
        mv2_done = sem("mv2_done")
        base2_done = sem("base2_done")
        root2_done = sem("root2_done")
        length_done = sem("length_done")
        guarded_done = sem("guarded_done")
        inverse_done = sem("inverse_done")
        scale2_done = sem("scale2_done")
        placed_done = sem("placed_done")
        hb_done = sem("hb_done")
        stat3_done = sem("stat3_done")
        dve_go = sem("dve_go")
        mv3_done = sem("mv3_done")
        var3_done = sem("var3_done")
        top_logit_done = sem("top_logit_done")
        sum_done = sem("sum_done")
        rec_done = sem("rec_done")
        probs_done = sem("probs_done")
        top8_done = sem("top8_done")
        top8_at_done = sem("top8_at_done")
        gates_done = sem("gates_done")
        top8_atf_done = sem("top8_atf_done")
        place_done = sem("place_done")
        chosen_done = sem("chosen_done")
        table_step = sem("table_step")
        yg_done = sem("yg_done")
        rstd1_done = sem("rstd1_done")
        scaled_done = sem("scaled_done")
        pool_go = sem("pool_go")
        dest_done = sem("dest_done")
        rstd3_done = sem("rstd3_done")
        tail_f_done = sem("tail_f_done")
        tails_out0 = sem("tails_out0")
        tails_out1 = sem("tails_out1")
        xv_in1 = sem("xv_in1")
        rank_done = sem("rank_done")
        ranked_done = sem("ranked_done")
        place_8_done = sem("place_8_done")
        place_4_done = sem("place_4_done")
        place_2_done = sem("place_2_done")
        place_f_done = sem("place_f_done")
        x_in = (x_in0, x_in1)
        part_in = [sem(f"part_in{k}") for k in range(PARTS)]
        tails_out = (tails_out0, tails_out1)
        scattered = (scattered0, scattered1)
        xv_in = (xv_in0, xv_in1)
        xb_in = [sem(f"xb_in{u}") for u in range(SLOTS)]
        y_out = [sem(f"y_out{u}") for u in range(SLOTS)]
        y_in = [sem(f"y_in{k}") for k in range(OUT_STEPS)]
        summed_dve = sem("summed_dve")
        summed_pool = sem("summed_pool")

        ident_w = const[0:WIN, CONST["ident"][0]:CONST["ident"][0] + WIN]
        causal = const_of("causal", WIN)
        power = const_of("power", WIN)
        result_row = const_of("result_row", WIN).rearrange("p (t b) -> p t b", t=2)
        group_tokens = const_of("group_tokens", WIN).rearrange("p (t b) -> p t b", t=2)
        expert_no = const_of("expert", WIN).rearrange("p (b e) -> p b e", b=GB)
        first_row = const_of("first_row", WIN).rearrange("p (b e) -> p b e", b=GB)
        b_a = col[:, COLS["b_a"][0]:COLS["b_a"][0] + CHUNKS]
        b1_all = col[:, COLS["b1"][0]:COLS["b1"][0] + EXPERTS * FFC]
        router_w = col[:, COLS["router_w"][0]:COLS["router_w"][0] + EXPERTS]

        def w_part(k):
            n = TOKEN_SIZE * D // PARTS
            return slice(k * n, (k + 1) * n)

        def x_part(k):
            n = XG // PARTS
            return slice(k * n, (k + 1) * n)

        def pad_tails(eng, half):
            for e in range(half, EXPERTS, 2):
                start = eng.value_load(tail_at[0:1, e:e + 1], min_val=e * CAP, max_val=e * CAP + TOKENS)
                eng.dma_start(sorted_rows[bass.ds(start, BLOCK), :], pad[:]).then_inc(tails_out[half], 16)

        def sort_group(eng, g, u):
            eng.wait_ge(counts_done, g - 2)
            eng.wait_ge(running_done, (g - 3) * (GB + 1) + 1)
            if eng is nc.gpsimd:
                eng.sem_inc(pool_go, 1)
            eng.tensor_copy(running[:, 0, :], running[:, GB, :]).then_inc(running_done, 1)
            for b in range(GB):
                eng.wait_ge(running_done, (g - 3) * (GB + 1) + 2 + b)
                eng.tensor_tensor(running[:, b + 1, :], counts[:, 1, b, :], running[:, b, :], ALU.add).then_inc(running_done, 1)
            eng.tensor_tensor(rank[:], counts[:, 0], running[:, 0:GB, :], ALU.add).then_inc(rank_done, 1)
            eng.wait_ge(rank_done, g - 2)
            eng.tensor_tensor(ranked[:], rank[:], first_row, ALU.add).then_inc(ranked_done, 1)
            eng.wait_ge(ranked_done, g - 2)
            for t in range(2):
                ins = eng.tensor_tensor(place[:, t], chosen[:, t], ranked[:], ALU.mult)
            ins.then_inc(place_done, 1)
            eng.wait_ge(place_done, g - 1)
            p = place[:].rearrange("p t b e -> p (t b) e")
            eng.tensor_tensor(place_8[:], p[:, :, 0:8], p[:, :, 8:16], ALU.add).then_inc(place_8_done, 1)
            eng.wait_ge(place_8_done, g - 2)
            eng.tensor_tensor(place_4[:], place_8[:, :, 0:4], place_8[:, :, 4:8], ALU.add).then_inc(place_4_done, 1)
            eng.wait_ge(place_4_done, g - 2)
            eng.tensor_tensor(place_2[:], place_4[:, :, 0:2], place_4[:, :, 2:4], ALU.add).then_inc(place_2_done, 1)
            eng.wait_ge(place_2_done, g - 2)
            eng.tensor_tensor(place_f[:], place_2[:, :, 0], place_2[:, :, 1], ALU.add).then_inc(place_f_done, 1)
            eng.wait_ge(place_f_done, g - 2)
            if eng is nc.gpsimd:
                eng.sem_inc(pool_go, 1)
            eng.tensor_copy(place_u[1 - u][:], place_f[:]).then_inc(placed_done, 1)

        def turned(role):
            return bank[3] if role < GROUPS else bank[4]

        def load_results(eng, t):
            for k in range(OUT_STEPS):
                a = t * TOKENS + k * OB * WIN
                y = (y1, y2)[t][k]
                eng.dma_start(y[:], results[a:a + OB * WIN, :].rearrange("(b i) d -> i b d", i=WIN)).then_inc(y_in[k], 16)

        def summed_by(k):
            if k in POOL_OUT:
                return summed_pool, POOL_OUT.index(k)
            return summed_dve, [i for i in range(OUT_STEPS) if i not in POOL_OUT].index(k)

        def add_results(eng, k):
            eng.wait_ge(y_in[k], 32)
            h = h_all[:, k * OB * D:(k + 1) * OB * D]
            f1, f2 = (y[k][:].rearrange("p b d -> p (b d)") for y in (y1, y2))
            summed, order = summed_by(k)
            eng.tensor_tensor(f1, f1, f2, ALU.add).then_inc(summed, 1)
            eng.wait_ge(summed, order * 2 + 1)
            eng.tensor_tensor(f1, f1, h, ALU.add).then_inc(summed, 1)

        def store_out(eng, half):
            for k in range(half, OUT_STEPS, 2):
                summed, order = summed_by(k)
                eng.wait_ge(summed, order * 2 + 2)
                eng.dma_start(out[k * OB:(k + 1) * OB].rearrange("b i d -> i b d"), y1[k][:]).then_inc(out_done, 16)

        def by_row(a):
            return a.rearrange("p (b d) -> p b d", b=GB)

        def each_row(name):
            return row_of(name).unsqueeze(1).to_broadcast([WIN, GB, D])

        def spread(a):
            return a.unsqueeze(2).to_broadcast([WIN, GB, EXPERTS])

        block = ctx.enter_context(nc.Block())

        def tokenizer_and_attention(eng, step, start, unit):
            for g in range(3):
                step(g, g % 2, g)
            with eng.Fori(0, 2) as i:
                for k in range(2):
                    step(i * 2 + 3 + k, (3 + k) % 2, 3)
            for g in range(7, GROUPS + 1):
                step(g, g % 2, g)
            start()
            step(GROUPS + 1, (GROUPS + 1) % 2, GROUPS + 1, FIRST)
            unit(0, 0, 0, 0)
            step(GROUPS + 1, (GROUPS + 1) % 2, GROUPS + 1, SECOND)
            unit(0, 0, 0, 1)
            step(GROUPS + 2, (GROUPS + 2) % 2, GROUPS + 2)
            for c in range(2, CHUNKS):
                unit(0, 0, 0, c)
            for g in range(1, 3):
                for c in range(CHUNKS):
                    unit(g, g % 2, g, c)
            with eng.Fori(0, 2) as i:
                for k in range(2):
                    for c in range(CHUNKS):
                        unit(i * 2 + 3 + k, (3 + k) % 2, 3, c)
            for g in range(7, GROUPS + 3):
                for c in range(CHUNKS):
                    unit(g, g % 2, g, c)

        def expert_steps(eng, step, run, first):
            def steps(j, slot, turn, role):
                word = None
                back = min(first, role)
                if eng is not nc.gpsimd:
                    word = eng.value_load(packed[0:1, at(j - back)], min_val=0, max_val=EXPERTS ** PACKED - 1)

                def expert(i):
                    return word // EXPERTS ** (i + back) % EXPERTS

                for k in range(2 if role == 0 else run):
                    step(j + k, (slot + k) % SLOTS, turn + (slot + k) // SLOTS, role if role == 2 else j + k,
                         lambda lag: expert(k - lag))

            steps(0, 0, 0, 0)
            loops = (BLOCKS - 3) // SLOTS
            with eng.Fori(0, loops) as i:
                for k in range(0, SLOTS, run):
                    steps(i * SLOTS + 2 + k, (2 + k) % SLOTS, i + (2 + k) // SLOTS, 2)
            for j in range(loops * SLOTS + 2, BLOCKS + 1, run):
                steps(j, j % SLOTS, j // SLOTS, j)

        def has_group(role, lag):
            return 0 <= role - lag < GROUPS

        def has_unit(role, c, lag):
            return 0 <= CHUNKS * role + c - lag < CHUNKS * GROUPS

        def has_block(role, lag):
            return 0 <= role - lag < BLOCKS
        @block.sync
        def _(sp):
            for k in range(PARTS):
                sp.dma_start(tw_raw[:, w_part(k)], tok_w[:, w_part(k)]).then_inc(part_in[k], 16)
                sp.dma_start(x_raw[0][:, x_part(k)], x[0, :, x_part(k)]).then_inc(part_in[k], 16)
                if k == 1:
                    sp.dma_start(col[:], cols).then_inc(const_in, 16)
            sp.dma_start(x_raw[1][:], x[1]).then_inc(x_in1, 16)
            sp.dma_start(const[:], consts).then_inc(const_in, 16)
            sp.dma_start(row[:], rows).then_inc(const_in, 16)
            sp.dma_start(pw_raw[:], proj_w).then_inc(pw_in, 16)
            sp.wait_ge(part_done, PARTS)
            sp.dma_start(x_raw[0][:], x[2]).then_inc(x_in0, 16)
            sp.wait_ge(lo_v_done, 1)
            sp.wait_ge(lo_p_done, 1)
            sp.dma_start(x_raw[1][:], x[3]).then_inc(x_in1, 16)
            with sp.Fori(1, GROUPS // 2 - 1) as i:
                for u in range(2):
                    sp.wait_ge(lo_v_done, i * 2 + u)
                    sp.wait_ge(lo_p_done, i * 2 + u)
                    sp.dma_start(x_raw[u][:], x[at(i * 2 + 2 + u), :, :].rearrange("a p n -> (a p) n")).then_inc(x_in[u], 16)

            def stage_v(g, u):
                t = at(g * GT, GT)
                sp.dma_start(xv_hi[u][:].bitcast(F32), xsT_hi[:, t].bitcast(F32)).then_inc(xv_in[u], 16)
                sp.dma_start(xv_lo[u][:].bitcast(F32), xsT_lo[:, t].bitcast(F32)).then_inc(xv_in[u], 16)

            sp.wait_ge(main_done, GROUPS)
            sp.wait_ge(pw_done, 1)
            sp.wait_ge(xsT_done, 2)
            for g in range(2):
                stage_v(g, g)
            sp.dma_start(ow[:], out_w).then_inc(ow_in, 16)
            sp.wait_ge(xsT_done, GROUPS)
            part = EXPERTS * FF // WEIGHT_PARTS
            sp.dma_start(b2_all[:], b2).then_inc(experts_in, 16)
            sp.dma_start(w1_all[:, 0:part], w1[:, 0:part]).then_inc(experts_in, 16)
            sp.dma_start(w2_all[:, 0:part], w2[:, 0:part]).then_inc(experts_in, 16)
            with sp.Fori(0, GROUPS // 2 - 1) as i:
                for u in range(2):
                    sp.wait_ge(v_done, i * (2 * GB) + (u + 1) * GB)
                    stage_v(i * 2 + 2 + u, u)
                    w, w_dram = (w1_all, w1) if u == 0 else (w2_all, w2)
                    sp.dma_start(w[:, at((i + 1) * part, part)], w_dram[:, at((i + 1) * part, part)]).then_inc(experts_in, 16)
            sp.wait_ge(proj_done, GROUPS)
            sp.dma_start(block_no[:], block_nos).then_inc(block_no_in, 16)
            sp.wait_ge(tail_done, 1)
            pad_tails(sp, 0)
            sp.wait_ge(table_done, 1)
            first_row_read = sp.value_load(blk_row[0:1, 0:1], min_val=0, max_val=DUMMY)
            sp.wait_ge(scattered0, GROUPS * GB * 16 + 16)
            sp.wait_ge(scattered1, GROUPS * GB * 16 + 16)
            for half in range(2):
                sp.wait_ge(tails_out[half], EXPERTS // 2 * 16)

            def load_block(j, slot):
                start = sp.value_load(blk_row[0:1, at(j)], min_val=0, max_val=DUMMY)
                sp.dma_start(xb[slot][:], sorted_rows[bass.ds(start, BLOCK), :]).then_inc(xb_in[slot], 16)

            sp.dma_start(xb[0][:], sorted_rows[bass.ds(first_row_read, BLOCK), :]).then_inc(xb_in[0], 16)
            for j in range(1, SLOTS):
                load_block(j, j)
            rounds = BLOCKS // SLOTS - 1
            with sp.Fori(0, rounds) as i:
                for k in range(SLOTS):
                    sp.wait_ge(y_out[k], i * 16 + 16)
                    load_block(i * SLOTS + SLOTS + k, k)
            for j in range((rounds + 1) * SLOTS, BLOCKS):
                sp.wait_ge(y_out[j % SLOTS], j // SLOTS * 16)
                load_block(j, j % SLOTS)
            for u in range(SLOTS):
                sp.wait_ge(y_out[u], 16 * len(range(u, BLOCKS, SLOTS)))
            load_results(sp, 0)
            store_out(sp, 0)
            sp.wait_ge(out_done, 16 * OUT_STEPS)

        @block.tensor
        def _(pe):
            def split_matmul(dst, w_hi, w_lo, m_hi, m_lo, first, last):
                pe.matmul(dst, w_hi, m_hi, start=first, stop=False)
                pe.matmul(dst, w_hi, m_lo, start=False, stop=False)
                return pe.matmul(dst, w_lo, m_hi, start=False, stop=last)

            def step(g, u, role, part=BOTH):
                def windows(t, r, half):
                    return t[:].rearrange("p (r b n) -> p r b n", r=STRIDE, b=GB)[:, r, :, half:half + WIN]

                def main(r0, r1):
                    for r in range(r0, r1):
                        for half in range(HALVES):
                            w = slice((r * HALVES + half) * D, (r * HALVES + half + 1) * D)
                            mm = split_matmul(bank[u][:, 0:GT], tw_hi[:, w], tw_lo[:, w], windows(x_hi[u], r, half),
                                              windows(x_lo[u], r, half), r == 0 and half == 0,
                                              r == STRIDE - 1 and half == HALVES - 1)
                    return mm

                if has_group(role, 0):
                    if role == 0:
                        for k in range(PARTS - 1):
                            pe.wait_ge(part_done, k + 1)
                            main(k * STRIDE // PARTS, (k + 1) * STRIDE // PARTS)
                        pe.wait_ge(part_done, PARTS)
                        main(STRIDE - STRIDE // PARTS, STRIDE).then_inc(main_done, 1)
                        return
                    pe.wait_ge(lo_v_done, g)
                    pe.wait_ge(lo_p_done, g)
                    if has_group(role, 2):
                        pe.wait_ge(gelu_done, g - 1)
                    main(0, 2)
                if has_group(role, 1):
                    pe.wait_ge(gelu_done, g)
                    if role == 1:
                        pe.wait_ge(const_in, 48)
                    if has_group(role, 2):
                        pe.wait_ge(normed_done, g - 1)
                    for b in range(GB):
                        mm = pe.transpose(bank[2][0:WIN, b * D:(b + 1) * D], geluT[1 - u][:, b * WIN:(b + 1) * WIN], ident)
                    mm.then_inc(t1_done, 1)
                if has_group(role, 0):
                    main(2, 5)
                if has_group(role, 3) and part != SECOND:
                    pe.wait_ge(xs_done, g - 2)
                    for b in range(GB):
                        mm = pe.transpose(bank[3][:, b * WIN:(b + 1) * WIN], xs[1 - u][:, b * D:(b + 1) * D], ident_w)
                    mm.then_inc(t2_done, 1)
                if has_group(role, 0):
                    main(5, STRIDE).then_inc(main_done, 1)

            def project(dst, first_col, g):
                w = slice(first_col, first_col + 128)
                t = at(g * GT, GT)
                return split_matmul(dst[:, 0:GT], pw_hi[:, w], pw_lo[:, w], xsT_hi[:, t], xsT_lo[:, t], True, True)

            def project_a(g, c):
                project(bank[0], 3 * INNER + c * 128, g).then_inc(a_done, 1)

            def project_v(u, b):
                t = slice(b * WIN, (b + 1) * WIN)
                w = slice(2 * INNER, 3 * INNER)
                pe.matmul(bank[5][0:WIN, :], xv_hi[u][:, t], pw_hi[:, w], start=True, stop=False)
                pe.matmul(bank[5][0:WIN, :], xv_lo[u][:, t], pw_hi[:, w], start=False, stop=False)
                pe.matmul(bank[5][0:WIN, :], xv_hi[u][:, t], pw_lo[:, w], start=False, stop=True).then_inc(v_done, 1)

            def start():
                pe.wait_ge(xsT_done, 2)
                pe.wait_ge(pw_done, 1)
                project_a(0, 0)
                pe.wait_ge(e_done, 1)
                project_a(0, 1)
                pe.wait_ge(xv_in0, 32)
                project_v(0, 0)
                pe.wait_ge(vT_done, 1)
                project_v(0, 1)

            def count_choices(g, results):
                pe.wait_ge(both_done, g - 2)
                pe.wait_ge(oT_done, results)
                m = both[:].rearrange("p b e -> p (b e)")
                pe.matmul(bank[2][0:WIN, GT:GT + GB * EXPERTS], const_of("before", WIN), m, start=True, stop=True)
                pe.matmul(bank[2][0:WIN, GT + GB * EXPERTS:GT + 2 * GB * EXPERTS], const_of("ones", WIN), m, start=True,
                          stop=True).then_inc(prefix_ps, 1)

            def router(g, queries, role):
                pe.wait_ge(qT_done, queries)
                pe.wait_ge(xmT_done, g - 1)
                for b in range(GB):
                    mm = pe.matmul(bank[1][0:WIN, GT + b * EXPERTS:GT + (b + 1) * EXPERTS], xmT[:, b * WIN:(b + 1) * WIN],
                                   router_w, start=True, stop=True)
                mm.then_inc(router_ps, 1)

            def unit(g, u, role, c):
                n = g * CHUNKS + c
                if has_unit(role, c, -2):
                    pe.wait_ge(e_done, n + 2)
                    project_a(g if c + 2 < CHUNKS else g + 1, (c + 2) % CHUNKS)
                if c == 3 and role < GROUPS and has_group(role, 2):
                    router(g, n, role)
                if has_unit(role, c, 0):
                    if has_unit(role, c, 1):
                        pe.wait_ge(qT_done, n)
                    if c == 0 and has_group(role, 3):
                        pe.wait_ge(logits_done, g - 2)
                    project(bank[1], c * 128, g).then_inc(q_done, 1)
                    if has_unit(role, c, 1):
                        pe.wait_ge(kb_done, n)
                    project(bank[4], INNER + c * 128, g).then_inc(k_done, 1)
                if has_unit(role, c, 1):
                    pe.wait_ge(qT_done, n)
                    pe.wait_ge(kT_done, n)
                    if has_unit(role, c, 2):
                        pe.wait_ge(attn_done, n * 2 - 2)
                    for hd in range(2):
                        f = slice(hd * DH, (hd + 1) * DH)
                        for b in range(GB):
                            t = slice(b * WIN, (b + 1) * WIN)
                            mm = pe.matmul(bank[6 + hd][0:WIN, t], kT[(c + 1) % 2][f, t], qT[(c + 1) % 2][f, t],
                                           start=True, stop=True)
                        mm.then_inc(sim_done, 1)
                if c == 2 and has_group(role, 2):
                    pe.wait_ge(xm_done, g - 1)
                    pe.wait_ge(h2_done, g - 1)
                    if role >= GROUPS:
                        pe.wait_ge(kb_done, GROUPS * CHUNKS)
                    for b in range(GB):
                        mm = pe.transpose(turned(role)[:, b * WIN:(b + 1) * WIN], xm[u][:, 0, b, 0:D], ident_w)
                    mm.then_inc(xmT_ps, 1)
                    if role >= GROUPS:
                        router(g, GROUPS * CHUNKS, role)
                if has_unit(role, c, -2) and (c + 2) // CHUNKS + role < GROUPS:
                    pe.wait_ge(vT_done, n + 2)
                    w = u if c < 2 else 1 - u
                    if c == 2:
                        pe.wait_ge(xv_in[w], g * 16 + (48 if u else 32))
                    project_v(w, (c + 2) % CHUNKS)
                if c == 1 and role <= GROUPS and has_group(role, 3):
                    count_choices(g, n - 2)
                if has_unit(role, c, 2):
                    pe.wait_ge(attn_done, n * 2 - 2)
                    if has_unit(role, c, 3):
                        pe.wait_ge(oT_done, n - 2)
                    if c == 2:
                        pe.wait_ge(vT_done, (g + 1) * GB)
                    w = u if c >= 2 else 1 - u
                    for hd in range(2):
                        h0 = (2 * ((c + 2) % CHUNKS) + hd) * DH
                        for b in range(GB):
                            t = slice(b * WIN, (b + 1) * WIN)
                            mm = pe.matmul(bank[2][hd * DH:(hd + 1) * DH, t], v[w][:, b, h0:h0 + DH],
                                           attnT[c % 2][:, hd, t], start=True, stop=True)
                    mm.then_inc(av_done, 1)
                if c == 2 and has_group(role, 1):
                    pe.wait_ge(oT_done, g * CHUNKS)
                    if has_group(role, 2):
                        pe.wait_ge(xmT_done, g - 1)
                    if role == 1:
                        pe.wait_ge(ow_in, 16)
                    for b in range(GB):
                        for k in range(CHUNKS):
                            mm = pe.matmul(bank[3][0:WIN, b * D:(b + 1) * D], oT[k][:, b * WIN:(b + 1) * WIN],
                                           ow[:, k * D:(k + 1) * D], start=k == 0, stop=k == CHUNKS - 1)
                    mm.then_inc(proj_done, 1)
                if c == 3 and role >= GROUPS and has_group(role, 2):
                    pe.wait_ge(counts_done, g - 2)
                    count_choices(g + 1, GROUPS * CHUNKS)

            tokenizer_and_attention(pe, step, start, unit)

            def turn_block(j, slot):
                pe.transpose(bank[slot % 2][:, 0:BLOCK], xb[slot][:, 0:D], ident).then_inc(xT_ps, 1)

            pe.wait_ge(xb_in[0], 16)
            pe.wait_ge(packed_done, 1)
            turn_block(0, 0)
            pe.wait_ge(experts_in, 16 + 2 * WEIGHT_PARTS * 16)

            def block_step(j, slot, turn, role, expert):
                nxt = (slot + 1) % SLOTS
                if has_block(role, -1):
                    pe.wait_ge(xb_in[nxt], turn * 16 + (16 if nxt else 32))
                    if has_block(role, 1):
                        pe.wait_ge(xT_done, j)
                    turn_block(j + 1, nxt)
                if has_block(role, 0):
                    pe.wait_ge(xT_done, j + 1)
                    pe.wait_ge(w1_done, j + 1)
                    for f in range(FFC):
                        mm = pe.matmul(bank[4 + slot % 2][:, f * BLOCK:(f + 1) * BLOCK], w1_blk[slot % 2][:, f * 128:(f + 1) * 128],
                                       xbT[slot % 2][:], start=True, stop=True)
                    mm.then_inc(hidden_ps, 1)
                if has_block(role, 1):
                    p = (slot + 1) % 2
                    e = expert(1)
                    pe.wait_ge(hidden_done, j)
                    if has_block(role, 2):
                        pe.wait_ge(yb_done, j - 1)
                    for f in range(FFC):
                        mm = pe.matmul(bank[6 + p][:, 0:D], hT[p][:, f, :], w2_all[:, bass.ds(e * FF + f * D, D)],
                                       start=f == 0, stop=f == FFC - 1)
                    mm.then_inc(y_ps, 1)

            expert_steps(pe, block_step, SLOTS // 2, 1)

        @block.scalar
        def _(act):
            act.preload_act_table_set("gelu_and_others")

            def split_hi(g, u):
                act.activation(x_hi[u][:], x_raw[u][:], ACT.Copy).then_inc(hi_done, 1)

            for k in range(PARTS):
                act.wait_ge(part_in[k], 32)
                act.activation(tw_hi[:, w_part(k)], tw_raw[:, w_part(k)], ACT.Copy).then_inc(part_hi_done, 1)
                act.activation(x_hi[0][:, x_part(k)], x_raw[0][:, x_part(k)], ACT.Copy).then_inc(part_hi_done, 1)
            act.wait_ge(x_in1, 16)
            split_hi(1, 1)
            act.wait_ge(const_in, 48)
            act.wait_ge(pw_scaled, 1)
            act.activation(pw_hi[:], pw_raw[:], ACT.Copy).then_inc(pw_hi_done, 1)

            def step(g, u, role, part=BOTH):
                if has_group(role, 1):
                    act.wait_ge(main_done, g)
                    if has_group(role, 3):
                        act.wait_ge(t1_done, g - 2)
                    act.activation(geluT[1 - u][:], bank[1 - u][:, 0:GT], ACT.Gelu, bias=col_of("tok_b")).then_inc(gelu_done, 1)
                if role == GROUPS:
                    act.preload_act_table_set("natural_log_exp_and_others")
                    act.wait_ge(neg_b_done, 1)
                    exp_minus_a(0, 0, False)
                    act.wait_ge(log_start_done, 1)
                    log(0, 0, False)
                    exp_minus_a(1, 1, False)
                if has_group(role, 1) and has_group(role, -1):
                    act.wait_ge(x_in[1 - u], g * 8 + (8 if u else 16))
                    split_hi(g + 1, 1 - u)
                if has_group(role, 1):
                    act.wait_ge(shift1_done, g)
                    if has_group(role, 3):
                        act.wait_ge(h_done, g - 2)
                    for b in range(GB):
                        ins = act.activation(normed[1 - u][:, b * D:(b + 1) * D], bank[2][0:WIN, b * D:(b + 1) * D], ACT.Identity,
                                             bias=shift1[:, b:b + 1], scale=rstd1[:, b:b + 1])
                    ins.then_inc(normed_done, 1)
                if has_group(role, 3) and part != FIRST:
                    act.wait_ge(t2_done, g - 2)
                    act.activation(xsT_hi[:, at((g - 3) * GT, GT)], bank[3][:, 0:GT], ACT.Copy).then_inc(xsT_hi_done, 1)

            def exp_minus_a(c, k, reused):
                act.wait_ge(a_done, k + 1)
                if reused:
                    act.wait_ge(log_done, k - 1)
                act.activation(growth[c % 2][:], bank[0][:, 0:GT], ACT.Exp, bias=neg_b_a[:, c:c + 1], scale=-1.0).then_inc(e_done, 1)

            def log(c, k, reused):
                act.wait_ge(clip_done, k + 1)
                if reused:
                    act.wait_ge(scan_done, k)
                act.activation(log_growth[:, :, 1:WIN + 1], growth[c % 2][:].rearrange("p (b i) -> p b i", b=GB),
                               ACT.Ln).then_inc(log_done, 1)

            def cumulate(c, k, reused):
                act.wait_ge(scan_done, k + 1)
                if reused:
                    act.wait_ge(qT_done, k - 1)
                    act.wait_ge(kT_done, k - 1)
                act.activation(a_cum[c % 2][:], log_sum[:, :, 1:WIN + 1], ACT.Exp, scale=-1.0).then_inc(cum_done, 1)
                act.activation(a_inv[c % 2][:], log_sum[:, :, 1:WIN + 1], ACT.Exp).then_inc(inv_done, 1)

            def copy_counts(g):
                act.wait_ge(prefix_ps, g - 2)
                act.activation(counts[:].rearrange("p t b e -> p (t b e)"), bank[2][0:WIN, GT:GT + 2 * GB * EXPERTS],
                               ACT.Copy).then_inc(counts_done, 1)

            def start():
                cumulate(0, 0, False)

            def unit(g, u, role, c):
                n = g * CHUNKS + c
                if has_unit(role, c, -1):
                    log((c + 1) % CHUNKS, n + 1, True)
                if c == 2 and role < GROUPS and has_group(role, 3):
                    act.wait_ge(av_done, n - 2)
                    copy_counts(g)
                if has_unit(role, c, 3):
                    act.wait_ge(av_done, n - 2)
                    if c == 3 and has_group(role, 1):
                        act.wait_ge(proj_done, g)
                    act.activation(oT[(c + 1) % CHUNKS][:], bank[2][:, 0:GT], ACT.Copy).then_inc(oT_done, 1)
                if c == 1 and role == GROUPS:
                    act.wait_ge(av_done, GROUPS * CHUNKS)
                    copy_counts(g)
                if has_unit(role, c, -2):
                    exp_minus_a((c + 2) % CHUNKS, n + 2, True)
                if has_unit(role, c, -1):
                    cumulate((c + 1) % CHUNKS, n + 1, has_unit(role, c, 1))
                if has_unit(role, c, 0):
                    act.wait_ge(k_done, n + 1)
                    if has_unit(role, c, 2):
                        act.wait_ge(kT_done, n - 1)
                    act.activation(kb[c % 2][:], bank[4][:, 0:GT], ACT.Identity, bias=col_of("b_k", c)).then_inc(kb_done, 1)
                if c == 1 and has_group(role, 2):
                    act.wait_ge(shift3_done, g - 1)
                    if has_group(role, 3):
                        act.wait_ge(scattered[u], (g - u - 2) * (GB * 16) + 16)
                    for b in range(GB):
                        ins = act.activation(xm[u][:, 0, b, 0:D], h_all[:, at((g - 2) * (GB * D) + b * D, D)], ACT.Identity,
                                             bias=shift3[:, b:b + 1], scale=rstd3[:, b:b + 1])
                    ins.then_inc(xm_done, 1)
                if c == 2 and has_group(role, 2):
                    act.wait_ge(xmT_ps, g - 1)
                    act.activation(xmT[:], turned(role)[:, 0:GT], ACT.Copy).then_inc(xmT_done, 1)
                if c == 3 and has_group(role, 2):
                    act.wait_ge(shifted_done, g - 1)
                    act.activation(expd[:], shifted[:], ACT.Exp).then_inc(exp_done, 1)
                    act.activation(xm[u][:, 1, :, 0:D], xm[u][:, 0, :, 0:D], ACT.Copy).then_inc(xm_twice, 1)
                if c == 3 and role >= GROUPS and has_group(role, 2):
                    copy_counts(g + 1)

            tokenizer_and_attention(act, step, start, unit)

            act.preload_act_table_set("gelu_and_others")
            act.wait_ge(tail_done, 1)
            pad_tails(act, 1)
            act.wait_ge(packed_done, 1)

            def block_step(j, slot, turn, role, expert):
                if has_block(role, 0):
                    p = slot % 2
                    e = expert(0)
                    act.wait_ge(hidden_ps, j + 1)
                    for f in range(FFC):
                        ins = act.activation(hT[p][:, f, :], bank[4 + p][:, f * BLOCK:(f + 1) * BLOCK], ACT.Gelu,
                                             bias=b1_all[:, bass.ds(e * FFC + f, 1)])
                    ins.then_inc(hidden_done, 1)

            expert_steps(act, block_step, SLOTS // 2, 0)

            for u in range(SLOTS):
                act.wait_ge(y_out[u], 16 * len(range(u, BLOCKS, SLOTS)))
            load_results(act, 1)
            store_out(act, 1)

        @block.vector
        def _(dve):
            dve.memset(pad[:], 0.0).then_inc(pad_done, 1)
            dve.memset(running[:], 0.0).then_inc(running_done, 1)
            dve.wait_ge(pad_done, 1)
            dve.memset(pad[:, D:D + 1].bitcast(U32), NO_ROW).then_inc(pad_done, 1)

            def split_lo(g, u):
                dve.tensor_tensor(x_lo[u][:, X_SPLIT:], x_raw[u][:, X_SPLIT:], x_hi[u][:, X_SPLIT:].bitcast(F32),
                                  ALU.subtract).then_inc(lo_v_done, 1)

            for k in range(PARTS):
                dve.wait_ge(part_hi_done, 2 * k + 1)
                dve.tensor_tensor(tw_lo[:, w_part(k)], tw_raw[:, w_part(k)], tw_hi[:, w_part(k)].bitcast(F32), ALU.subtract)
                dve.wait_ge(part_hi_done, 2 * k + 2)
                dve.tensor_tensor(x_lo[0][:, x_part(k)], x_raw[0][:, x_part(k)], x_hi[0][:, x_part(k)].bitcast(F32),
                                  ALU.subtract).then_inc(part_done, 1)
            dve.wait_ge(hi_done, 1)
            split_lo(1, 1)
            dve.wait_ge(pw_in, 16)
            dve.wait_ge(const_in, 48)
            dve.tensor_scalar(pw_raw[:], pw_raw[:], col_of("attn_gamma"), None, ALU.mult).then_inc(pw_scaled, 1)
            dve.tensor_scalar(neg_b_a[:], b_a, -1.0, None, ALU.mult).then_inc(neg_b_done, 1)
            dve.wait_ge(pw_hi_done, 1)
            dve.tensor_tensor(pw_lo[:], pw_raw[:], pw_hi[:].bitcast(F32), ALU.subtract).then_inc(pw_done, 1)

            def step(g, u, role, part=BOTH):
                if has_group(role, 1):
                    dve.wait_ge(t1_done, g)
                    for b in range(GB):
                        ins = dve.bn_stats(stat1[:, b, :], bank[2][0:WIN, b * D:(b + 1) * D])
                    ins.then_inc(stat1_done, 1)
                    dve.wait_ge(const_in, 48)
                    dve.wait_ge(stat1_done, g)
                    for b in range(GB):
                        ins = dve.bn_aggr(mv1[:, b, :], stat1[:, b, :])
                    ins.then_inc(mv1_done, 1)
                    dve.wait_ge(mv1_done, g)
                    dve.tensor_scalar(neg_mean1[:], mv1[:, :, 0], -1.0, None, ALU.mult)
                    dve.tensor_scalar(var1[:], mv1[:, :, 1], EPS, None, ALU.add).then_inc(var1_done, 1)
                if role == GROUPS:
                    dve.wait_ge(main_done, GROUPS)
                    dve.memset(log_growth[:, :, 0:1], 0.0).then_inc(log_start_done, 1)
                    clip(0, 0)
                if has_group(role, 2) and part != SECOND:
                    dve.wait_ge(h_done, g - 1)
                    for b in range(GB):
                        ins = dve.bn_stats(stat2[:, b, :], h_all[:, at((g - 2) * (GB * D) + b * D, D)])
                    ins.then_inc(stat2_done, 1)
                    dve.wait_ge(const_in, 48)
                    dve.wait_ge(stat2_done, g - 1)
                    for b in range(GB):
                        ins = dve.bn_aggr(mv2[:, u, b, :], stat2[:, b, :])
                    ins.then_inc(mv2_done, 1)
                    dve.wait_ge(mv2_done, g - 1)
                    dve.tensor_scalar(base2[:, 0:GB], mv2[:, u, :, 1], EPS, None, ALU.add)
                    dve.tensor_scalar(base2[:, GB:2 * GB], mv2[:, u, :, 1], float(D), None, ALU.mult).then_inc(base2_done, 1)
                    if role == GROUPS:
                        scan(0, False)
                        clip(1, 1)
                        store_v(0, 0, 1)
                if has_group(role, 1) and has_group(role, -1):
                    dve.wait_ge(hi_done, g + 1)
                    split_lo(g + 1, 1 - u)
                if has_group(role, 3) and part != FIRST:
                    dve.wait_ge(xsT_hi_done, g - 2)
                    t = at((g - 3) * GT, GT)
                    dve.tensor_tensor(xsT_lo[:, t], bank[3][:, 0:GT], xsT_hi[:, t].bitcast(F32), ALU.subtract).then_inc(xsT_done, 1)
                if has_group(role, 2) and part != FIRST:
                    dve.wait_ge(root2_done, g - 1)
                    dve.tensor_tensor(norm2[:, 0, :], root2[:, 0:GB], root2[:, GB:2 * GB], ALU.mult).then_inc(length_done, 1)
                    dve.wait_ge(length_done, g - 1)
                    dve.tensor_scalar(norm2[:, 1, :], norm2[:, 0, :], 1e-12, None, ALU.max).then_inc(guarded_done, 1)
                    dve.wait_ge(guarded_done, g - 1)
                    dve.reciprocal(norm2[:, 2, :], norm2[:, 1, :]).then_inc(inverse_done, 1)
                    dve.wait_ge(inverse_done, g - 1)
                    dve.scalar_tensor_tensor(scale2[:], root2[:, 0:GB], float(D) ** 0.5, norm2[:, 2, :], ALU.mult,
                                             ALU.mult).then_inc(scale2_done, 1)
                    dve.wait_ge(scale2_done, g - 1)
                    for b in range(GB):
                        ins = dve.tensor_scalar(xs[u][:, b * D:(b + 1) * D], h_all[:, at((g - 2) * (GB * D) + b * D, D)],
                                                mv2[:, u, b, 0:1], scale2[:, b:b + 1], ALU.subtract, ALU.mult)
                    ins.then_inc(xs_done, 1)

            def clip(c, k):
                dve.wait_ge(e_done, k + 1)
                dve.tensor_scalar(growth[c % 2][:], growth[c % 2][:], 1.0, 1e10, ALU.add, ALU.min).then_inc(clip_done, 1)

            def scan(k, reused):
                dve.wait_ge(log_done, k + 1)
                if reused:
                    dve.wait_ge(inv_done, k)
                dve.tensor_tensor_scan(log_sum[:].rearrange("p b i -> p (b i)"), log_growth[:].rearrange("p b i -> p (b i)"),
                                       const_of("log_cap"), 0.0, ALU.add, ALU.min).then_inc(scan_done, 1)

            def store_v(w, b, count):
                dve.wait_ge(v_done, count)
                dve.tensor_tensor(v[w][:, b, :], bank[5][0:WIN, :], row_of("b_v"), ALU.add).then_inc(vT_done, 1)

            def start():
                store_v(0, 1, 2)

            def unit(g, u, role, c):
                n = g * CHUNKS + c
                choosing = c == 0 and role < GROUPS and has_group(role, 3)
                routing = c == 3 and role < GROUPS and has_group(role, 2)

                def mask(hd):
                    dve.wait_ge(sim_done, n * 2 - 1 + hd)
                    if hd == 0 and has_unit(role, c, 3):
                        dve.wait_ge(av_done, n - 2)
                    dve.tensor_tensor(attnT[(c + 1) % 2][:, hd, :], bank[6 + hd][0:WIN, 0:GT], causal,
                                      ALU.mult).then_inc(attn_done, 1)

                if has_unit(role, c, -1):
                    scan(n + 1, True)
                if choosing:
                    exp_total(g)
                if has_unit(role, c, 0):
                    dve.wait_ge(q_done, n + 1)
                    dve.wait_ge(cum_done, n + 1)
                    dve.scalar_tensor_tensor(qT[c % 2][:], bank[1][:, 0:GT], col_of("b_q", c),
                                             a_cum[c % 2][:].rearrange("p b i -> p (b i)"), ALU.add, ALU.mult).then_inc(qT_done, 1)
                if choosing:
                    exp_inverse(g)
                if routing:
                    biased_logits(g, role)
                if has_unit(role, c, -2):
                    clip((c + 2) % CHUNKS, n + 2)
                if choosing:
                    probabilities(g)
                if routing:
                    largest_logit(g)
                if has_unit(role, c, 1):
                    mask(0)
                if choosing:
                    top_values(g)
                if routing:
                    shifted_logits(g)
                if has_unit(role, c, 0):
                    dve.wait_ge(kb_done, n + 1)
                    dve.wait_ge(inv_done, n + 1)
                    dve.scalar_tensor_tensor(kT[c % 2][:], a_inv[c % 2][:].rearrange("p b i -> p (b i)"), 1e8,
                                             kb[c % 2][:], ALU.min, ALU.mult).then_inc(kT_done, 1)
                if choosing:
                    top_experts(g, u)
                if has_unit(role, c, 1):
                    mask(1)
                if choosing:
                    mark_chosen(g)
                if has_unit(role, c, -2) and (c + 2) // CHUNKS + role < GROUPS:
                    store_v(u if c < 2 else 1 - u, (c + 2) % CHUNKS, n + 3)
                if choosing:
                    choices(g)
                if c == 0 and role == GROUPS:
                    choose(g, u)
                if c == 0 and has_group(role, 2):
                    statistics_3(g)
                if c == 3 and role >= GROUPS and has_group(role, 2):
                    biased_logits(g, role)
                    largest_logit(g)
                    shifted_logits(g)
                    choose(g + 1, 1 - u)
                if c == 1 and role >= GROUPS and has_group(role, 3):
                    dve.wait_ge(placed_done, g - 3)
                    sort_group(dve, g, u)
                if c == 3 and has_group(role, 1):
                    residual(g)

            def residual(g):
                dve.wait_ge(proj_done, g)
                dve.wait_ge(hb_done, g)
                h = at((g - 1) * (GB * D), GB * D)
                dve.tensor_tensor(h_all[:, h], bank[3][0:WIN, :], h_all[:, h], ALU.add).then_inc(h2_done, 1)
                dve.wait_ge(const_in, 48)
                dve.wait_ge(h2_done, g)
                for b in range(GB):
                    ins = dve.bn_stats(stat3[:, b, :], h_all[:, at((g - 1) * (GB * D) + b * D, D)])
                ins.then_inc(stat3_done, 1)

            def statistics_3(g):
                dve.wait_ge(stat3_done, g - 1)
                dve.sem_inc(dve_go, 1)
                for b in range(GB):
                    ins = dve.bn_aggr(mv3[:, b, :], stat3[:, b, :])
                ins.then_inc(mv3_done, 1)
                dve.wait_ge(mv3_done, g - 1)
                dve.tensor_scalar(neg_mean3[:], mv3[:, :, 0], -1.0, None, ALU.mult)
                dve.tensor_scalar(var3[:], mv3[:, :, 1], EPS, None, ALU.add).then_inc(var3_done, 1)

            def biased_logits(g, role):
                dve.wait_ge(router_ps, g - 1)
                if has_group(role, 0):
                    dve.wait_ge(q_done, (g + 1) * CHUNKS)
                dve.tensor_tensor(logits[:].rearrange("p b e -> p (b e)"), bank[1][0:WIN, GT:GT + GB * EXPERTS], row_of("router_b"),
                                  ALU.add).then_inc(logits_done, 1)

            def largest_logit(g):
                dve.wait_ge(logits_done, g - 1)
                dve.tensor_reduce(top_logit[:], logits[:], AX_X, ALU.max).then_inc(top_logit_done, 1)

            def shifted_logits(g):
                dve.wait_ge(top_logit_done, g - 1)
                dve.tensor_tensor(shifted[:], logits[:], spread(top_logit[:]), ALU.subtract).then_inc(shifted_done, 1)

            def exp_total(g):
                dve.wait_ge(exp_done, g - 2)
                dve.tensor_reduce(exp_sum[:], expd[:], AX_X, ALU.add).then_inc(sum_done, 1)

            def exp_inverse(g):
                dve.wait_ge(sum_done, g - 2)
                dve.reciprocal(exp_rec[:], exp_sum[:]).then_inc(rec_done, 1)

            def probabilities(g):
                dve.wait_ge(rec_done, g - 2)
                dve.tensor_tensor(probs[:], expd[:], spread(exp_rec[:]), ALU.mult).then_inc(probs_done, 1)

            def top_values(g):
                dve.wait_ge(const_in, 48)
                dve.wait_ge(probs_done, g - 2)
                for b in range(GB):
                    ins = dve.max(top8[:, b, :], probs[:, b, :])
                ins.then_inc(top8_done, 1)

            def top_experts(g, u):
                dve.wait_ge(const_in, 48)
                dve.wait_ge(top8_done, g - 2)
                for b in range(GB):
                    ins = dve.max_index(top8_at[:, b, :], top8[:, b, :], probs[:, b, :])
                ins.then_inc(top8_at_done, 1)
                dve.tensor_copy(xm[1 - u][:, :, :, D + 1], top8[:, :, 0:2].rearrange("p b t -> p t b")).then_inc(gates_done, 1)
                dve.wait_ge(top8_at_done, g - 2)
                dve.tensor_copy(top8_atf[:], top8_at[:]).then_inc(top8_atf_done, 1)

            def mark_chosen(g):
                dve.wait_ge(top8_atf_done, g - 2)
                dve.wait_ge(place_done, g - 2)
                for t in range(2):
                    ins = dve.tensor_tensor(chosen[:, t], expert_no, spread(top8_atf[:, :, t]), ALU.is_equal)
                ins.then_inc(chosen_done, 1)

            def choices(g):
                dve.wait_ge(chosen_done, g - 2)
                dve.tensor_tensor(both[:], chosen[:, 0], chosen[:, 1], ALU.add).then_inc(both_done, 1)

            def choose(g, u):
                exp_total(g)
                exp_inverse(g)
                probabilities(g)
                top_values(g)
                top_experts(g, u)
                mark_chosen(g)
                choices(g)

            tokenizer_and_attention(dve, step, start, unit)

            dve.wait_ge(running_done, GROUPS * (GB + 1) + 1)
            dve.wait_ge(proj_done, GROUPS)
            in_all = running[0:1, GB, :]
            dve.tensor_scalar(n_int[:], in_all, float(BLOCK - 1), None, ALU.add).then_inc(table_step, 1)
            dve.memset(zero16[:], 0.0)
            dve.wait_ge(table_step, 1)
            dve.tensor_scalar(nb_int[:], n_int[:], BLOCK.bit_length() - 1, None, ALU.arith_shift_right).then_inc(table_step, 1)
            dve.wait_ge(table_step, 2)
            dve.tensor_copy(nb_f[:], nb_int[:]).then_inc(table_step, 1)
            dve.wait_ge(table_step, 3)
            dve.tensor_tensor_scan(nb_end[:], nb_f[:], zero16[:], 0.0, ALU.add, ALU.add).then_inc(table_step, 1)
            dve.wait_ge(table_step, 4)
            dve.wait_ge(block_no_in, 16)
            dve.tensor_tensor(past[:], nb_end[:].unsqueeze(1).to_broadcast([1, TABLE, EXPERTS]), block_no[:],
                              ALU.is_le).then_inc(table_step, 1)
            dve.wait_ge(table_step, 5)
            dve.tensor_reduce(blk_e[:], past[:], AX_X, ALU.add).then_inc(table_step, 1)
            dve.wait_ge(table_step, 6)
            dve.tensor_tensor(past[:], past[:], nb_f[:].unsqueeze(1).to_broadcast([1, TABLE, EXPERTS]),
                              ALU.mult).then_inc(table_step, 1)
            dve.wait_ge(table_step, 7)
            dve.tensor_reduce(blk_s[:], past[:], AX_X, ALU.add).then_inc(table_step, 1)
            dve.tensor_scalar(blk_expert[:], blk_e[:], float(EXPERTS - 1), None, ALU.min).then_inc(table_step, 1)
            dve.wait_ge(table_step, 8)
            dve.tensor_tensor(blk_r[:], block_no[:, :, 0], blk_s[:], ALU.subtract).then_inc(table_step, 1)
            dve.tensor_scalar(blk_q[:], blk_e[:], float(CAP), None, ALU.mult).then_inc(table_step, 1)
            dve.wait_ge(table_step, 11)
            dve.scalar_tensor_tensor(blk_t[:], blk_r[:], float(BLOCK), blk_q[:], ALU.mult, ALU.add).then_inc(table_step, 1)
            dve.wait_ge(table_step, 12)
            dve.tensor_scalar(blk_row[:], blk_t[:], float(DUMMY), None, ALU.min).then_inc(table_done, 1)
            n2, n4 = TABLE - 1, TABLE - 3
            dve.scalar_tensor_tensor(expert_pairs[:, 0:n2], blk_expert[:, 1:1 + n2], float(EXPERTS), blk_expert[:, 0:n2],
                                     ALU.mult, ALU.add).then_inc(table_step, 1)
            dve.wait_ge(table_step, 13)
            dve.scalar_tensor_tensor(expert_fours[:, 0:n4], expert_pairs[:, 2:2 + n4], float(EXPERTS ** 2), expert_pairs[:, 0:n4],
                                     ALU.mult, ALU.add).then_inc(table_step, 1)
            dve.wait_ge(table_step, 14)
            dve.scalar_tensor_tensor(packed[:], expert_pairs[:, 4:4 + BLOCKS], float(EXPERTS ** 4), expert_fours[:, 0:BLOCKS],
                                     ALU.mult, ALU.add).then_inc(packed_done, 1)
            dve.wait_ge(packed_done, 1)
            dve.wait_ge(experts_in, 16 + 2 * WEIGHT_PARTS * 16)

            def prepare(j, p, e):
                dve.tensor_copy(w1_blk[p][:], w1_all[:, bass.ds(e * FF, FF)]).then_inc(w1_done, 1)
                dve.wait_ge(xT_ps, j + 1)
                dve.tensor_copy(xbT[p][:], bank[p][:, 0:BLOCK]).then_inc(xT_done, 1)

            prepare(0, 0, dve.value_load(packed[0:1, 0:1], min_val=0, max_val=EXPERTS ** PACKED - 1) % EXPERTS)

            def block_step(j, slot, turn, role, expert):
                if has_block(role, -1):
                    if has_block(role, 1):
                        dve.wait_ge(hidden_ps, j)
                    prepare(j + 1, (slot + 1) % 2, expert(-1))
                if has_block(role, 1):
                    p, last = (slot + 1) % 2, (slot - 1) % SLOTS
                    e = expert(1)
                    dve.wait_ge(y_ps, j)
                    dve.tensor_tensor(yb[p][:], bank[6 + p][:, 0:D], b2_all[:, bass.ds(e * D, D)], ALU.add).then_inc(yb_done, 1)
                    dve.wait_ge(yb_done, j)
                    dve.tensor_scalar(yg[last][:], yb[p][:], xb[last][:, D + 1:D + 2], None, ALU.mult).then_inc(yg_done, 1)

            expert_steps(dve, block_step, SLOTS // 3, 1)

            for k in range(OUT_STEPS):
                if k not in POOL_OUT:
                    add_results(dve, k)

        @block.gpsimd
        def _(pool):
            def split_lo(g, u):
                pool.tensor_tensor(x_lo[u][:, 0:X_SPLIT], x_raw[u][:, 0:X_SPLIT], x_hi[u][:, 0:X_SPLIT].bitcast(F32),
                                   ALU.subtract).then_inc(lo_p_done, 1)

            pool.wait_ge(hi_done, 1)
            split_lo(1, 1)
            pool.wait_ge(const_in, 48)
            pool.wait_ge(pad_done, 2)
            half = BLOCK // 2
            for u in range(2):
                pool.dma_start(sorted_rows[DUMMY + u * half:DUMMY + (u + 1) * half, :], pad[u * half:(u + 1) * half, :]).then_inc(scattered[u], 16)

            def step(g, u, role, part=BOTH):
                if has_group(role, 1):
                    pool.wait_ge(var1_done, g)
                    if has_group(role, 2):
                        pool.wait_ge(normed_done, g - 1)
                    pool.tensor_tensor(rstd1[:], var1[:], power[:, 0:GB], ALU.pow).then_inc(rstd1_done, 1)
                    pool.wait_ge(rstd1_done, g)
                    pool.tensor_tensor(shift1[:], neg_mean1[:], rstd1[:], ALU.mult).then_inc(shift1_done, 1)
                if has_group(role, 2) and part != SECOND:
                    pool.wait_ge(base2_done, g - 1)
                    pool.tensor_tensor(root2[:], base2[:], power, ALU.pow).then_inc(root2_done, 1)
                if has_group(role, 1) and has_group(role, -1):
                    pool.wait_ge(hi_done, g + 1)
                    split_lo(g + 1, 1 - u)
                if has_group(role, 1):
                    pool.wait_ge(normed_done, g)
                    pool.tensor_tensor(by_row(scaled[:]), by_row(normed[1 - u][:]), each_row("gamma"), ALU.mult).then_inc(scaled_done, 1)
                    pool.wait_ge(scaled_done, g)
                    pool.tensor_tensor(by_row(h_all[:, at((g - 1) * (GB * D), GB * D)]), by_row(scaled[:]), each_row("beta"), ALU.add).then_inc(h_done, 1)

            def scatter(g, u, batches):
                for b in batches:
                    for t in range(2):
                        pool.indirect_dma_start(sorted_rows, bass.IndirectOffsetOnAxis(ap=place_u[1 - u][:, t * GB + b:t * GB + b + 1], axis=0),
                                                xm[1 - u][:, t, b, :], None).then_inc(scattered[1 - u], 16)

            def address_results(g, u, role):
                if has_group(role, 3):
                    pool.wait_ge(scattered[u], (g - u - 2) * (GB * 16) + 16)
                    pool.sem_inc(pool_go, 1)
                pool.tensor_copy(xm[u][:, :, :, D].bitcast(U32), result_row).then_inc(dest_done, 1)
                pool.wait_ge(dest_done, g * 2 - 3)
                pool.tensor_tensor(result_row, result_row, group_tokens, ALU.add).then_inc(dest_done, 1)
                pool.wait_ge(dest_done, g * 2 - 2)

            def start():
                pool.sem_inc(place_done, 1)

            def unit(g, u, role, c):
                if c == 0 and has_group(role, 2):
                    pool.wait_ge(var3_done, g - 1)
                    pool.tensor_tensor(rstd3[:], var3[:], power[:, 0:GB], ALU.pow).then_inc(rstd3_done, 1)
                    pool.wait_ge(rstd3_done, g - 1)
                    pool.tensor_tensor(shift3[:], neg_mean3[:], rstd3[:], ALU.mult).then_inc(shift3_done, 1)
                if c == 0 and has_group(role, 0):
                    h = by_row(h_all[:, at(g * (GB * D), GB * D)])
                    pool.tensor_tensor(h, h, each_row("b_out"), ALU.add).then_inc(hb_done, 1)
                if c == 1 and role < GROUPS and has_group(role, 2):
                    address_results(g, u, role)
                if c == 2 and has_group(role, 3):
                    if role < GROUPS:
                        sort_group(pool, g, u)
                    if role == GROUPS + 2:
                        pool.wait_ge(running_done, GROUPS * (GB + 1) + 1)
                        pool.wait_ge(proj_done, GROUPS)
                        pool.tensor_tensor(tail_f[:], running[0:1, GB, :], first_row[0:1, 0, :], ALU.add).then_inc(tail_f_done, 1)
                        pool.wait_ge(tail_f_done, 1)
                        pool.tensor_copy(tail_at[:], tail_f[:]).then_inc(tail_done, 1)
                    pool.wait_ge(placed_done, g - 2)
                    pool.wait_ge(gates_done, g - 2)
                    pool.wait_ge(dest_done, g * 2 - 4)
                    pool.wait_ge(xm_twice, g - 2)
                    pool.sem_inc(pool_go, 1)
                if c >= 2 and has_group(role, 3):
                    scatter(g, u, range(2 * c - 4, 2 * c - 2))
                if c == 3 and role >= GROUPS and has_group(role, 2):
                    address_results(g, u, role)

            tokenizer_and_attention(pool, step, start, unit)

            def block_step(j, slot, turn, role, expert):
                if has_block(role, 1):
                    last = (slot - 1) % SLOTS
                    pool.wait_ge(yg_done, j)
                    pool.sem_inc(pool_go, 1)
                    pool.indirect_dma_start(results, bass.IndirectOffsetOnAxis(ap=xb[last][:, D:D + 1].bitcast(U32), axis=0),
                                            yg[last][:], None, bounds_check=NO_ROW - 1, oob_is_err=False).then_inc(y_out[last], 16)

            expert_steps(pool, block_step, SLOTS // 2, 0)
            for k in POOL_OUT:
                add_results(pool, k)


def shape_constants(np):
    f = np.float32
    i = np.arange(WIN)
    parts = {
        "ident": np.eye(128),
        "causal": np.tile(np.where(i[None, :] >= i[:, None], SCALE, 0.0), (1, GB)),
        "before": (i[:, None] < i[None, :]).astype(f),
        "ones": np.ones((WIN, WIN)),
        "log_cap": np.tile(np.where(np.arange(WIN + 1) == 0, 0.0, LOG_CAP), (128, GB)),
        "first_row": np.tile(np.arange(EXPERTS) * CAP, (128, GB)),
        "expert": np.tile(np.arange(EXPERTS), (128, GB)),
        "result_row": (np.arange(2)[None, :, None] * TOKENS + np.arange(GB)[None, None, :] * WIN
                       + np.arange(128)[:, None, None]).reshape(128, 2 * GB),
        "group_tokens": np.full((128, 2 * GB), GT),
        "power": np.tile(np.repeat([-0.5, 0.5], GB), (128, 1)),
    }
    out = np.zeros((128, CONST_COLS), f)
    for name, a in parts.items():
        out[:a.shape[0], CONST[name][0]:CONST[name][0] + a.shape[1]] = a
    return out


def kernel(x, L0_tok_W, L0_tok_b, L0_tok_gamma, L0_tok_beta, L0_attn_gamma, L0_attn_w_qkv, L0_attn_b_qkv, L0_attn_w_a,
           L0_attn_b_a, L0_attn_w_out, L0_attn_b_out, L0_ffn_router_w, L0_ffn_router_b, L0_ffn_w1, L0_ffn_b1, L0_ffn_w2, L0_ffn_b2):
    import numpy as np
    import concourse.bacc as bacc
    from concourse.bass_utils import run_bass_kernel_spmd

    def repeated(a, n):
        return np.broadcast_to(np.asarray(a).reshape(1, -1), (n, np.asarray(a).size))

    def columns(a):
        return np.asarray(a).reshape(-1, 128).T

    used = np.asarray(x)[:, :CELLS * STRIDE].reshape(GROUPS, GB, CELLS, STRIDE, D)
    rows = np.zeros((WIN, ROWS_COLS), np.float32)
    for name, a in (("gamma", L0_tok_gamma), ("beta", L0_tok_beta), ("b_out", L0_attn_b_out),
                    ("b_v", np.asarray(L0_attn_b_qkv)[2 * INNER:]), ("router_b", np.tile(L0_ffn_router_b, GB))):
        rows[:, ROWS[name][0]:ROWS[name][0] + ROWS[name][1]] = repeated(a, WIN)
    cols = np.zeros((128, COLS_COLS), np.float32)
    for name, a in (("tok_b", columns(L0_tok_b)), ("attn_gamma", columns(L0_attn_gamma)),
                    ("b_q", columns(np.asarray(L0_attn_b_qkv)[:INNER])), ("b_k", columns(np.asarray(L0_attn_b_qkv)[INNER:2 * INNER])),
                    ("b_a", columns(L0_attn_b_a)), ("b1", columns(L0_ffn_b1)), ("router_w", np.asarray(L0_ffn_router_w).T)):
        cols[:, COLS[name][0]:COLS[name][0] + COLS[name][1]] = a
    arrays = {
        "x_dram": used.transpose(0, 4, 3, 1, 2).reshape(GROUPS, D, STRIDE * GB * CELLS),
        "tok_w_dram": np.asarray(L0_tok_W).reshape(HALVES, STRIDE, D, D).transpose(2, 1, 0, 3).reshape(D, TOKEN_SIZE * D),
        "proj_w_dram": np.concatenate([np.asarray(L0_attn_w_qkv), np.asarray(L0_attn_w_a)], axis=1),
        "out_w_dram": np.asarray(L0_attn_w_out).reshape(CHUNKS, 128, D).transpose(1, 0, 2).reshape(128, CHUNKS * D),
        "w1_dram": np.asarray(L0_ffn_w1).transpose(2, 0, 1).reshape(D, EXPERTS * FF),
        "w2_dram": np.asarray(L0_ffn_w2).reshape(EXPERTS, D, FFC, 128).transpose(3, 0, 2, 1).reshape(128, EXPERTS * FF),
        "b2_dram": repeated(L0_ffn_b2, 128),
        "consts_dram": shape_constants(np),
        "rows_dram": rows,
        "cols_dram": cols,
        "block_nos_dram": np.repeat(np.arange(TABLE), EXPERTS).reshape(1, TABLE, EXPERTS).astype(np.float32),
    }
    arrays = {name: np.ascontiguousarray(a) for name, a in arrays.items()}
    nc = bacc.Bacc("TRN2", target_bir_lowering=False, num_devices=1)
    args = [nc.dram_tensor(name, a.shape, mybir.dt.from_np(a.dtype), kind="ExternalInput").ap() for name, a in arrays.items()]
    out = nc.dram_tensor("out_dram", (BATCH, WIN, D), F32, kind="ExternalOutput").ap()
    build(nc, *args, out)
    got = run_bass_kernel_spmd(nc, [arrays], core_ids=[0])
    return got.results[0]["out_dram"]
```
